# Optimizing a Trainium2 kernel written in Bass

```python
import numpy as np
import jax
import jax.numpy as jnp

def _softmax(x, axis=-1):
    return jax.nn.softmax(x, axis=axis)

def _gelu(x):
    return jax.nn.gelu(x, approximate=True)

def _silu(x):
    return jax.nn.silu(x)

def _sigmoid(x):
    return jax.nn.sigmoid(x)

def _layernorm(x, axis=-1, eps=1e-05):
    m = jnp.mean(x, axis=axis, keepdims=True)
    v = jnp.var(x, axis=axis, keepdims=True)
    return (x - m) / jnp.sqrt(v + eps)

def _scatter_add(tgt, idx, src, axis=0):
    return tgt.at[idx].add(src)

def _segment_sum(src, seg, n):
    return jax.ops.segment_sum(src, seg, n)
kernel_name = 'mk_xattn_ffn_d2_seqx_r8_66b887'

def setup_inputs(seed: int=0):
    np.random.seed(seed)
    _w = jnp.asarray

    def _rec_inputs():
        import jax
        import jax.numpy as jnp
        _rk = jax.random.key(seed)
        x = -7.109e-05 + 0.9999 * jax.random.normal(jax.random.fold_in(_rk, 1), (4, 256, 512), jnp.float32)
        _lenS = 256 - jax.random.randint(jax.random.fold_in(_rk, 7), (4,), 0, max(1, 256 // 4) + 1, jnp.int32)
        _lenS2 = 1601 - jax.random.randint(jax.random.fold_in(_rk, 8), (4,), 0, max(1, 1601 // 4) + 1, jnp.int32)
        _ctx_4096P = jax.random.normal(jax.random.fold_in(_rk, 11), (4, 16, 512), jnp.float32)
        _ctx_4096c = jax.random.dirichlet(jax.random.fold_in(_rk, 511), 0.3 * jnp.ones((16,), jnp.float32), (4, 1601))
        _ctx_4096t = jnp.einsum('bsk,bkd->bsd', _ctx_4096c, _ctx_4096P)
        _ctx_4096t = _ctx_4096t * jax.lax.rsqrt(jnp.mean(jnp.square(_ctx_4096t)) + 1e-12) * 0.953939
        ctx_4096 = -2.6191e-05 + 0.999952 * (_ctx_4096t + 0.3 * jax.random.normal(jax.random.fold_in(_rk, 611), (4, 1601, 512), jnp.float32))
        return (x, ctx_4096)
    x, ctx_4096 = _rec_inputs()

    def _L0_xattn_setup():
        import jax, jax.numpy as jnp
        import numpy as np
        TEXT_DIM = 512
        FEATURE_DIM = 512

        def _xavier_uniform(key, shape):
            fan_in, fan_out = (shape[1], shape[0])
            limit = float(np.sqrt(6.0 / (fan_in + fan_out)))
            return jax.random.uniform(key, shape, jnp.float32, -limit, limit)
        key = jax.random.key(seed)
        k1, k2, k3, k4 = jax.random.split(key, 4)
        text = jax.random.normal(k1, (8, 256, TEXT_DIM), jnp.float32)
        features = jax.random.normal(k2, (8, 72, FEATURE_DIM), jnp.float32)
        Wq = _xavier_uniform(k3, (FEATURE_DIM, TEXT_DIM))
        bq = jnp.zeros((FEATURE_DIM,), jnp.float32)
        Wk = _xavier_uniform(k4, (FEATURE_DIM, FEATURE_DIM))
        bk = jnp.zeros((FEATURE_DIM,), jnp.float32)
        return {'text': text, 'features': features, 'Wq': Wq, 'bq': bq, 'Wk': Wk, 'bk': bk}
    _L0_xattn_all = _L0_xattn_setup()
    _L0_xattn_in = {k: v for k, v in _L0_xattn_all.items() if k in ('Wq', 'bq', 'Wk', 'bk')}
    del _L0_xattn_all

    def _L0_ffn_setup():
        import jax, jax.numpy as jnp
        import numpy as np
        STE_SCALE = 1.0
        CLAMP_MAX = 1.0
        EPS = 1e-05

        def _act_quant(x):
            amax = jnp.clip(jnp.max(jnp.abs(x), axis=-1, keepdims=True), EPS, None)
            s = 127.0 / amax
            xq = jnp.clip(jnp.round(x * s), -128.0, 127.0) / s
            return x + jax.lax.stop_gradient(xq - x)

        def _weight_quant(w):
            wc = jnp.clip(w, -CLAMP_MAX, CLAMP_MAX)
            scale = jnp.mean(jnp.abs(wc)) + EPS
            wq = jnp.clip(jnp.round(wc / scale), -1.0, 1.0) * scale
            ws = STE_SCALE * wc
            return ws + jax.lax.stop_gradient(wq - ws)

        def _bitlinear(x, w):
            return jnp.einsum('bsi,oi->bso', _act_quant(x), _weight_quant(w))
        key = jax.random.key(seed)
        k1, k2, k3 = jax.random.split(key, 3)
        H, F = (512, 2048)
        x = jax.random.normal(k1, (2, 256, H), dtype=jnp.float32)
        w_up = jax.random.normal(k2, (F, H), dtype=jnp.float32) * 0.02
        w_down = jax.random.normal(k3, (H, F), dtype=jnp.float32) * 0.02
        return {'x': x, 'w_up': w_up, 'w_down': w_down}
    _L0_ffn_all = _L0_ffn_setup()
    _L0_ffn_in = {k: v for k, v in _L0_ffn_all.items() if k in ('w_up', 'w_down')}
    del _L0_ffn_all

    def _L1_xattn_setup():
        import jax, jax.numpy as jnp
        import numpy as np
        import math
        HIDDEN = 512
        N_HEADS = 32
        HEAD_DIM = 128
        N_KV_HEADS = 4
        N_GROUPS = N_HEADS // N_KV_HEADS
        key = jax.random.key(seed)
        ks = jax.random.split(key, 6)
        B, NL, S = (8, 64, 512)
        latents = jax.random.normal(ks[0], (B, NL, HIDDEN), dtype=jnp.float32)
        context = jax.random.normal(ks[1], (B, S, HIDDEN), dtype=jnp.float32)
        scale = 1.0 / math.sqrt(HIDDEN)
        Wq = jax.random.normal(ks[2], (HIDDEN, N_HEADS * HEAD_DIM), dtype=jnp.float32) * scale
        Wk = jax.random.normal(ks[3], (HIDDEN, N_KV_HEADS * HEAD_DIM), dtype=jnp.float32) * scale
        Wv = jax.random.normal(ks[4], (HIDDEN, N_KV_HEADS * HEAD_DIM), dtype=jnp.float32) * scale
        Wo = jax.random.normal(ks[5], (N_HEADS * HEAD_DIM, HIDDEN), dtype=jnp.float32) * scale
        return {'latents': latents, 'context': context, 'Wq': Wq, 'Wk': Wk, 'Wv': Wv, 'Wo': Wo}
    _L1_xattn_all = _L1_xattn_setup()
    _L1_xattn_in = {k: v for k, v in _L1_xattn_all.items() if k in ('Wq', 'Wk', 'Wv', 'Wo')}
    del _L1_xattn_all

    def _L1_ffn_setup():
        import jax, jax.numpy as jnp
        import numpy as np
        N_EXPERTS = 28
        TOP_K = 2
        RANK = 8
        LORA_ALPHA = 16
        SCALING = LORA_ALPHA / RANK
        TEMP = 1.0
        key = jax.random.key(seed)
        ks = jax.random.split(key, 5)
        B, S, D_IN, D_OUT = (4, 256, 512, 512)
        x = jax.random.normal(ks[0], (B, S, D_IN), dtype=jnp.float32)
        base_W = jax.random.normal(ks[1], (D_OUT, D_IN), dtype=jnp.float32) * (1.0 / np.sqrt(D_IN))
        gate_W = jax.random.normal(ks[2], (N_EXPERTS, D_IN), dtype=jnp.float32) * (1.0 / np.sqrt(D_IN))
        lora_A = jax.random.normal(ks[3], (N_EXPERTS, RANK, D_IN), dtype=jnp.float32) * (1.0 / np.sqrt(D_IN))
        lora_B = jax.random.normal(ks[4], (N_EXPERTS, D_OUT, RANK), dtype=jnp.float32) * 0.01
        return {'x': x, 'base_W': base_W, 'gate_W': gate_W, 'lora_A': lora_A, 'lora_B': lora_B}
    _L1_ffn_all = _L1_ffn_setup()
    _L1_ffn_in = {k: v for k, v in _L1_ffn_all.items() if k in ('base_W', 'gate_W', 'lora_A', 'lora_B')}
    del _L1_ffn_all
    return {'x': x, 'ctx_4096': ctx_4096, 'L0_xattn_Wq': _L0_xattn_in['Wq'], 'L0_xattn_bq': _L0_xattn_in['bq'], 'L0_xattn_Wk': _L0_xattn_in['Wk'], 'L0_xattn_bk': _L0_xattn_in['bk'], 'L0_ffn_w_up': _L0_ffn_in['w_up'], 'L0_ffn_w_down': _L0_ffn_in['w_down'], 'L1_xattn_Wq': _L1_xattn_in['Wq'], 'L1_xattn_Wk': _L1_xattn_in['Wk'], 'L1_xattn_Wv': _L1_xattn_in['Wv'], 'L1_xattn_Wo': _L1_xattn_in['Wo'], 'L1_ffn_base_W': _L1_ffn_in['base_W'], 'L1_ffn_gate_W': _L1_ffn_in['gate_W'], 'L1_ffn_lora_A': _L1_ffn_in['lora_A'], 'L1_ffn_lora_B': _L1_ffn_in['lora_B']}

def reference(x, ctx_4096, L0_xattn_Wq, L0_xattn_bq, L0_xattn_Wk, L0_xattn_bk, L0_ffn_w_up, L0_ffn_w_down, L1_xattn_Wq, L1_xattn_Wk, L1_xattn_Wv, L1_xattn_Wo, L1_ffn_base_W, L1_ffn_gate_W, L1_ffn_lora_A, L1_ffn_lora_B):
    import jax
    import jax.numpy as jnp

    def _L0_xattn_ref(text, features, Wq, bq, Wk, bk):
        import jax, jax.numpy as jnp
        import numpy as np
        TEXT_DIM = 512
        FEATURE_DIM = 512

        def _xavier_uniform(key, shape):
            fan_in, fan_out = (shape[1], shape[0])
            limit = float(np.sqrt(6.0 / (fan_in + fan_out)))
            return jax.random.uniform(key, shape, jnp.float32, -limit, limit)
        Q = jnp.einsum('btx,dx->btd', text, Wq) + bq
        K = jnp.einsum('bpx,dx->bpd', features, Wk) + bk
        scale = 1.0 / jnp.sqrt(jnp.asarray(K.shape[-1], K.dtype))
        scores = jnp.einsum('btd,bpd->btp', Q, K) * scale
        attn = jax.nn.softmax(scores, axis=-1)
        attended = jnp.einsum('btp,bpd->btd', attn, features)
        return attended

    def _L0_ffn_ref(x, w_up, w_down):
        import jax, jax.numpy as jnp
        import numpy as np
        STE_SCALE = 1.0
        CLAMP_MAX = 1.0
        EPS = 1e-05

        def _act_quant(x):
            amax = jnp.clip(jnp.max(jnp.abs(x), axis=-1, keepdims=True), EPS, None)
            s = 127.0 / amax
            xq = jnp.clip(jnp.round(x * s), -128.0, 127.0) / s
            return x + jax.lax.stop_gradient(xq - x)

        def _weight_quant(w):
            wc = jnp.clip(w, -CLAMP_MAX, CLAMP_MAX)
            scale = jnp.mean(jnp.abs(wc)) + EPS
            wq = jnp.clip(jnp.round(wc / scale), -1.0, 1.0) * scale
            ws = STE_SCALE * wc
            return ws + jax.lax.stop_gradient(wq - ws)

        def _bitlinear(x, w):
            return jnp.einsum('bsi,oi->bso', _act_quant(x), _weight_quant(w))
        h = _bitlinear(x, w_up)
        h = jnp.square(jax.nn.relu(h))
        return _bitlinear(h, w_down)

    def _L1_xattn_ref(latents, context, Wq, Wk, Wv, Wo):
        import jax, jax.numpy as jnp
        import numpy as np
        import math
        HIDDEN = 512
        N_HEADS = 32
        HEAD_DIM = 128
        N_KV_HEADS = 4
        N_GROUPS = N_HEADS // N_KV_HEADS
        b, q_len, _ = latents.shape
        kv_len = q_len + context.shape[1]
        hidden_states = jnp.concatenate([context, latents], axis=1)
        q = (latents @ Wq).reshape(b, q_len, N_KV_HEADS, N_GROUPS, HEAD_DIM)
        k = (hidden_states @ Wk).reshape(b, kv_len, N_KV_HEADS, HEAD_DIM)
        v = (hidden_states @ Wv).reshape(b, kv_len, N_KV_HEADS, HEAD_DIM)
        scale = 1.0 / math.sqrt(HEAD_DIM)
        scores = jnp.einsum('bqhgd,bkhd->bhgqk', q, k) * scale
        attn = jax.nn.softmax(scores.astype(jnp.float32), axis=-1).astype(q.dtype)
        out = jnp.einsum('bhgqk,bkhd->bqhgd', attn, v)
        out = out.reshape(b, q_len, N_HEADS * HEAD_DIM)
        return out @ Wo

    def _L1_ffn_ref(x, base_W, gate_W, lora_A, lora_B):
        import jax, jax.numpy as jnp
        import numpy as np
        N_EXPERTS = 28
        TOP_K = 2
        RANK = 8
        LORA_ALPHA = 16
        SCALING = LORA_ALPHA / RANK
        TEMP = 1.0
        B, S, D_in = x.shape
        xf = x.reshape(B * S, D_in)
        base = xf @ base_W.T
        logits = xf @ gate_W.T
        top_vals, top_idx = jax.lax.top_k(logits, TOP_K)
        top_probs = jax.nn.softmax(top_vals / TEMP, axis=-1)
        N = xf.shape[0]
        gate_full = jnp.zeros((N, N_EXPERTS), dtype=xf.dtype).at[jnp.arange(N)[:, None], top_idx].add(top_probs)
        h = jnp.einsum('nd,erd->ner', xf, lora_A)
        h = h * (gate_full * SCALING)[:, :, None]
        lora_out = jnp.einsum('ner,eor->no', h, lora_B)
        out = base + lora_out
        return out.reshape(B, S, -1)
    x = x + _L0_xattn_ref(_layernorm(x, axis=-1), ctx_4096, L0_xattn_Wq, L0_xattn_bq, L0_xattn_Wk, L0_xattn_bk)
    x = x + _L0_ffn_ref(_layernorm(x, axis=-1), L0_ffn_w_up, L0_ffn_w_down)
    x = x + _L1_xattn_ref(_layernorm(x, axis=-1), ctx_4096, L1_xattn_Wq, L1_xattn_Wk, L1_xattn_Wv, L1_xattn_Wo)
    x = x + _L1_ffn_ref(_layernorm(x, axis=-1), L1_ffn_base_W, L1_ffn_gate_W, L1_ffn_lora_A, L1_ffn_lora_B)
    return x

_drawn_inputs = setup_inputs


def setup_inputs(seed=0):
    import zlib

    import numpy as np

    out = dict(_drawn_inputs(seed))
    spreads = {'L0_xattn_bq': (0.0, 0.6), 'L0_xattn_bk': (0.0, 0.8)}
    factors = {'L1_ffn_gate_W': 3.055, 'L1_ffn_lora_A': 2.978, 'L1_ffn_lora_B': 2.936}
    for name, (base, spread) in spreads.items():
        noise = np.random.default_rng([zlib.crc32(name.encode()), seed]).standard_normal(out[name].shape)
        drawn = base * np.exp(spread * noise) if base else spread * noise
        out[name] = jnp.asarray(drawn.astype(out[name].dtype))
    for name, factor in factors.items():
        out[name] = (out[name] * factor).astype(out[name].dtype)
    return out
```

```python
import concourse.bass as bass
from concourse import mybir
from contextlib import ExitStack
import math

fp32 = mybir.dt.float32
fp16 = mybir.dt.float16
bf16 = mybir.dt.bfloat16
u32 = mybir.dt.uint32
ALU = mybir.AluOpType
ACT = mybir.ActivationFunctionType
AX = mybir.AxisListType

NB = 4
NTOK = 256
QT = NTOK // 128
NT = NB * QT
D = 512
DC = D // 128
NC = 1601
KT0 = -(-NC // 128)
REST = NC - (KT0 - 1) * 128
F = 2048
FC = F // 128
KVH = 4
GRP = 8
HD = 128
NK = NTOK + NC
KT1 = -(-NK // 128)
NCP = NC + NC % 2
NKP = NTOK + NCP
NE, RANK, TOPK_SCALE = 28, 8, 2.0
NR = NE * RANK
EPS = 1e-5
MAGIC = 1.5 * 2.0 ** 23

SX = 64.0
SW = 1024.0
SQ = 512.0
SP_ = 4096.0


def banks(n):
    return [(o, min(512, n - o)) for o in range(0, n, 512)]


CUT0 = banks(NC)
CUT1 = banks(NK)


def mm3(nc, out, a, b, start, stop):
    nc.tensor.matmul(out, a[0], b[0], start=start, stop=False)
    nc.tensor.matmul(out, a[0], b[1], start=False, stop=False)
    return nc.tensor.matmul(out, a[1], b[0], start=False, stop=stop)


class Chain:

    def __init__(self, eng, sem, base=0):
        self.eng, self.sem, self.base, self.n = eng, sem, base, 0

    def __call__(self, ins):
        self.n += 1
        ins.then_inc(self.sem, 1)
        self.eng.wait_ge(self.sem, self.base + self.n)


LN_STEPS = 6


def layer_norm_stats(nc, dve, chain, x2, st, mv, ve, yh, s_var, var_at, s_pow, pow_at):
    for q in range(QT):
        last = nc.vector.bn_stats(st[:, q, :], x2[:, q, :])
    chain(last)
    nc.vector.memset(ve[:, :], EPS)
    for q in range(QT):
        last = nc.vector.bn_aggr(mv[:, q, :], st[:, q, :])
    chain(last)
    nc.vector.tensor_tensor(ve[:, :], mv[:, :, 1], ve[:, :], ALU.add).then_inc(s_var, 1)
    dve.wait_ge(s_var, var_at)
    dve.wait_ge(s_pow, pow_at)
    chain(nc.vector.tensor_tensor(yh[:, 1, :], yh[:, 0, :], yh[:, 0, :], ALU.mult))
    chain(nc.vector.tensor_tensor(yh[:, 1, :], yh[:, 1, :], ve[:, :], ALU.mult))
    chain(nc.vector.tensor_scalar(yh[:, 1, :], yh[:, 1, :], -0.5, 1.5, ALU.mult, ALU.add))
    chain(nc.vector.tensor_tensor(yh[:, 2, :], yh[:, 0, :], yh[:, 1, :], ALU.mult))


def build(nc, x, ctx4, Wq0, bq0, Wk0, bk0, Wup, Wdn, Wq1, Wk1, Wv1, Wo1, baseW, gateW, loraA, loraB, out):
    k_scr = nc.dram_tensor("k_scr", (NB, KVH, 128, 2 * NCP), fp16, kind="Internal").ap()
    v_scr = nc.dram_tensor("v_scr", (NB, KVH, 128, KT0 * 2 * HD), fp16, kind="Internal").ap()
    wq_scr = nc.dram_tensor("wq_scr", (KVH, 8, 128, 2 * 512), fp16, kind="Internal").ap()
    wo_scr = nc.dram_tensor("wo_scr", (KVH, 8, 128, 2 * 512), fp16, kind="Internal").ap()

    with ExitStack() as keep:
        def sbk(name, shape, dt):
            return keep.enter_context(nc.sbuf_tensor(name, shape, dt))

        ps = keep.enter_context(nc.psum_tensor("ps", [128, 8, 512], fp32))
        K = {
            "id32": sbk("id32", [128, 128], fp32),
            "id16": sbk("id16", [128, 128], fp16),
            "x": sbk("x_all", [128, NT, D], fp32),
            "wk": sbk("wk_split", [128, 2, DC, 512], fp16),
            "wv": sbk("wv_split", [128, 2, DC, 512], fp16),
            "mhalf": sbk("mhalf", [128, QT], fp32),
        }
        with ExitStack() as a:
            M = {
                "m": a.enter_context(nc.sbuf_tensor("m_split", [128, 2, DC, 512], fp16)),
                "qb": a.enter_context(nc.sbuf_tensor("q_bias", [128, DC], fp32)),
                "wb": a.enter_context(nc.sbuf_tensor("wb_split", [128, 2, DC], fp16)),
                "c0": a.enter_context(nc.sbuf_tensor("c0", [128, 1], fp32)),
            }
            prepare(nc, ps, K, M, x, Wq0, bq0, Wk0, bk0, Wk1, Wv1)
            attention0(nc, ps, K, M, ctx4, Wq1, Wo1, k_scr, v_scr, wq_scr, wo_scr)
        ffn0(nc, ps, K, Wup, Wdn)
        attention1(nc, ps, K, k_scr, v_scr, wq_scr, wo_scr)
        ffn1(nc, ps, K, baseW, gateW, loraA, loraB, out)


def prepare(nc, ps, K, M, x, Wq0, bq0, Wk0, bk0, Wk1, Wv1):
    with ExitStack() as c:
        def sb(name, shape, dt):
            return c.enter_context(nc.sbuf_tensor(name, shape, dt))

        def sem(name):
            return c.enter_context(nc.semaphore(name))

        raw = sb("w_raw", [128, 4, DC, 512], fp32)
        spl = sb("w_spl", [128, 2, 2, DC, 512], fp16)
        bcol = sb("b_col", [128, 2, DC], fp32)
        wb32 = sb("wb32", [128, DC], fp32)
        s_w = [sem(f"p_w{i}") for i in range(4)]
        s_b, s_xin, s_id, s_hi, s_lo, s_m, s_mh, s_ml, s_col, s_wb = (
            sem(n) for n in ("p_b", "p_x", "p_id", "p_hi", "p_lo", "p_m", "p_mh", "p_ml", "p_col", "p_wb"))
        block = c.enter_context(nc.Block())

        @block.sync
        def _(sp):
            for i, w in enumerate((Wq0, Wk0, Wk1, Wv1)):
                sp.dma_start(raw[:, i], w.rearrange("(c p) n -> p c n", p=128)).then_inc(s_w[i], 16)
            sp.dma_start(K["x"][:, :, :], x.rearrange("b (q p) d -> p (b q) d", p=128)).then_inc(s_xin, 16)
            sp.wait_ge(s_xin, 16)

        @block.gpsimd
        def _(pool):
            nc.gpsimd.memset(K["id32"][:, :], 0.0).then_inc(s_id, 1)
            nc.gpsimd.memset(K["id16"][:, :], 0.0).then_inc(s_id, 1)
            nc.gpsimd.memset(K["mhalf"][:, :], -0.5)
            pool.wait_ge(s_id, 2)
            for m in (K["id32"], K["id16"]):
                nc.gpsimd.affine_select(out=m[:, :], in_=m[:, :], compare_op=ALU.not_equal, fill=1.0, base=0,
                                        pattern=[[-1, 128]], channel_multiplier=1).then_inc(s_id, 1)

        @block.scalar
        def _(act):
            act.dma_start(bcol[:, 0, :], bq0.rearrange("(c p) -> p c", p=128), allow_slow_non_contiguous=True).then_inc(s_b, 16)
            act.dma_start(bcol[:, 1, :], bk0.rearrange("(c p) -> p c", p=128), allow_slow_non_contiguous=True).then_inc(s_b, 16)
            for i, dst in enumerate((spl[:, 0, 0], spl[:, 1, 0], K["wk"][:, 0], K["wv"][:, 0])):
                act.wait_ge(s_w[i], 16)
                nc.scalar.activation(dst, raw[:, i], ACT.Copy, scale=SW).then_inc(s_hi, 1)
            for i in range(DC):
                act.wait_ge(s_m, i + 1)
                nc.scalar.activation(M["m"][:, 0, i, :], ps[:, i, :], ACT.Copy, scale=1.0 / SW).then_inc(s_mh, 1)

        @block.vector
        def _(dve):
            for i, (hi, lo) in enumerate(((spl[:, 0, 0], spl[:, 0, 1]), (spl[:, 1, 0], spl[:, 1, 1]),
                                          (K["wk"][:, 0], K["wk"][:, 1]), (K["wv"][:, 0], K["wv"][:, 1]))):
                dve.wait_ge(s_hi, i + 1)
                nc.vector.scalar_tensor_tensor(lo.rearrange("p c n -> p (c n)"), raw[:, i].rearrange("p c n -> p (c n)"),
                                               SW, hi.rearrange("p c n -> p (c n)"),
                                               ALU.mult, ALU.subtract).then_inc(s_lo, 1)
            for i in range(DC):
                dve.wait_ge(s_mh, i + 1)
                nc.vector.scalar_tensor_tensor(M["m"][:, 1, i, :], ps[:, i, :], 1.0 / SW, M["m"][:, 0, i, :],
                                               ALU.mult, ALU.subtract).then_inc(s_ml, 1)
            f0 = SQ / math.sqrt(D)
            dve.wait_ge(s_col, 1)
            nc.vector.tensor_scalar(M["qb"][:, :], ps[:, 4, 0:DC], f0, None, ALU.mult)
            nc.vector.tensor_scalar(M["c0"][:, :], ps[:, 6, 0:1], SX * f0, None, ALU.mult)
            nc.vector.tensor_scalar(wb32[:, :], ps[:, 5, 0:DC], SX, None, ALU.mult).then_inc(s_wb, 1)
            dve.wait_ge(s_wb, 1)
            nc.vector.tensor_copy(M["wb"][:, 0, :], wb32[:, :]).then_inc(s_wb, 1)
            dve.wait_ge(s_wb, 2)
            nc.vector.tensor_tensor(M["wb"][:, 1, :], wb32[:, :], M["wb"][:, 0, :], ALU.subtract)

        @block.tensor
        def _(pe):
            pe.wait_ge(s_lo, 2)
            for i in range(DC):
                for d in range(DC):
                    last = mm3(nc, ps[:, i, :], [spl[:, 0, h, d, i * 128:(i + 1) * 128] for h in range(2)],
                               [spl[:, 1, h, d, :] for h in range(2)], d == 0, d == DC - 1)
                last.then_inc(s_m, 1)
            pe.wait_ge(s_b, 32)
            for bank, w, v in ((4, 1, 0), (5, 0, 1)):
                for i in range(DC):
                    for d in range(DC):
                        nc.tensor.matmul(ps[:, bank, i:i + 1], raw[:, w, d, i * 128:(i + 1) * 128],
                                         bcol[:, v, d:d + 1], start=(d == 0), stop=(d == DC - 1))
            for d in range(DC):
                last = nc.tensor.matmul(ps[:, 6, 0:1], bcol[:, 0, d:d + 1].to_broadcast([128, 128]),
                                        bcol[:, 1, d:d + 1], start=(d == 0), stop=(d == DC - 1))
            last.then_inc(s_col, 1)



def attention0(nc, ps, K, M, ctx4, Wq1, Wo1, k_scr, v_scr, wq_scr, wo_scr):
    with ExitStack() as c:
        def sb(name, shape, dt):
            return c.enter_context(nc.sbuf_tensor(name, shape, dt))

        def sem(name):
            return c.enter_context(nc.semaphore("a_" + name))

        raw = sb("ctx_raw", [128, KT0, D], fp32)
        nat = sb("ctx_nat", [128, 2, KT0, D], fp16)
        ctT = sb("ctx_T", [128, 2, DC, NCP], fp16)
        prob = sb("prob0", [128, NC], fp32)
        pT = sb("probT0", [128, 2, KT0, 128], fp16)
        kst = sb("k_stage", [128, 2, 2, NCP], fp16)
        vst = sb("v_stage", [128, KVH, KT0, 2, HD], fp16)
        xln = sb("xln0", [128, QT, D], fp32)
        xT = sb("xT0", [128, 2, DC, NTOK], fp16)
        q32 = sb("q32", [128, DC, NTOK], fp32)
        qT = sb("qT0", [128, 2, DC, NTOK], fp16)
        wraw = sb("wp_raw", [128, 2, 512], fp32)
        wspl = sb("wp_spl", [128, 2, 2, 512], fp16)
        st = sb("st0", [128, QT, 6], fp32)
        mv = sb("mv0", [128, QT, 2], fp32)
        ve = sb("ve0", [128, QT], fp32)
        yh = sb("yh0", [128, 3, QT], fp32)
        cc = sb("cc0", [128, QT], fp32)
        mx = sb("mx0", [128, QT, 8], fp32)
        rs = sb("rs0", [128, QT, 4], fp32)

        TB, PB = 4, 6
        NG = -(-KT0 // 4)
        t_order = [(s, kt) for kt in range(KT0) for s in ("ctx_hi", "ctx_lo")] + [("ln", q) for q in range(QT)]
        t_order += [("p", q, g) for q in range(QT) for g in range(NG)]
        tj = {name: n for n, name in enumerate(t_order)}
        TJ = len(tj)
        p_order = [("q", i) for i in range(DC)] + [("c", 0)] + [("k", h, j) for h in (0, 1) for j in range(4)]
        p_order += [("k", h, j) for h in (2, 3) for j in range(4)] + [("pv", 0)]
        p_order += [("v", kt) for kt in range(KT0)] + [("pv", 1)]
        pj = {name: n for n, name in enumerate(p_order)}
        PJ = len(pj)
        assert TJ % 2 == 0 and PJ % 2 == 0
        t_split = [x for x in t_order if x[0] in ("ln", "p")]
        p_split = [x for x in p_order if x[0] in ("k", "v")]
        NP = 16
        CH = LN_STEPS + 3 * QT + 3 * QT

        ctx_loaded, nat_hi, nat_lo = sem("ctx_loaded"), sem("nat_hi"), sem("nat_lo")
        t_ready, t_hi, t_free = sem("t_ready"), sem("t_hi"), [sem(f"t_free{i}") for i in range(2)]
        p_ready, p_hi, p_free = sem("p_ready"), sem("p_hi"), [sem(f"p_free{i}") for i in range(2)]
        var_ready, pow_ready, xln_ready, chain_s = sem("var_ready"), sem("pow_ready"), sem("xln_ready"), sem("chain")
        q32_ready, q_hi, q_lo = sem("q32_ready"), sem("q_hi"), sem("q_lo")
        s_ready, s_free, bias_ready = sem("s_ready"), sem("s_free"), sem("bias_ready")
        k_staged, v_staged = sem("k_staged"), sem("v_staged")
        k_stored, v_stored = [sem(f"k_stored{i}") for i in range(2)], sem("v_stored")
        w_hi, w_lo, padded = sem("w_hi"), sem("w_lo"), sem("padded")
        w_loaded, w_stored = [sem(f"w_loaded{i}") for i in range(2)], [sem(f"w_stored{i}") for i in range(2)]
        block = c.enter_context(nc.Block())

        def tbank(n):
            return ps[:, TB + n % 2, :]

        def pbank(n):
            return ps[:, PB + n % 2, :]

        def rows(kt):
            return 128 if kt < KT0 - 1 else REST

        def t_at(b, *job):
            return b * TJ + tj[job] + 1

        def p_at(b, *job):
            return b * PJ + pj[job] + 1

        def t_hi_at(b, *job):
            return b * len(t_split) + t_split.index(job) + 1

        def p_hi_at(b, *job):
            return b * len(p_split) + p_split.index(job) + 1

        def piece(b, i):
            if i < 8:
                return Wq1[i // 2 * 128:(i // 2 + 1) * 128, bass.ds(b * 1024 + i % 2 * 512, 512)], wq_scr[bass.ds(b, 1), i]
            return Wo1[bass.ds(b * 1024 + (i - 8) * 128, 128), :], wo_scr[bass.ds(b, 1), i - 8]

        @block.sync
        def _(sp):
            def load(b):
                sp.dma_start(raw[:, 0:KT0 - 1, :],
                             ctx4[bass.ds(b, 1), 0:(KT0 - 1) * 128, :].rearrange("a (t p) d -> p (a t) d", p=128)
                             ).then_inc(ctx_loaded, 16)
                sp.dma_start(raw[0:REST, KT0 - 1, :],
                             ctx4[bass.ds(b, 1), (KT0 - 1) * 128:NC, :].rearrange("a p d -> p (a d)")
                             ).then_inc(ctx_loaded, 16)

            def stores(b):
                for h in range(KVH):
                    sp.wait_ge(k_staged, b * KVH + h + 1)
                    sp.dma_start(k_scr[bass.ds(b, 1), h].rearrange("a p n -> p (a n)"),
                                 kst[:, h % 2].rearrange("p s n -> p (s n)")).then_inc(k_stored[h % 2], 16)
                sp.wait_ge(v_staged, b + 1)
                for h in range(KVH):
                    sp.dma_start(v_scr[bass.ds(b, 1), h].rearrange("a p n -> p (a n)"),
                                 vst[:, h].rearrange("p t s n -> p (t s n)")).then_inc(v_stored, 16)

            load(0)
            with sp.Fori(0, NB - 1) as b:
                sp.wait_ge(nat_lo, (b + 1) * KT0)
                load(b + 1)
                stores(b)
            stores(NB - 1)
            for s in k_stored:
                sp.wait_ge(s, 16 * (2 * NB + 1))
            sp.wait_ge(v_stored, 16 * KVH * (NB + 1))
            for s in w_stored:
                sp.wait_ge(s, 16 * (NP // 2 * NB + 1))

        @block.gpsimd
        def _(pool):
            nc.gpsimd.memset(kst[:, :, :, NC - 1:NCP], 0.0).then_inc(padded, 1)
            nc.gpsimd.memset(vst[:, :, KT0 - 1], 0.0).then_inc(padded, 1)
            with pool.Fori(0, NB) as b:
                pool.wait_ge(var_ready, b + 1)
                nc.gpsimd.tensor_tensor(yh[:, 0, :], ve[:, :], K["mhalf"][:, :], ALU.pow).then_inc(pow_ready, 1)

        @block.scalar
        def _(act):
            for s in k_stored:
                act.sem_inc(s, 16)
            act.sem_inc(v_stored, 16 * KVH)
            for s in w_stored:
                act.sem_inc(s, 16)
            act.wait_ge(padded, 2)

            def natural_hi(kt):
                nc.scalar.activation(nat[0:rows(kt), 0, kt, :], raw[0:rows(kt), kt, :], ACT.Copy,
                                     scale=SX).then_inc(nat_hi, 1)

            def load_piece(b, i):
                act.dma_start(wraw[:, i % 2, :], piece(b, i)[0]).then_inc(w_loaded[i % 2], 16)

            def store_piece(b, i):
                act.wait_ge(w_lo, b * NP + i + 1)
                act.dma_start(piece(b, i)[1].rearrange("a p n -> p (a n)"),
                              wspl[:, i % 2].rearrange("p s n -> p (s n)")).then_inc(w_stored[i % 2], 16)

            def weights_hi(b, i):
                if i:
                    store_piece(b, i - 1)
                if i + 1 < NP:
                    load_piece(b, i + 1)
                act.wait_ge(w_loaded[i % 2], 16 * (b * (NP // 2) + i // 2 + 1))
                act.wait_ge(w_stored[i % 2], 16 * (b * (NP // 2) + i // 2 + 1))
                nc.scalar.activation(wspl[:, i % 2, 0, :], wraw[:, i % 2, :], ACT.Copy, scale=SW).then_inc(w_hi, 1)

            def exps(b, q):
                act.wait_ge(bias_ready, b * QT + q + 1)
                for j, (o, w) in enumerate(CUT0):
                    nc.scalar.activation(prob[:, o:o + w], ps[:, j, 0:w], ACT.Exp, bias=mx[:, q, 6:7],
                                         scale=1.0 / (SQ * SX), accum_out=rs[:, q, j:j + 1]).then_inc(s_free, 1)

            def keys_hi(b, h):
                act.wait_ge(k_stored[h % 2], 16 * (2 * b + h // 2 + 1))
                for j, (o, w) in enumerate(CUT0):
                    act.wait_ge(p_ready, p_at(b, "k", h, j))
                    nc.scalar.activation(kst[:, h % 2, 0, o:o + w], pbank(pj["k", h, j])[:, 0:w], ACT.Copy,
                                         scale=1.0 / SW).then_inc(p_hi, 1)

            def probs_hi(b, q):
                for g in range(NG):
                    t = min(4, KT0 - 4 * g)
                    r = rows(4 * g)
                    act.wait_ge(t_ready, t_at(b, "p", q, g))
                    nc.scalar.activation(pT[0:r, 0, 4 * g:4 * g + t, :],
                                         tbank(tj["p", q, g])[0:r, 0:t * 128].rearrange("p (t n) -> p t n", t=t),
                                         ACT.Copy, scale=SP_).then_inc(t_hi, 1)

            with act.Fori(0, NB) as b:
                load_piece(b, 0)
                act.wait_ge(ctx_loaded, (b + 1) * 32)
                natural_hi(0)
                for kt in range(KT0):
                    if kt + 1 < KT0:
                        natural_hi(kt + 1)
                    n = tj["ctx_lo", kt]
                    act.wait_ge(t_ready, t_at(b, "ctx_lo", kt))
                    nc.scalar.activation(ctT[:, 1, :, kt * 128:kt * 128 + rows(kt)],
                                         tbank(n)[:, 0:256].bitcast(fp16).rearrange("p (c n) -> p c n", c=DC)
                                         [:, :, 0:rows(kt)], ACT.Copy).then_inc(t_free[n % 2], 1)
                for q in range(QT):
                    act.wait_ge(t_ready, t_at(b, "ln", q))
                    nc.scalar.activation(xT[:, 0, :, q * 128:(q + 1) * 128],
                                         tbank(tj["ln", q]).rearrange("p (c n) -> p c n", c=DC), ACT.Copy,
                                         scale=SX).then_inc(t_hi, 1)
                for i in range(DC):
                    n = pj["q", i]
                    act.wait_ge(p_ready, p_at(b, "q", i))
                    nc.scalar.activation(q32[:, i, :], pbank(n)[:, 0:NTOK], ACT.Identity, bias=M["qb"][:, i:i + 1],
                                         scale=SQ / math.sqrt(D) / (SX * SW)).then_inc(p_free[n % 2], 1)
                for i in range(DC):
                    n = pj["q", i]
                    act.wait_ge(p_free[n % 2], b * (PJ // 2) + n // 2 + 2)
                    nc.scalar.activation(qT[:, 0, i, :], q32[:, i, :], ACT.Copy).then_inc(q_hi, 1)
                keys_hi(b, 0)
                exps(b, 0)
                keys_hi(b, 1)
                probs_hi(b, 0)
                keys_hi(b, 2)
                exps(b, 1)
                weights_hi(b, 0)
                keys_hi(b, 3)
                weights_hi(b, 1)
                probs_hi(b, 1)
                weights_hi(b, 2)
                act.wait_ge(v_stored, 16 * KVH * (b + 1))
                for kt in range(KT0):
                    act.wait_ge(p_ready, p_at(b, "v", kt))
                    nc.scalar.activation(vst[0:rows(kt), :, kt, 0, :],
                                         pbank(pj["v", kt])[0:rows(kt), :].rearrange("p (h n) -> p h n", h=KVH),
                                         ACT.Copy, scale=1.0 / SW).then_inc(p_hi, 1)
                    weights_hi(b, kt + NP - KT0)
                store_piece(b, NP - 1)
                act.wait_ge(p_ready, p_at(b, "pv", 1))

        @block.vector
        def _(dve):
            def lo(dst, src, scale, hi, done):
                nc.vector.scalar_tensor_tensor(dst, src, scale, hi, ALU.mult, ALU.subtract).then_inc(done, 1)

            def bias(b, q, chain):
                dve.wait_ge(s_ready, b * QT + q + 1)
                for j, (o, w) in enumerate(CUT0):
                    last = nc.vector.reduce_max(mx[:, q, j:j + 1], ps[:, j, 0:w], AX.X)
                chain(last)
                chain(nc.vector.reduce_max(mx[:, q, 4:5], mx[:, q, 0:4], AX.X))
                chain(nc.vector.tensor_scalar(mx[:, q, 5:6], mx[:, q, 4:5], cc[:, q:q + 1], None, ALU.add))
                nc.vector.tensor_scalar(mx[:, q, 6:7], mx[:, q, 5:6], cc[:, q:q + 1], -1.0 / (SQ * SX),
                                        ALU.subtract, ALU.mult).then_inc(bias_ready, 1)

            def keys_lo(b, h):
                for j, (o, w) in enumerate(CUT0):
                    n = pj["k", h, j]
                    dve.wait_ge(p_hi, p_hi_at(b, "k", h, j))
                    lo(kst[:, h % 2, 1, o:o + w], pbank(n)[:, 0:w], 1.0 / SW, kst[:, h % 2, 0, o:o + w], p_free[n % 2])
                dve.wait_ge(p_free[n % 2], b * (PJ // 2) + n // 2 + 2)
                dve.sem_inc(k_staged, 1)

            def probs_lo(b, q):
                for g in range(NG):
                    t = min(4, KT0 - 4 * g)
                    n, r = tj["p", q, g], rows(4 * g)
                    dve.wait_ge(t_hi, t_hi_at(b, "p", q, g))
                    lo(pT[0:r, 1, 4 * g:4 * g + t, :].rearrange("p t n -> p (t n)"), tbank(n)[0:r, 0:t * 128], SP_,
                       pT[0:r, 0, 4 * g:4 * g + t, :].rearrange("p t n -> p (t n)"), t_free[n % 2])

            def weights_lo(b, i):
                dve.wait_ge(w_hi, b * NP + i + 1)
                lo(wspl[:, i % 2, 1, :], wraw[:, i % 2, :], SW, wspl[:, i % 2, 0, :], w_lo)

            def row_sum(b, q, chain):
                dve.wait_ge(s_free, 4 * (b * QT + q + 1) + 4)
                chain(nc.vector.reduce_sum(mx[:, q, 7:8], rs[:, q, :], AX.X))
                chain(nc.vector.reciprocal(mx[:, q, 7:8], mx[:, q, 7:8]))
                chain(nc.vector.tensor_scalar(mx[:, q, 7:8], mx[:, q, 7:8], 1.0 / (SP_ * SX), None, ALU.mult))

            def attended(b, q):
                n = pj["pv", q]
                xs = K["x"][:, bass.ds(b * QT + q, 1), :].rearrange("p a d -> p (a d)")
                dve.wait_ge(p_ready, p_at(b, "pv", q))
                nc.vector.scalar_tensor_tensor(xs, pbank(n), mx[:, q, 7:8], xs, ALU.mult,
                                               ALU.add).then_inc(p_free[n % 2], 1)

            with dve.Fori(0, NB) as b:
                chain = Chain(dve, chain_s, b * CH)
                layer_norm_stats(nc, dve, chain, K["x"][:, bass.ds(b * QT, QT), :], st, mv, ve, yh,
                                 var_ready, b + 1, pow_ready, b + 1)
                for q in range(QT):
                    nc.vector.tensor_scalar(xln[:, q, :],
                                            K["x"][:, bass.ds(b * QT + q, 1), :].rearrange("p a d -> p (a d)"),
                                            mv[:, q, 0:1], yh[:, 2, q:q + 1], ALU.subtract,
                                            ALU.mult).then_inc(xln_ready, 1)
                for kt in range(KT0):
                    r = rows(kt)
                    dve.wait_ge(nat_hi, b * KT0 + kt + 1)
                    lo(nat[0:r, 1, kt, :], raw[0:r, kt, :], SX, nat[0:r, 0, kt, :], nat_lo)
                    n = tj["ctx_hi", kt]
                    dve.wait_ge(t_ready, t_at(b, "ctx_hi", kt))
                    nc.vector.tensor_copy(ctT[:, 0, :, kt * 128:kt * 128 + r],
                                          tbank(n)[:, 0:256].bitcast(fp16).rearrange("p (c n) -> p c n", c=DC)
                                          [:, :, 0:r]).then_inc(t_free[n % 2], 1)
                for q in range(QT):
                    n = tj["ln", q]
                    dve.wait_ge(t_hi, t_hi_at(b, "ln", q))
                    lo(xT[:, 1, :, q * 128:(q + 1) * 128], tbank(n).rearrange("p (c n) -> p c n", c=DC), SX,
                       xT[:, 0, :, q * 128:(q + 1) * 128], t_free[n % 2])
                for i in range(DC):
                    dve.wait_ge(q_hi, b * DC + i + 1)
                    nc.vector.tensor_tensor(qT[:, 1, i, :], q32[:, i, :], qT[:, 0, i, :],
                                            ALU.subtract).then_inc(q_lo, 1)
                n = pj["c", 0]
                dve.wait_ge(p_ready, p_at(b, "c", 0))
                nc.vector.tensor_scalar(cc[:, :], pbank(n)[:, 0:QT], SQ / math.sqrt(D) / SX, M["c0"][:, 0:1],
                                        ALU.mult, ALU.add).then_inc(p_free[n % 2], 1)
                bias(b, 0, chain)
                keys_lo(b, 0)
                keys_lo(b, 1)
                probs_lo(b, 0)
                row_sum(b, 0, chain)
                bias(b, 1, chain)
                keys_lo(b, 2)
                weights_lo(b, 0)
                keys_lo(b, 3)
                weights_lo(b, 1)
                attended(b, 0)
                probs_lo(b, 1)
                row_sum(b, 1, chain)
                weights_lo(b, 2)
                for kt in range(KT0):
                    n, r = pj["v", kt], rows(kt)
                    dve.wait_ge(p_hi, p_hi_at(b, "v", kt))
                    lo(vst[0:r, :, kt, 1, :], pbank(n)[0:r, :].rearrange("p (h n) -> p h n", h=KVH), 1.0 / SW,
                       vst[0:r, :, kt, 0, :], p_free[n % 2])
                    weights_lo(b, kt + NP - KT0)
                dve.wait_ge(p_free[n % 2], b * (PJ // 2) + n // 2 + 2)
                dve.sem_inc(v_staged, 1)
                attended(b, 1)
                assert chain.n == CH, chain.n

        @block.tensor
        def _(pe):
            for s in t_free + p_free:
                pe.sem_inc(s, 1)
            pe.sem_inc(s_free, 4)

            def take(b, ring, free, per, n):
                pe.wait_ge(free[n % 2], b * (per // 2) + n // 2 + 1)
                return ring(n)

            def t_take(b, *job):
                return take(b, tbank, t_free, TJ, tj[job])

            def p_take(b, *job):
                return take(b, pbank, p_free, PJ, pj[job])

            def scores(b, q):
                for j, (o, w) in enumerate(CUT0):
                    pe.wait_ge(s_free, 4 * (b * QT + q) + j + 1)
                    for i in range(DC):
                        last = mm3(nc, ps[:, j, 0:w], [qT[:, s, i, q * 128:(q + 1) * 128] for s in range(2)],
                                   [ctT[:, s, i, o:o + w] for s in range(2)], i == 0, i == DC - 1)
                last.then_inc(s_ready, 1)

            def keys(b, h):
                for j, (o, w) in enumerate(CUT0):
                    out = p_take(b, "k", h, j)
                    for i in range(DC):
                        last = mm3(nc, out[:, 0:w], [K["wk"][:, s, i, h * 128:(h + 1) * 128] for s in range(2)],
                                   [ctT[:, s, i, o:o + w] for s in range(2)], i == 0, i == DC - 1)
                    last.then_inc(p_ready, 1)

            def turn(b, q):
                pe.wait_ge(s_free, 4 * (b * QT + q + 1) + 4)
                for g in range(NG):
                    out = t_take(b, "p", q, g)
                    for kt in range(4 * g, min(4 * g + 4, KT0)):
                        o = (kt - 4 * g) * 128
                        last = nc.tensor.transpose(out[0:rows(kt), o:o + 128], prob[:, kt * 128:kt * 128 + rows(kt)],
                                                   K["id32"][:, :])
                    last.then_inc(t_ready, 1)

            def attend(b, q):
                out = p_take(b, "pv", q)
                n = tj["p", q, NG - 1]
                pe.wait_ge(t_free[n % 2], b * (TJ // 2) + n // 2 + 2)
                n = tj["p", q, NG - 2]
                pe.wait_ge(t_free[n % 2], b * (TJ // 2) + n // 2 + 2)
                for kt in range(KT0):
                    r = rows(kt)
                    last = mm3(nc, out, [pT[0:r, s, kt, :] for s in range(2)], [nat[0:r, s, kt, :] for s in range(2)],
                               kt == 0, kt == KT0 - 1)
                last.then_inc(p_ready, 1)

            with pe.Fori(0, NB) as b:
                for kt in range(KT0):
                    r = rows(kt)
                    for s, (name, sm) in enumerate((("ctx_hi", nat_hi), ("ctx_lo", nat_lo))):
                        pe.wait_ge(sm, b * KT0 + kt + 1)
                        out = t_take(b, name, kt)[:, 0:256].bitcast(fp16)
                        for i in range(DC):
                            last = nc.tensor.transpose(out[:, i * 128:i * 128 + r], nat[0:r, s, kt, i * 128:(i + 1) * 128],
                                                       K["id16"][0:r, 0:r])
                        last.then_inc(t_ready, 1)
                for q in range(QT):
                    pe.wait_ge(xln_ready, b * QT + q + 1)
                    out = t_take(b, "ln", q)
                    for i in range(DC):
                        last = nc.tensor.transpose(out[:, i * 128:(i + 1) * 128], xln[:, q, i * 128:(i + 1) * 128],
                                                   K["id32"][:, :])
                    last.then_inc(t_ready, 1)
                for q in range(QT):
                    n = tj["ln", q]
                    pe.wait_ge(t_free[n % 2], b * (TJ // 2) + n // 2 + 2)
                for i in range(DC):
                    out = p_take(b, "q", i)
                    for j in range(DC):
                        last = mm3(nc, out[:, 0:NTOK], [M["m"][:, s, j, i * 128:(i + 1) * 128] for s in range(2)],
                                   [xT[:, s, j, :] for s in range(2)], j == 0, j == DC - 1)
                    last.then_inc(p_ready, 1)
                out = p_take(b, "c", 0)
                for q in range(QT):
                    for j in range(DC):
                        last = mm3(nc, out[:, q:q + 1], [xT[:, s, j, q * 128:(q + 1) * 128] for s in range(2)],
                                   [M["wb"][:, s, j:j + 1] for s in range(2)], j == 0, j == DC - 1)
                last.then_inc(p_ready, 1)
                pe.wait_ge(q_lo, (b + 1) * DC)
                for s in ("ctx_hi", "ctx_lo"):
                    n = tj[s, KT0 - 1]
                    pe.wait_ge(t_free[n % 2], b * (TJ // 2) + n // 2 + 2)
                scores(b, 0)
                keys(b, 0)
                keys(b, 1)
                turn(b, 0)
                scores(b, 1)
                keys(b, 2)
                keys(b, 3)
                attend(b, 0)
                turn(b, 1)
                for kt in range(KT0):
                    r = rows(kt)
                    out = p_take(b, "v", kt)
                    for i in range(DC):
                        last = mm3(nc, out[0:r, :], [ctT[:, s, i, kt * 128:kt * 128 + r] for s in range(2)],
                                   [K["wv"][:, s, i, :] for s in range(2)], i == 0, i == DC - 1)
                    last.then_inc(p_ready, 1)
                attend(b, 1)


def ffn0(nc, ps, K, Wup, Wdn):
    with ExitStack() as c:
        def sb(name, shape, dt):
            return c.enter_context(nc.sbuf_tensor(name, shape, dt))

        def sem(name):
            return c.enter_context(nc.semaphore("f_" + name))

        upT = sb("up_T", [128, DC, F], bf16)
        dnT = sb("down_T", [128, FC, D], bf16)
        id_b = sb("id_b", [128, 128], bf16)
        ones = sb("ones", [128, 128], fp32)
        tot = sb("tot", [128, 2, 6], fp32)
        with ExitStack() as w:
            NWT = F * D // 128 // 2048
            raw = w.enter_context(nc.sbuf_tensor("ffn_raw", [128, 2, NWT, 2048], fp32))
            gt = w.enter_context(nc.sbuf_tensor("ffn_gt", [128, 2, 2048], bf16))
            tern = w.enter_context(nc.sbuf_tensor("ffn_tern", [128, 2, NWT, 2048], bf16))
            part = w.enter_context(nc.sbuf_tensor("ffn_part", [128, 2, NWT], fp32))

            def semw(name):
                return w.enter_context(nc.semaphore("fw_" + name))

            loaded = [[semw(f"loaded{i}_{t}") for t in range(NWT)] for i in range(2)]
            ones_s, sum_s, tot_s, thr_s, tern_s, tr_s, ev_s, ch_s, idb_s = (
                semw(n) for n in ("ones", "sum", "tot", "thr", "tern", "tr", "ev", "ch", "idb"))
            block = w.enter_context(nc.Block())

            @block.sync
            def _(sp):
                for t in range(NWT):
                    sp.dma_start(raw[:, 0, t, :].rearrange("p (a n) -> p a n", a=4),
                                 Wup[t * 512:(t + 1) * 512, :].rearrange("(a p) n -> p a n", p=128)
                                 ).then_inc(loaded[0][t], 16)
                for t in range(NWT):
                    sp.dma_start(raw[:, 1, t, :], Wdn[t * 128:(t + 1) * 128, :]).then_inc(loaded[1][t], 16)

            @block.gpsimd
            def _(pool):
                nc.gpsimd.memset(ones[:, :], 1.0).then_inc(ones_s, 1)
                nc.gpsimd.tensor_copy(id_b[:, :], K["id16"][:, :]).then_inc(idb_s, 1)

            @block.vector
            def _(dve):
                chain = Chain(dve, ch_s)
                for i in range(2):
                    for t in range(NWT):
                        dve.wait_ge(loaded[i][t], 16)
                        chain(nc.vector.tensor_scalar(raw[:, i, t, :], raw[:, i, t, :], 1.0, -1.0, ALU.min, ALU.max))
                        last = nc.vector.tensor_reduce(part[:, i, t:t + 1], raw[:, i, t, :], AX.X, ALU.add,
                                                       apply_absolute_value=True)
                    chain(last)
                    nc.vector.reduce_sum(tot[:, i, 0:1], part[:, i, :], AX.X).then_inc(sum_s, 1)
                for i in range(2):
                    dve.wait_ge(tot_s, i + 1)
                    chain(nc.vector.tensor_scalar(tot[:, i, 1:2], ps[:, 6 + i, 0:1], 1.0 / (F * D), EPS, ALU.mult, ALU.add))
                    nc.vector.tensor_scalar(tot[:, i, 2:3], tot[:, i, 1:2], 0.5, None, ALU.mult)
                    chain(nc.vector.tensor_scalar(tot[:, i, 3:4], tot[:, i, 1:2], -0.5, None, ALU.mult))
                    for t in range(NWT):
                        chain(nc.vector.tensor_scalar(gt[:, t % 2, :], raw[:, i, t, :], tot[:, i, 2:3], None, ALU.is_gt))
                        nc.vector.scalar_tensor_tensor(tern[:, i, t, :], raw[:, i, t, :], tot[:, i, 3:4], gt[:, t % 2, :],
                                                       ALU.is_lt, ALU.subtract).then_inc(tern_s, 1)

            @block.tensor
            def _(pe):
                pe.wait_ge(ones_s, 1)
                for i in range(2):
                    pe.wait_ge(sum_s, i + 1)
                    nc.tensor.matmul(ps[:, 6 + i, 0:1], ones[:, :], tot[:, i, 0:1], start=True, stop=True).then_inc(tot_s, 1)
                pe.wait_ge(idb_s, 1)
                n = 0
                for t in range(NWT):
                    pe.wait_ge(tern_s, t + 1)
                    for i in range(DC):
                        if n >= 4:
                            pe.wait_ge(ev_s, n - 3)
                        for a in range(4):
                            last = nc.tensor.transpose(ps[:, n % 4, 0:256].bitcast(bf16)[:, a * 128:(a + 1) * 128],
                                                       tern[:, 0, t, a * 512 + i * 128:a * 512 + (i + 1) * 128], id_b[:, :])
                        last.then_inc(tr_s, 1)
                        n += 1
                for t in range(FC):
                    if t == 0:
                        pe.wait_ge(tern_s, 2 * NWT)
                    pe.wait_ge(ev_s, n - 3)
                    for a in range(DC):
                        last = nc.tensor.transpose(ps[:, n % 4, 0:256].bitcast(bf16)[:, a * 128:(a + 1) * 128],
                                                   tern[:, 1, a, t * 128:(t + 1) * 128], id_b[:, :])
                    last.then_inc(tr_s, 1)
                    n += 1

            @block.scalar
            def _(act):
                n = 0
                for t in range(NWT):
                    for i in range(DC):
                        act.wait_ge(tr_s, n + 1)
                        nc.scalar.activation(upT[:, i, t * 512:(t + 1) * 512], ps[:, n % 4, 0:256].bitcast(bf16),
                                             ACT.Copy, scale=-1.0).then_inc(ev_s, 1)
                        n += 1
                for t in range(FC):
                    act.wait_ge(tr_s, n + 1)
                    nc.scalar.activation(dnT[:, t, :], ps[:, n % 4, 0:256].bitcast(bf16), ACT.Copy,
                                         scale=-1.0).then_inc(ev_s, 1)
                    n += 1

        hr = sb("h_relu", [128, QT, F], fp32)
        hq = sb("h32", [128, F], fp32)
        hb = sb("h_int", [128, QT, F], bf16)
        hT = sb("h_intT", [128, FC, 128], bf16)
        xln = sb("xlnf", [128, QT, D], fp32)
        xq = sb("xq", [128, QT, D], bf16)
        xqT = sb("xqT", [128, QT, DC, 128], bf16)
        st = sb("stf", [128, QT, 6], fp32)
        mv = sb("mvf", [128, QT, 2], fp32)
        ve = sb("vef", [128, QT], fp32)
        yh = sb("yhf", [128, 3, QT], fp32)
        sx = sb("sxf", [128, QT, 3], fp32)
        unit = sb("unit", [128, QT], fp32)
        sh = sb("shf", [128, QT, 4], fp32)
        (var_ready, pow_ready, chain_s, xq_ready, xt_ready, xt_done, up_ready, relu_done,
         hb_ready, ht_ready, ht_done, dn_ready, dn_done, unit_ready) = (sem(n) for n in (
             "var_ready", "pow_ready", "chain", "xq_ready", "xt_ready", "xt_done", "up_ready", "relu_done",
             "hb_ready", "ht_ready", "ht_done", "dn_ready", "dn_done", "unit_ready"))
        CHX, CHH = LN_STEPS + 1 + QT * 5, 5
        CHF = CHX + QT * CHH
        block = c.enter_context(nc.Block())

        @block.gpsimd
        def _(pool):
            with pool.Fori(0, NB) as b:
                pool.wait_ge(var_ready, b + 1)
                nc.gpsimd.tensor_tensor(yh[:, 0, :], ve[:, :], K["mhalf"][:, :], ALU.pow).then_inc(pow_ready, 1)

        @block.tensor
        def _(pe):
            pe.sem_inc(xt_done, 1)
            pe.sem_inc(dn_done, 1)
            pe.sem_inc(ht_done, 2)
            pe.sem_inc(relu_done, 4)

            def turn_tokens(n, q):
                pe.wait_ge(xq_ready, n + 1)
                pe.wait_ge(xt_done, n + 1)
                for i in range(DC):
                    last = nc.tensor.transpose(ps[:, 6, 0:256].bitcast(bf16)[:, i * 128:(i + 1) * 128],
                                               xq[:, q, i * 128:(i + 1) * 128], id_b[:, :])
                last.then_inc(xt_ready, 1)

            def up(n, q):
                pe.wait_ge(xt_done, n + 2)
                for j in range(4):
                    pe.wait_ge(relu_done, 4 * n + j + 1)
                    for i in range(DC):
                        last = nc.tensor.matmul(ps[:, j, :], xqT[:, q, i, :], upT[:, i, j * 512:(j + 1) * 512],
                                                start=(i == 0), stop=(i == DC - 1))
                    last.then_inc(up_ready, 1)

            def down(n, q):
                pe.wait_ge(hb_ready, n + 1)
                for g in range(4):
                    pe.wait_ge(ht_done, 4 * n + g + 1)
                    for a in range(4):
                        t = 4 * g + a
                        last = nc.tensor.transpose(ps[:, 4 + g % 2, 0:256].bitcast(bf16)[:, a * 128:(a + 1) * 128],
                                                   hb[:, q, t * 128:(t + 1) * 128], id_b[:, :])
                    last.then_inc(ht_ready, 1)
                pe.wait_ge(dn_done, n + 1)
                pe.wait_ge(ht_done, 4 * n + 4 + 2)
                for t in range(FC):
                    last = nc.tensor.matmul(ps[:, 7, :], hT[:, t, :], dnT[:, t, :], start=(t == 0), stop=(t == FC - 1))
                last.then_inc(dn_ready, 1)

            def body(b, more):
                up(b * QT + 1, 1)
                down(b * QT, 0)
                if more:
                    turn_tokens(b * QT + 2, 0)
                    turn_tokens(b * QT + 3, 1)
                    up(b * QT + 2, 0)
                down(b * QT + 1, 1)

            turn_tokens(0, 0)
            turn_tokens(1, 1)
            up(0, 0)
            with pe.Fori(0, NB - 1) as b:
                body(b, True)
            body(NB - 1, False)

        @block.scalar
        def _(act):
            def tokens(n, q):
                act.wait_ge(xt_ready, n + 1)
                nc.scalar.activation(xqT[:, q].rearrange("p c n -> p (c n)"), ps[:, 6, 0:256].bitcast(bf16),
                                     ACT.Copy).then_inc(xt_done, 1)

            def relu(n, q):
                act.wait_ge(unit_ready, n + 1)
                for j in range(4):
                    act.wait_ge(up_ready, 4 * n + j + 1)
                    nc.scalar.activation(hr[:, q, j * 512:(j + 1) * 512], ps[:, j, :], ACT.Relu,
                                         scale=unit[:, q:q + 1]).then_inc(relu_done, 1)

            def hidden(n):
                for g in range(4):
                    act.wait_ge(ht_ready, 4 * n + g + 1)
                    nc.scalar.activation(hT[:, 4 * g:4 * g + 4, :].rearrange("p t n -> p (t n)"),
                                         ps[:, 4 + g % 2, 0:256].bitcast(bf16), ACT.Copy).then_inc(ht_done, 1)

            def body(b, more):
                relu(b * QT + 1, 1)
                hidden(b * QT)
                if more:
                    tokens(b * QT + 2, 0)
                    tokens(b * QT + 3, 1)
                    relu(b * QT + 2, 0)
                hidden(b * QT + 1)

            tokens(0, 0)
            tokens(1, 1)
            relu(0, 0)
            with act.Fori(0, NB - 1) as b:
                body(b, True)
            body(NB - 1, False)

        @block.vector
        def _(dve):
            def xs(n):
                return K["x"][:, n, :] if isinstance(n, int) else K["x"][:, bass.ds(n, 1), :].rearrange("p a d -> p (a d)")

            def unit_of(q):
                nc.vector.tensor_scalar(unit[:, q:q + 1], sx[:, q, 0:1], tot[:, 0, 1:2], 1.0 / 127.0, ALU.mult,
                                        ALU.mult).then_inc(unit_ready, 1)

            def quantised_tokens(b, chain):
                layer_norm_stats(nc, dve, chain, K["x"][:, bass.ds(b * QT, QT), :], st, mv, ve, yh,
                                 var_ready, b + 1, pow_ready, b + 1)
                for q in range(QT):
                    last = nc.vector.tensor_scalar(xln[:, q, :], xs(b * QT + q), mv[:, q, 0:1], yh[:, 2, q:q + 1],
                                                   ALU.subtract, ALU.mult)
                chain(last)
                for q in range(QT):
                    chain(nc.vector.tensor_reduce(sx[:, q, 0:1], xln[:, q, :], AX.X, ALU.max, apply_absolute_value=True))
                    chain(nc.vector.tensor_scalar(sx[:, q, 0:1], sx[:, q, 0:1], EPS, None, ALU.max))
                    chain(nc.vector.reciprocal(sx[:, q, 1:2], sx[:, q, 0:1]))
                    chain(nc.vector.tensor_scalar(sx[:, q, 1:2], sx[:, q, 1:2], 127.0, None, ALU.mult))
                    if q == 0:
                        unit_of(0)
                    chain(nc.vector.tensor_scalar(xln[:, q, :], xln[:, q, :], sx[:, q, 1:2], MAGIC, ALU.mult, ALU.add))
                    nc.vector.tensor_scalar(xq[:, q, :], xln[:, q, :], MAGIC, 127.0, ALU.subtract,
                                            ALU.min).then_inc(xq_ready, 1)

            def quantised_hidden(n, q, chain):
                if q:
                    dve.wait_ge(hb_ready, n)
                dve.wait_ge(relu_done, 4 * n + 4 + 4)
                nc.vector.memset(sh[:, q, 3:4], EPS)
                chain(nc.vector.tensor_tensor_reduce(out=hq[:, :], in0=hr[:, q, :], in1=hr[:, q, :], scale=1.0, scalar=0.0,
                                                     op0=ALU.mult, op1=ALU.max, accum_out=sh[:, q, 0:1]))
                chain(nc.vector.tensor_scalar(sh[:, q, 0:1], sh[:, q, 0:1], sh[:, q, 3:4], None, ALU.max))
                chain(nc.vector.reciprocal(sh[:, q, 1:2], sh[:, q, 0:1]))
                chain(nc.vector.tensor_scalar(sh[:, q, 1:2], sh[:, q, 1:2], 127.0, None, ALU.mult))
                nc.vector.tensor_scalar(sh[:, q, 2:3], sh[:, q, 0:1], tot[:, 1, 1:2], 1.0 / 127.0, ALU.mult, ALU.mult)
                chain(nc.vector.tensor_scalar(hq[:, :], hq[:, :], sh[:, q, 1:2], MAGIC, ALU.mult, ALU.add))
                nc.vector.tensor_scalar(hb[:, q, :], hq[:, :], MAGIC, 127.0, ALU.subtract, ALU.min).then_inc(hb_ready, 1)

            def result(n, q):
                dve.wait_ge(dn_ready, n + 1)
                nc.vector.scalar_tensor_tensor(xs(n), ps[:, 7, :], sh[:, q, 2:3], xs(n), ALU.mult,
                                               ALU.add).then_inc(dn_done, 1)

            def body(b, more):
                chain = Chain(dve, chain_s, b * CHF + CHX)
                quantised_hidden(b * QT, 0, chain)
                if more:
                    quantised_tokens(b + 1, chain)
                quantised_hidden(b * QT + 1, 1, chain)
                if more:
                    unit_of(1)
                result(b * QT, 0)
                result(b * QT + 1, 1)
                assert chain.n == (CHF if more else CHF - CHX), chain.n

            quantised_tokens(0, Chain(dve, chain_s))
            unit_of(1)
            with dve.Fori(0, NB - 1) as b:
                body(b, True)
            body(NB - 1, False)


def attention1(nc, ps, K, k_scr, v_scr, wq_scr, wo_scr):
    NTL = GRP * QT
    TB, OB = 4, 6
    with ExitStack() as c:
        def sb(name, shape, dt):
            return c.enter_context(nc.sbuf_tensor(name, shape, dt))

        xT = sb("xT1", [128, 2, DC, NB * NTOK], fp16)
        layer_norm_turned(nc, ps, K, xT, SX, "c")

        def sem(name):
            return c.enter_context(nc.semaphore("c_" + name))

        wq = sb("wq_s", [128, DC, 2, 2, 512], fp16)
        wo = sb("wo_s", [128, GRP, 2, 512], fp16)
        kb = sb("keys", [128, 2, NKP], fp16)
        vb = sb("values", [128, KT1, 2, HD], fp16)
        qT = sb("qT1", [128, 2, GRP, NTOK], fp16)
        prob = sb("prob1", [128, 2, NK], fp32)
        pT = sb("probT1", [128, 2, 2, KT1, NTOK], fp16)
        rb = sb("rb", [128, 2, NTOK], fp32)
        o32 = sb("o32", [128, 2, NTOK], fp32)
        oT = sb("oT", [128, 2, GRP, NTOK], fp16)
        mx = sb("mx1", [128, 4, 6], fp32)
        rs = sb("rs1", [128, 4, 4], fp32)

        order = [("kl",), ("q", 0), ("vl",), ("q", 1), ("q", 2), ("q", 3)] + [("p", 0, 0, g) for g in range(4)]
        order += [("q", h) for h in range(4, 8)] + [("p", 0, 1, g) for g in range(4)]
        order += [("p", h, q, g) for h in range(1, GRP) for q in range(QT) for g in range(4)]
        order += [("wo", q) for q in range(QT)]
        jobs = {name: n for n, name in enumerate(order)}
        TJ = len(order)
        SPLIT = TJ - QT
        assert TJ % 2 == 0

        wq_loaded, wo_loaded, k_loaded, v_loaded = sem("wq_loaded"), sem("wo_loaded"), sem("k_loaded"), sem("v_loaded")
        t_ready, t_hi, t_free = sem("t_ready"), sem("t_hi"), [sem(f"t_free{i}") for i in range(2)]
        s_ready, max_done, bias_ready, s_free = sem("s_ready"), sem("max_done"), sem("bias_ready"), sem("s_free")
        sum_done, r_ready = sem("sum_done"), sem("r_ready")
        o_ready, rb_ready, o_free = sem("o_ready"), sem("rb_ready"), sem("o_free")
        ot_hi, ot_lo = sem("ot_hi"), sem("ot_lo")
        block = c.enter_context(nc.Block())

        def job(h, q, g):
            if isinstance(h, int):
                return jobs["p", h, q, g]
            return (h - 1) * 8 + (jobs["p", 1, 0, 0] + 4 * q + g)

        def bank(par):
            return ps[:, TB + par, :]

        def par(q, g):
            return (jobs["p", 1, q, g]) % 2

        assert jobs["p", 0, 0, 0] % 2 == jobs["p", 1, 0, 0] % 2 == jobs["p", 0, 1, 0] % 2

        def flat(p):
            return ps[:, 2 * p:2 * p + 2, :].rearrange("p b n -> p (b n)")

        HALF = [(0, 1024), (1024, NK - 1024)]

        def heads(eng, body):
            with eng.Fori(0, (GRP - 2) // 2) as i:
                for e in range(2):
                    body(i * 2 + (1 + e), (1 + e) % 2)

        @block.sync
        def _(sp):
            def load_wq(kv):
                sp.dma_start(wq[:, :, :, :, :].rearrange("p i c s n -> p (i c) (s n)"),
                             wq_scr[bass.ds(kv, 1)].rearrange("a i p n -> p (a i) n")
                             ).then_inc(wq_loaded, 16)

            def units(kv):
                sp.wait_ge(t_ready, kv * (NB * TJ) + 1)
                sp.dma_start(wo[:, :, :, :].rearrange("p i s n -> p i (s n)"),
                             wo_scr[bass.ds(kv, 1)].rearrange("a i p n -> p (a i) n")
                             ).then_inc(wo_loaded, 16)
                with sp.Fori(0, NB) as b:
                    u = kv * NB + b
                    sp.wait_ge(s_ready, u * (4 * NTL) + 1)
                    sp.dma_start(kb[:, :, NTOK:NKP], k_scr[bass.ds(b, 1), bass.ds(kv, 1)].rearrange(
                        "a h p (s n) -> p (a h s) n", s=2)).then_inc(k_loaded, 16)
                    sp.wait_ge(o_ready, u * GRP + 1)
                    sp.dma_start(vb[:, 2:KT1], v_scr[bass.ds(b, 1), bass.ds(kv, 1)].rearrange(
                        "a h p n -> p (a h n)")).then_inc(v_loaded, 16)

            load_wq(0)
            with sp.Fori(0, KVH - 1) as kv:
                units(kv)
                sp.wait_ge(t_ready, kv * (NB * TJ) + (NB - 1) * TJ + jobs["q", 7] + 2)
                load_wq(kv + 1)
            units(KVH - 1)

        @block.gpsimd
        def _(pool):
            with pool.Fori(0, KVH * NB) as u:
                def post(h, p):
                    G = u * GRP + h
                    pool.wait_ge(o_free, G + 3)
                    dst = [oT[:, s, bass.ds(h, 1), :].rearrange("p a n -> p (a n)") for s in range(2)]
                    nc.gpsimd.tensor_copy(dst[0], o32[:, p, :]).then_inc(ot_hi, 1)
                    pool.wait_ge(ot_hi, G + 1)
                    nc.gpsimd.tensor_tensor(dst[1], o32[:, p, :], dst[0], ALU.subtract).then_inc(ot_lo, 1)

                with pool.Fori(0, GRP // 2) as i:
                    for e in range(2):
                        post(i * 2 + e, e)

        @block.scalar
        def _(act):
            with act.Fori(0, KVH * NB) as u:
                def hi(n, dst, src, scale):
                    act.wait_ge(t_ready, u * TJ + n + 2)
                    nc.scalar.activation(dst, src, ACT.Copy, scale=scale).then_inc(t_hi, 1)

                def query_hi(h):
                    n = jobs["q", h]
                    hi(n, qT[:, 0, h, :], bank(n % 2)[:, 0:NTOK], SQ / math.sqrt(HD) / (SX * SW))

                def exps(h, q, p):
                    s = 2 * p + q
                    act.wait_ge(bias_ready, u * NTL + h * QT + q + 1)
                    for k, (o, w) in enumerate(HALF):
                        nc.scalar.activation(prob[:, q, o:o + w], flat(k)[:, 0:w], ACT.Exp, bias=mx[:, s, 5:6],
                                             scale=1.0 / (SQ * SX), accum_out=rs[:, s, k:k + 1]).then_inc(s_free, 1)

                def turned_hi(h, q, p):
                    for g in range(4):
                        t = min(4, KT1 - 4 * g)
                        hi(job(h, q, g), pT[:, p, 0, 4 * g:4 * g + t, q * 128:(q + 1) * 128],
                           bank(par(q, g))[:, 0:t * 128].rearrange("p (t n) -> p t n", t=t), SP_)

                def recip(h, p):
                    act.wait_ge(o_ready, u * GRP + h + 2)
                    nc.scalar.activation(rb[:, p, :], ps[:, OB + p, NTOK:2 * NTOK], ACT.Copy,
                                         scale=1.0 / SP_).then_inc(rb_ready, 1)

                n = jobs["kl",]
                hi(n, kb[:, 0, 0:NTOK], bank(n % 2)[:, 0:NTOK], 1.0 / SW)
                query_hi(0)
                n = jobs["vl",]
                hi(n, vb[:, 0:QT, 0, :], bank(n % 2)[:, 0:NTOK].rearrange("p (t n) -> p t n", t=QT), 1.0 / SW)
                exps(0, 0, 0)
                for h in range(1, 4):
                    query_hi(h)
                turned_hi(0, 0, 0)
                exps(0, 1, 0)
                for h in range(4, 8):
                    query_hi(h)
                turned_hi(0, 1, 0)
                exps(1, 0, 1)

                def body(h, p):
                    turned_hi(h, 0, p)
                    exps(h, 1, p)
                    turned_hi(h, 1, p)
                    exps(h + 1, 0, 1 - p)
                    recip(h - 1, 1 - p)

                heads(act, body)
                h = GRP - 1
                turned_hi(h, 0, h % 2)
                exps(h, 1, h % 2)
                turned_hi(h, 1, h % 2)
                recip(h - 1, 1 - h % 2)
                recip(h, h % 2)

        @block.vector
        def _(dve):
            with dve.Fori(0, KVH * NB) as u:
                def lo(n, p, dst, src, scale, hi):
                    dve.wait_ge(t_hi, u * SPLIT + n + 1)
                    nc.vector.scalar_tensor_tensor(dst, src, scale, hi, ALU.mult, ALU.subtract).then_inc(t_free[p], 1)

                def query_lo(h):
                    n = jobs["q", h]
                    lo(n, n % 2, qT[:, 1, h, :], bank(n % 2)[:, 0:NTOK], SQ / math.sqrt(HD) / (SX * SW), qT[:, 0, h, :])

                def bank_max(h, q, p, k):
                    T = u * NTL + h * QT + q
                    s = 2 * p + q
                    if k == 3:
                        dve.wait_ge(max_done, 5 * T + 3)
                        nc.vector.reduce_max(mx[:, s, 4:5], mx[:, s, 0:3], AX.X).then_inc(max_done, 1)
                    dve.wait_ge(s_ready, 4 * T + k + 2)
                    nc.vector.reduce_max(mx[:, s, k:k + 1], ps[:, k, 0:CUT1[k][1]], AX.X).then_inc(max_done, 1)

                def bias(h, q, p):
                    s = 2 * p + q
                    dve.wait_ge(max_done, (u * NTL + h * QT + q) * 5 + 5)
                    nc.vector.tensor_scalar(mx[:, s, 5:6], mx[:, s, 3:4], mx[:, s, 4:5], -1.0 / (SQ * SX), ALU.max,
                                            ALU.mult).then_inc(bias_ready, 1)

                def turned_lo(h, q, p, g):
                    t = min(4, KT1 - 4 * g)
                    dst = [pT[:, p, s, 4 * g:4 * g + t, q * 128:(q + 1) * 128] for s in range(2)]
                    lo(job(h, q, g), par(q, g), dst[1],
                       bank(par(q, g))[:, 0:t * 128].rearrange("p (t n) -> p t n", t=t), SP_, dst[0])

                def sums(h, q, p):
                    s = 2 * p + q
                    T = u * NTL + h * QT + q
                    dve.wait_ge(s_free, 2 * T + 4)
                    nc.vector.tensor_tensor(rs[:, s, 2:3], rs[:, s, 0:1], rs[:, s, 1:2], ALU.add).then_inc(sum_done, 1)
                    dve.wait_ge(sum_done, T + 1)
                    nc.vector.reciprocal(rs[:, s, 3:4], rs[:, s, 2:3]).then_inc(r_ready, 1)

                def normalise(h, p):
                    G = u * GRP + h
                    dve.wait_ge(rb_ready, G + 1)
                    dve.wait_ge(ot_lo, G + 1)
                    nc.vector.tensor_tensor(o32[:, p, :], ps[:, OB + p, 0:NTOK], rb[:, p, :],
                                            ALU.mult).then_inc(o_free, 1)

                def step(h, q, p, nxt):
                    if nxt:
                        bank_max(*nxt, 0)
                    turned_lo(h, q, p, 0)
                    if nxt:
                        bank_max(*nxt, 1)
                    turned_lo(h, q, p, 1)
                    if nxt:
                        bank_max(*nxt, 2)
                        bank_max(*nxt, 3)
                        bias(*nxt)
                    turned_lo(h, q, p, 2)
                    turned_lo(h, q, p, 3)
                    sums(h, q, p)

                n = jobs["kl",]
                lo(n, n % 2, kb[:, 1, 0:NTOK], bank(n % 2)[:, 0:NTOK], 1.0 / SW, kb[:, 0, 0:NTOK])
                query_lo(0)
                for k in range(4):
                    bank_max(0, 0, 0, k)
                bias(0, 0, 0)
                n = jobs["vl",]
                lo(n, n % 2, vb[:, 0:QT, 1, :], bank(n % 2)[:, 0:NTOK].rearrange("p (t n) -> p t n", t=QT), 1.0 / SW,
                   vb[:, 0:QT, 0, :])
                for h in range(1, 4):
                    query_lo(h)
                step(0, 0, 0, (0, 1, 0))
                for h in range(4, 8):
                    query_lo(h)
                step(0, 1, 0, (1, 0, 1))

                def body(h, p):
                    step(h, 0, p, (h, 1, p))
                    step(h, 1, p, (h + 1, 0, 1 - p))
                    normalise(h - 1, 1 - p)

                heads(dve, body)
                h = GRP - 1
                step(h, 0, h % 2, (h, 1, h % 2))
                step(h, 1, h % 2, None)
                normalise(h - 1, 1 - h % 2)
                normalise(h, h % 2)
                b = u % NB
                for q in range(QT):
                    n = jobs["wo", q]
                    dve.wait_ge(t_ready, u * TJ + n + 2)
                    xs = K["x"][:, bass.ds(b * QT + q, 1), :].rearrange("p a d -> p (a d)")
                    nc.vector.scalar_tensor_tensor(xs, bank(n % 2), 1.0 / (SX * SW), xs, ALU.mult,
                                                   ALU.add).then_inc(t_free[n % 2], 1)

        @block.tensor
        def _(pe):
            for s in t_free:
                pe.sem_inc(s, 1)
            for s in (s_free, o_free, ot_lo):
                pe.sem_inc(s, 2)
            for s in (s_ready, o_ready, t_ready):
                pe.sem_inc(s, 1)

            def unit(kv, b):
                u = kv * NB + b

                def take(n, p):
                    pe.wait_ge(t_free[p], u * (TJ // 2) + (n + 2 - p) // 2 if isinstance(n, int)
                               else u * (TJ // 2) + n)
                    return bank(p)

                def t_take(h, q, g):
                    p = par(q, g)
                    if isinstance(h, int):
                        pe.wait_ge(t_free[p], u * (TJ // 2) + jobs["p", h, q, g] // 2 + 1)
                    else:
                        pe.wait_ge(t_free[p], u * (TJ // 2) + (h - 1) * 4 + jobs["p", 1, q, g] // 2 + 1)
                    return bank(p)

                def q_take(name):
                    n = jobs[name]
                    pe.wait_ge(t_free[n % 2], u * (TJ // 2) + n // 2 + 1)
                    return bank(n % 2)

                tok = [xT[:, s, :, bass.ds(b * NTOK, NTOK)] for s in range(2)]

                def keys_of_latents():
                    out = q_take(("kl",))
                    for i in range(DC):
                        last = mm3(nc, out[:, 0:NTOK], [K["wk"][:, s, i, bass.ds(kv * HD, HD)] for s in range(2)],
                                   [tok[s][:, i, :] for s in range(2)], i == 0, i == DC - 1)
                    last.then_inc(t_ready, 1)

                def values_of_latents():
                    out = q_take(("vl",))
                    for q in range(QT):
                        for i in range(DC):
                            last = mm3(nc, out[:, q * 128:(q + 1) * 128],
                                       [xT[:, s, i, bass.ds(b * NTOK + q * 128, 128)] for s in range(2)],
                                       [K["wv"][:, s, i, bass.ds(kv * HD, HD)] for s in range(2)], i == 0, i == DC - 1)
                    last.then_inc(t_ready, 1)

                def query(h):
                    out = q_take(("q", h))
                    for i in range(DC):
                        last = mm3(nc, out[:, 0:NTOK], [wq[:, i, h // 4, s, h % 4 * HD:(h % 4 + 1) * HD] for s in range(2)],
                                   [tok[s][:, i, :] for s in range(2)], i == 0, i == DC - 1)
                    last.then_inc(t_ready, 1)

                def scores(h, q, j):
                    T = u * NTL + h * QT + q
                    if j % 2 == 0:
                        pe.wait_ge(s_free, 2 * T + j // 2 + 1)
                    o, w = CUT1[j]
                    qs = [qT[:, s, bass.ds(h, 1), q * 128:(q + 1) * 128].rearrange("p a n -> p (a n)") for s in range(2)]
                    last = mm3(nc, ps[:, j, 0:w], qs, [kb[:, s, o:o + w] for s in range(2)], True, True)
                    last.then_inc(s_ready, 1)

                def turn(h, q, g):
                    T = u * NTL + h * QT + q
                    if g % 2 == 0:
                        pe.wait_ge(s_free, 2 * T + g // 2 + 3)
                    out = t_take(h, q, g)
                    for kt in range(4 * g, min(4 * g + 4, KT1)):
                        r = min(128, NK - kt * 128)
                        o = (kt - 4 * g) * 128
                        last = nc.tensor.transpose(out[0:r, o:o + 128], prob[:, q, kt * 128:kt * 128 + r],
                                                   K["id32"][:, :])
                    last.then_inc(t_ready, 1)

                def step(h, q, nxt):
                    for g in range(4):
                        if nxt:
                            scores(*nxt, g)
                        turn(h, q, g)

                def attend(h, p, k0, k1):
                    if k0 == 0:
                        pe.wait_ge(o_free, u * GRP + h + 1)
                    out = ps[:, OB + p, 0:NTOK]
                    for kt in range(k0, k1):
                        r = min(128, NK - kt * 128)
                        last = mm3(nc, out, [vb[0:r, kt, s, :] for s in range(2)], [pT[0:r, p, s, kt, :] for s in range(2)],
                                   kt == 0, kt == KT1 - 1)

                def spread(h, p):
                    pe.wait_ge(r_ready, u * NTL + h * QT + 2)
                    for q in range(QT):
                        last = nc.tensor.transpose(ps[:, OB + p, NTOK + q * 128:NTOK + (q + 1) * 128],
                                                   rs[:, 2 * p + q, 3:4].to_broadcast([128, 128]), K["id32"][:, :])
                    last.then_inc(o_ready, 1)

                def turned(h, q):
                    for g in (2, 3):
                        n = jobs["p", h, q, g]
                        pe.wait_ge(t_free[par(q, g)], u * (TJ // 2) + n // 2 + 2)

                KM = 8
                pe.wait_ge(wq_loaded, (kv + 1) * 16)
                keys_of_latents()
                query(0)
                pe.wait_ge(v_loaded, (u + 1) * 16)
                pe.wait_ge(k_loaded, (u + 1) * 16)
                for name in (("kl",), ("q", 0)):
                    n = jobs[name]
                    pe.wait_ge(t_free[n % 2], u * (TJ // 2) + n // 2 + 2)
                for j in range(4):
                    scores(0, 0, j)
                values_of_latents()
                for h in range(1, 4):
                    query(h)
                step(0, 0, (0, 1))
                for h in range(4, 8):
                    query(h)
                step(0, 1, (1, 0))

                def body(h, p):
                    step(h, 0, (h, 1))
                    attend(h - 1, 1 - p, 0, KM)
                    step(h, 1, (h + 1, 0))
                    attend(h - 1, 1 - p, KM, KT1)
                    spread(h - 1, 1 - p)

                heads(pe, body)
                h = GRP - 1
                p = h % 2
                step(h, 0, (h, 1))
                attend(h - 1, 1 - p, 0, KM)
                step(h, 1, None)
                attend(h - 1, 1 - p, KM, KT1)
                spread(h - 1, 1 - p)

                def project(q, hs):
                    n = jobs["wo", q]
                    for hh in hs:
                        last = mm3(nc, bank(n % 2), [oT[:, s, hh, q * 128:(q + 1) * 128] for s in range(2)],
                                   [wo[:, hh, s, :] for s in range(2)],
                                   hh == 0, hh == GRP - 1)
                    return last

                pe.wait_ge(wo_loaded, (kv + 1) * 16)
                pe.wait_ge(ot_lo, u * GRP + (GRP - 2) + 2)
                for q in range(QT):
                    q_take(("wo", q))
                    project(q, range(GRP - 2))
                turned(h, 1)
                attend(h, p, 0, KT1)
                spread(h, p)
                pe.wait_ge(ot_lo, u * GRP + (GRP - 1) + 2)
                for q in range(QT):
                    project(q, [GRP - 2])
                pe.wait_ge(ot_lo, u * GRP + GRP + 2)
                for q in range(QT):
                    project(q, [GRP - 1]).then_inc(t_ready, 1)

            with pe.Fori(0, KVH) as kv:
                with pe.Fori(0, NB) as b:
                    unit(kv, b)


def layer_norm_turned(nc, ps, K, xT, scale, tag):
    with ExitStack() as c:
        def sb(name, shape, dt):
            return c.enter_context(nc.sbuf_tensor(name + tag, shape, dt))

        def sem(name):
            return c.enter_context(nc.semaphore(tag + "n_" + name))

        xln = sb("xlnn", [128, 2, QT, D], fp32)
        st = sb("stn", [128, QT, 6], fp32)
        mv = sb("mvn", [128, QT, 2], fp32)
        ve = sb("ven", [128, QT], fp32)
        yh = sb("yhn", [128, 3, QT], fp32)
        var_ready, pow_ready, chain_s, xln_ready, t_ready, t_hi, t_lo = (
            sem(n) for n in ("var_ready", "pow_ready", "chain", "xln_ready", "t_ready", "t_hi", "t_lo"))
        block = c.enter_context(nc.Block())

        @block.gpsimd
        def _(pool):
            for b in range(NB):
                pool.wait_ge(var_ready, b + 1)
                nc.gpsimd.tensor_tensor(yh[:, 0, :], ve[:, :], K["mhalf"][:, :], ALU.pow).then_inc(pow_ready, 1)

        @block.vector
        def _(dve):
            chain = Chain(dve, chain_s)

            def low(b):
                for q in range(QT):
                    n = b * QT + q
                    dve.wait_ge(t_hi, n + 1)
                    nc.vector.scalar_tensor_tensor(xT[:, 1, :, n * 128:(n + 1) * 128],
                                                   ps[:, n % 4, :].rearrange("p (c n) -> p c n", c=DC), scale,
                                                   xT[:, 0, :, n * 128:(n + 1) * 128], ALU.mult,
                                                   ALU.subtract).then_inc(t_lo, 1)

            for b in range(NB):
                layer_norm_stats(nc, dve, chain, K["x"][:, b * QT:(b + 1) * QT, :], st, mv, ve, yh,
                                 var_ready, b + 1, pow_ready, b + 1)
                for q in range(QT):
                    last = nc.vector.tensor_scalar(xln[:, b % 2, q, :], K["x"][:, b * QT + q, :], mv[:, q, 0:1],
                                                   yh[:, 2, q:q + 1], ALU.subtract, ALU.mult)
                    last.then_inc(xln_ready, 1)
                dve.wait_ge(xln_ready, (b + 1) * QT)
                if b:
                    low(b - 1)
            low(NB - 1)

        @block.tensor
        def _(pe):
            for n in range(NT):
                pe.wait_ge(xln_ready, n + 1)
                if n >= 4:
                    pe.wait_ge(t_lo, n - 3)
                for i in range(DC):
                    last = nc.tensor.transpose(ps[:, n % 4, i * 128:(i + 1) * 128],
                                               xln[:, (n // QT) % 2, n % QT, i * 128:(i + 1) * 128], K["id32"][:, :])
                last.then_inc(t_ready, 1)

        @block.scalar
        def _(act):
            for n in range(NT):
                act.wait_ge(t_ready, n + 1)
                nc.scalar.activation(xT[:, 0, :, n * 128:(n + 1) * 128],
                                     ps[:, n % 4, :].rearrange("p (c n) -> p c n", c=DC), ACT.Copy,
                                     scale=scale).then_inc(t_hi, 1)


def ffn1(nc, ps, K, baseW, gateW, loraA, loraB, out):
    GA = NE + NR
    HR = NR // 2
    with ExitStack() as c:
        def sb(name, shape, dt):
            return c.enter_context(nc.sbuf_tensor(name, shape, dt))

        def sem(name):
            return c.enter_context(nc.semaphore("d_" + name))

        xT = sb("xT2", [128, 2, DC, NB * NTOK], fp16)
        layer_norm_turned(nc, ps, K, xT, SX, "d")

        braw = sb("base_raw", [128, DC, D], fp32)
        graw = sb("gate_raw", [NE, D], fp32)
        araw = sb("a_raw", [HR, 2, D], fp32)
        lraw = sb("b_raw", [128, DC, NE, RANK], fp32)
        bT = sb("base_T", [128, 2, DC, D], fp16)
        gaT = sb("ga_T", [128, 2, DC, GA], fp16)
        lT = sb("b_T", [HR, 2, 2, D], fp16)
        iota = sb("iota", [128, NE], fp32)
        ga = sb("ga", [128, 2, GA], fp32)
        top = sb("top", [128, 2, 8], fp32)
        topi = sb("topi", [128, 2, 8], u32)
        tf = sb("tf", [128, 2, 8], fp32)
        gate = sb("gate", [128, 2, 2, NE], fp32)
        hg = sb("hg", [128, 2, NR], fp32)
        hgT = sb("hgT", [HR, 2, 2, 2, 128], fp16)
        y = sb("y", [128, 2, D], fp32)
        loaded = [sem(f"loaded{i}") for i in range(4)]
        (iota_s, w_ready, w_hi, w_lo, ga_ready, ga_free, top_s, ex_ready, pr_ready, hg_ready, ht_ready, ht_hi, ht_lo,
         y_ready, y_free, chain_s) = (sem(n) for n in (
             "iota", "w_ready", "w_hi", "w_lo", "ga_ready", "ga_free", "top", "ex_ready", "pr_ready", "hg_ready",
             "ht_ready", "ht_hi", "ht_lo", "y_ready", "y_free", "chain"))
        stored = [sem(f"stored{i}") for i in range(2)]
        block = c.enter_context(nc.Block())

        prep = []
        for i in range(DC):
            prep.append(([bT[:, s, i, :] for s in range(2)], D, 128))
        for i in range(DC):
            prep.append(([gaT[:, s, i, :] for s in range(2)], GA, 128))
        for r in range(2):
            prep.append(([lT[:, s, r, :] for s in range(2)], D, HR))

        @block.sync
        def _(sp):
            sp.dma_start(braw[:, :, :], baseW.rearrange("(c p) n -> p c n", p=128)).then_inc(loaded[0], 16)
            sp.dma_start(graw[:, :], gateW).then_inc(loaded[1], 16)
            sp.dma_start(araw[:, :, :], loraA.rearrange("e r n -> (e r) n").rearrange("(c p) n -> p c n", p=HR)
                         ).then_inc(loaded[2], 16)
            for i in range(DC):
                sp.dma_start(lraw[:, i], loraB[:, i * 128:(i + 1) * 128, :].rearrange("e p r -> p e r")
                             ).then_inc(loaded[3], 16)
            for n in range(NT):
                sp.wait_ge(y_free, n + 1)
                sp.dma_start(out[n // QT, (n % QT) * 128:(n % QT + 1) * 128, :], y[:, n % 2, :]).then_inc(stored[n % 2], 16)
            for s in stored:
                sp.wait_ge(s, 16 * NT // 2)

        @block.gpsimd
        def _(pool):
            nc.gpsimd.iota(iota[:, :], pattern=[[1, NE]], base=0, channel_multiplier=0,
                           allow_small_or_imprecise_dtypes=True).then_inc(iota_s, 1)

        @block.tensor
        def _(pe):
            for n in range(len(prep)):
                if n >= 4:
                    pe.wait_ge(w_lo, n - 3)
                o = ps[:, n % 4, :]
                if n < DC:
                    pe.wait_ge(loaded[0], 16)
                    for a in range(DC):
                        last = nc.tensor.transpose(o[:, a * 128:(a + 1) * 128], braw[:, a, n * 128:(n + 1) * 128],
                                                   K["id32"][:, :])
                elif n < 2 * DC:
                    i = n - DC
                    pe.wait_ge(loaded[1], 16)
                    pe.wait_ge(loaded[2], 16)
                    nc.tensor.transpose(o[:, 0:NE], graw[:, i * 128:(i + 1) * 128], K["id32"][0:NE, 0:NE])
                    for a in range(2):
                        last = nc.tensor.transpose(o[:, NE + a * HR:NE + (a + 1) * HR], araw[:, a, i * 128:(i + 1) * 128],
                                                   K["id32"][0:HR, 0:HR])
                else:
                    r = n - 2 * DC
                    pe.wait_ge(loaded[3], 16 * DC)
                    for a in range(DC):
                        last = nc.tensor.transpose(o[0:HR, a * 128:(a + 1) * 128],
                                                   lraw[:, a].rearrange("p e r -> p (e r)")[:, r * HR:(r + 1) * HR],
                                                   K["id32"][:, :])
                last.then_inc(w_ready, 1)
            pe.wait_ge(w_lo, len(prep))

            def gates(n):
                if n >= 2:
                    pe.wait_ge(ga_free, n - 1)
                for i in range(DC):
                    last = mm3(nc, ps[:, 4 + n % 2, 0:GA], [xT[:, s, i, n * 128:(n + 1) * 128] for s in range(2)],
                               [gaT[:, s, i, :] for s in range(2)], i == 0, i == DC - 1)
                last.then_inc(ga_ready, 1)

            gates(0)
            for n in range(NT):
                if n + 1 < NT:
                    gates(n + 1)
                if n >= 2:
                    pe.wait_ge(y_free, n - 1)
                yb = ps[:, 6 + n % 2, :]
                for i in range(DC):
                    mm3(nc, yb, [xT[:, s, i, n * 128:(n + 1) * 128] for s in range(2)],
                        [bT[:, s, i, :] for s in range(2)], i == 0, False)
                pe.wait_ge(hg_ready, n + 1)
                if n >= 2:
                    pe.wait_ge(ht_lo, n - 1)
                for r in range(2):
                    last = nc.tensor.transpose(ps[0:HR, n % 2, r * 128:(r + 1) * 128],
                                               hg[:, n % 2, r * HR:(r + 1) * HR], K["id32"][:, :])
                last.then_inc(ht_ready, 1)
                pe.wait_ge(ht_lo, n + 1)
                for r in range(2):
                    last = mm3(nc, yb, [hgT[:, n % 2, s, r, :] for s in range(2)], [lT[:, s, r, :] for s in range(2)],
                               False, r == 1)
                last.then_inc(y_ready, 1)

        @block.scalar
        def _(act):
            for n, (dst, w, r) in enumerate(prep):
                act.wait_ge(w_ready, n + 1)
                nc.scalar.activation(dst[0], ps[0:r, n % 4, 0:w], ACT.Copy, scale=SW).then_inc(w_hi, 1)
            for n in range(NT):
                act.wait_ge(top_s, n + 1)
                nc.scalar.activation(tf[:, n % 2, 3:4], tf[:, n % 2, 2:3], ACT.Exp).then_inc(ex_ready, 1)
                act.wait_ge(ht_ready, n + 1)
                nc.scalar.activation(hgT[:, n % 2, 0], ps[0:HR, n % 2, 0:256].rearrange("p (r n) -> p r n", r=2),
                                     ACT.Copy, scale=SX).then_inc(ht_hi, 1)

        @block.vector
        def _(dve):
            chain = Chain(dve, chain_s)
            for n, (dst, w, r) in enumerate(prep):
                dve.wait_ge(w_hi, n + 1)
                nc.vector.scalar_tensor_tensor(dst[1], ps[0:r, n % 4, 0:w], SW, dst[0], ALU.mult,
                                               ALU.subtract).then_inc(w_lo, 1)
            dve.wait_ge(iota_s, 1)
            for n in range(NT):
                p = n % 2
                dve.wait_ge(ga_ready, n + 1)
                nc.vector.tensor_scalar(ga[:, p, :], ps[:, 4 + p, 0:GA], 1.0 / (SX * SW), None,
                                        ALU.mult).then_inc(ga_free, 1)
                dve.wait_ge(ga_free, n + 1)
                chain(nc.vector.max(top[:, p, :], ga[:, p, 0:NE]))
                chain(nc.vector.max_index(topi[:, p, :], top[:, p, :], ga[:, p, 0:NE]))
                nc.vector.tensor_tensor(tf[:, p, 2:3], top[:, p, 1:2], top[:, p, 0:1], ALU.subtract).then_inc(top_s, 1)
                chain(nc.vector.tensor_copy(tf[:, p, 0:2], topi[:, p, 0:2]))
                dve.wait_ge(ex_ready, n + 1)
                chain(nc.vector.tensor_scalar(tf[:, p, 4:5], tf[:, p, 3:4], 1.0, None, ALU.add))
                chain(nc.vector.reciprocal(tf[:, p, 5:6], tf[:, p, 4:5]))
                chain(nc.vector.tensor_scalar(tf[:, p, 6:7], tf[:, p, 5:6], TOPK_SCALE, None, ALU.mult))
                chain(nc.vector.tensor_scalar(tf[:, p, 7:8], tf[:, p, 6:7], tf[:, p, 3:4], None, ALU.mult))
                nc.vector.tensor_scalar(gate[:, p, 0, :], iota[:, :], tf[:, p, 0:1], tf[:, p, 6:7], ALU.is_equal, ALU.mult)
                chain(nc.vector.tensor_scalar(gate[:, p, 1, :], iota[:, :], tf[:, p, 1:2], tf[:, p, 7:8], ALU.is_equal,
                                              ALU.mult))
                chain(nc.vector.tensor_tensor(gate[:, p, 0, :], gate[:, p, 0, :], gate[:, p, 1, :], ALU.add))
                nc.vector.tensor_tensor(hg[:, p, :].rearrange("p (e r) -> p e r", r=RANK),
                                        ga[:, p, NE:GA].rearrange("p (e r) -> p e r", r=RANK),
                                        gate[:, p, 0, :].rearrange("p (e a) -> p e a", a=1).to_broadcast([128, NE, RANK]),
                                        ALU.mult).then_inc(hg_ready, 1)
                dve.wait_ge(ht_hi, n + 1)
                nc.vector.scalar_tensor_tensor(hgT[:, p, 1], ps[0:HR, p, 0:256].rearrange("p (r n) -> p r n", r=2), SX,
                                               hgT[:, p, 0], ALU.mult, ALU.subtract).then_inc(ht_lo, 1)
                dve.wait_ge(y_ready, n + 1)
                if n >= 2:
                    dve.wait_ge(stored[p], 16 * (n // 2))
                nc.vector.scalar_tensor_tensor(y[:, p, :], ps[:, 6 + p, :], 1.0 / (SX * SW), K["x"][:, n, :], ALU.mult,
                                               ALU.add).then_inc(y_free, 1)


_INS = ['x', 'ctx_4096', 'L0_xattn_Wq', 'L0_xattn_bq', 'L0_xattn_Wk', 'L0_xattn_bk', 'L0_ffn_w_up', 'L0_ffn_w_down',
        'L1_xattn_Wq', 'L1_xattn_Wk', 'L1_xattn_Wv', 'L1_xattn_Wo', 'L1_ffn_base_W', 'L1_ffn_gate_W', 'L1_ffn_lora_A',
        'L1_ffn_lora_B']
_OUTS = [((4, 256, 512), 'float32')]


def kernel(**inputs):
    import numpy as _np
    import concourse.bacc as _bacc
    from concourse import mybir as _mybir
    from concourse.bass_utils import run_bass_kernel_spmd as _run

    nc = _bacc.Bacc("TRN2", target_bir_lowering=False, num_devices=1)
    arrays, args = {}, []
    for name in _INS:
        a = _np.ascontiguousarray(inputs[name])
        arrays[f"in_{name}_dram"] = a
        args.append(nc.dram_tensor(f"in_{name}_dram", a.shape, _mybir.dt.from_np(a.dtype), kind="ExternalInput").ap())
    for i, (shape, dtype) in enumerate(_OUTS):
        dt = _mybir.dt.from_np(_np.dtype(dtype))
        args.append(nc.dram_tensor(f"out_{i}_dram", shape, dt, kind="ExternalOutput").ap())
    build(nc, *args)
    r = _run(nc, [arrays], core_ids=[0])
    got = tuple(r.results[0][f"out_{i}_dram"] for i in range(len(_OUTS)))
    return got[0]
```

```python
import concourse.bass as bass
from concourse import mybir
from contextlib import ExitStack
import math

fp32 = mybir.dt.float32
fp16 = mybir.dt.float16
bf16 = mybir.dt.bfloat16
u32 = mybir.dt.uint32
ALU = mybir.AluOpType
ACT = mybir.ActivationFunctionType
AX = mybir.AxisListType

NB = 4
NTOK = 256
QT = NTOK // 128
NT = NB * QT
D = 512
DC = D // 128
NC = 1601
KT0 = -(-NC // 128)
REST = NC - (KT0 - 1) * 128
F = 2048
FC = F // 128
NFP = F // 128
KVH = 4
GRP = 8
HD = 128
NK = NTOK + NC
KT1 = -(-NK // 128)
NCP = NC + NC % 2
NKP = NTOK + NCP
NE, RANK, TOPK_SCALE = 28, 8, 2.0
NR = NE * RANK
EPS = 1e-5
MAGIC = 1.5 * 2.0 ** 23

SX = 64.0
SW = 1024.0
SQ = 512.0
SP_ = 4096.0


def banks(n):
    return [(o, min(512, n - o)) for o in range(0, n, 512)]


CUT0 = banks(NC)
CUT1 = banks(NK)


def mm3(nc, out, a, b, start, stop):
    nc.tensor.matmul(out, a[0], b[0], start=start, stop=False)
    nc.tensor.matmul(out, a[0], b[1], start=False, stop=False)
    return nc.tensor.matmul(out, a[1], b[0], start=False, stop=stop)


class Chain:

    def __init__(self, eng, sem, base=0):
        self.eng, self.sem, self.base, self.n = eng, sem, base, 0

    def __call__(self, ins):
        self.n += 1
        ins.then_inc(self.sem, 1)
        self.eng.wait_ge(self.sem, self.base + self.n)


LN_STEPS = 5


def layer_norm_stats(nc, dve, chain, K, stats, s_var, s_pow):
    st, mv, ve, yh = stats
    for n in range(NT):
        last = nc.vector.bn_stats(st[:, n, :], K["x"][:, n, :])
    chain(last)
    for n in range(NT):
        last = nc.vector.bn_aggr(mv[:, n, :], st[:, n, :])
    chain(last)
    nc.vector.tensor_scalar(ve[:, :], mv[:, :, 1], EPS, None, ALU.add).then_inc(s_var, 1)
    dve.wait_ge(s_var, 1)
    dve.wait_ge(s_pow, 1)
    chain(nc.vector.tensor_tensor(yh[:, 1, :], yh[:, 0, :], yh[:, 0, :], ALU.mult))
    chain(nc.vector.tensor_tensor(yh[:, 1, :], yh[:, 1, :], ve[:, :], ALU.mult))
    chain(nc.vector.tensor_scalar(yh[:, 1, :], yh[:, 1, :], -0.5, 1.5, ALU.mult, ALU.add))
    nc.vector.tensor_tensor(yh[:, 2, :], yh[:, 0, :], yh[:, 1, :], ALU.mult).then_inc(s_var, 1)
    dve.wait_ge(s_var, 2)


def stats_tiles(sb, tag):
    return (sb("st" + tag, [128, NT, 6], fp32), sb("mv" + tag, [128, NT, 2], fp32), sb("ve" + tag, [128, NT], fp32),
            sb("yh" + tag, [128, 3, NT], fp32))


def build(nc, x, ctx4, Wq0, bq0, Wk0, bk0, Wup, Wdn, Wq1, Wk1, Wv1, Wo1, baseW, gateW, loraA, loraB, out):
    k_scr = nc.dram_tensor("k_scr", (NB, KVH, 128, 2 * NCP), fp16, kind="Internal").ap()
    v_scr = nc.dram_tensor("v_scr", (NB, KVH, 128, KT0 * 2 * HD), fp16, kind="Internal").ap()
    wq_scr = nc.dram_tensor("wq_scr", (KVH, 8, 128, 2 * 512), fp16, kind="Internal").ap()
    wo_scr = nc.dram_tensor("wo_scr", (KVH, 8, 128, 2 * 512), fp16, kind="Internal").ap()

    with ExitStack() as keep:
        def sbk(name, shape, dt):
            return keep.enter_context(nc.sbuf_tensor(name, shape, dt))

        ps = keep.enter_context(nc.psum_tensor("ps", [128, 8, 512], fp32))
        K = {
            "id32": sbk("id32", [128, 128], fp32),
            "id16": sbk("id16", [128, 128], fp16),
            "x": sbk("x_all", [128, NT, D], fp32),
            "wk": sbk("wk_split", [128, 2, DC, 512], fp16),
            "wv": sbk("wv_split", [128, 2, DC, 512], fp16),
            "mhalf": sbk("mhalf", [128, NT], fp32),
            "part": sbk("ffn_part", [128, 2, NFP], fp32),
        }
        with ExitStack() as a:
            M = {
                "m": a.enter_context(nc.sbuf_tensor("m_split", [128, 2, DC, 512], fp16)),
                "qb": a.enter_context(nc.sbuf_tensor("q_bias", [128, DC], fp32)),
                "wb": a.enter_context(nc.sbuf_tensor("wb_split", [128, 2, DC], fp16)),
                "c0": a.enter_context(nc.sbuf_tensor("c0", [128, 1], fp32)),
                "ctx": a.enter_context(nc.sbuf_tensor("ctx_raw", [128, KT0, D], fp32)),
                "loaded": a.enter_context(nc.semaphore("ctx_loaded")),
                "stats": stats_tiles(lambda name, shape, dt: a.enter_context(nc.sbuf_tensor(name, shape, dt)), "0"),
            }
            prepare(nc, ps, K, M, x, ctx4, Wq0, bq0, Wk0, bk0, Wk1, Wv1)
            attention0(nc, ps, K, M, ctx4, Wq1, Wo1, Wup, Wdn, k_scr, v_scr, wq_scr, wo_scr)
        ffn0(nc, ps, K, Wup, Wdn)
        attention1(nc, ps, K, k_scr, v_scr, wq_scr, wo_scr)
        ffn1(nc, ps, K, baseW, gateW, loraA, loraB, out)


def load_context(sp, M, ctx4, b):
    sp.dma_start(M["ctx"][:, 0:KT0 - 1, :],
                 ctx4[bass.ds(b, 1), 0:(KT0 - 1) * 128, :].rearrange("a (t p) d -> p (a t) d", p=128)
                 ).then_inc(M["loaded"], 16)
    sp.dma_start(M["ctx"][0:REST, KT0 - 1, :],
                 ctx4[bass.ds(b, 1), (KT0 - 1) * 128:NC, :].rearrange("a p d -> p (a d)")
                 ).then_inc(M["loaded"], 16)


def prepare(nc, ps, K, M, x, ctx4, Wq0, bq0, Wk0, bk0, Wk1, Wv1):
    with ExitStack() as c:
        def sb(name, shape, dt):
            return c.enter_context(nc.sbuf_tensor(name, shape, dt))

        def sem(name):
            return c.enter_context(nc.semaphore(name))

        raw = sb("w_raw", [128, 4, DC, 512], fp32)
        spl = sb("w_spl", [128, 2, 2, DC, 512], fp16)
        bcol = sb("b_col", [128, 2, DC], fp32)
        wb32 = sb("wb32", [128, DC], fp32)
        s_w = [sem(f"p_w{i}") for i in range(4)]
        s_var, s_pow, s_ch = sem("p_var"), sem("p_pow"), sem("p_ch")
        s_b, s_xin, s_id, s_hi, s_lo, s_m, s_mh, s_ml, s_col, s_wb = (
            sem(n) for n in ("p_b", "p_x", "p_id", "p_hi", "p_lo", "p_m", "p_mh", "p_ml", "p_col", "p_wb"))
        block = c.enter_context(nc.Block())

        @block.sync
        def _(sp):
            for i, w in enumerate((Wq0, Wk0, Wk1, Wv1)):
                if i == 2:
                    sp.dma_start(K["x"][:, :, :], x.rearrange("b (q p) d -> p (b q) d", p=128)).then_inc(s_xin, 16)
                sp.dma_start(raw[:, i], w.rearrange("(c p) n -> p c n", p=128)).then_inc(s_w[i], 16)
            load_context(sp, M, ctx4, 0)
            sp.wait_ge(s_xin, 16)

        @block.gpsimd
        def _(pool):
            nc.gpsimd.memset(K["id32"][:, :], 0.0).then_inc(s_id, 1)
            nc.gpsimd.memset(K["id16"][:, :], 0.0).then_inc(s_id, 1)
            nc.gpsimd.memset(K["mhalf"][:, :], -0.5).then_inc(s_id, 1)
            pool.wait_ge(s_id, 3)
            for m in (K["id32"], K["id16"]):
                nc.gpsimd.affine_select(out=m[:, :], in_=m[:, :], compare_op=ALU.not_equal, fill=1.0, base=0,
                                        pattern=[[-1, 128]], channel_multiplier=1).then_inc(s_id, 1)
            pool.wait_ge(s_var, 1)
            nc.gpsimd.tensor_tensor(M["stats"][3][:, 0, :], M["stats"][2][:, :], K["mhalf"][:, :], ALU.pow).then_inc(s_pow, 1)

        @block.scalar
        def _(act):
            act.dma_start(bcol[:, 0, :], bq0.rearrange("(c p) -> p c", p=128), allow_slow_non_contiguous=True).then_inc(s_b, 16)
            act.dma_start(bcol[:, 1, :], bk0.rearrange("(c p) -> p c", p=128), allow_slow_non_contiguous=True).then_inc(s_b, 16)
            for i, dst in enumerate((spl[:, 0, 0], spl[:, 1, 0], K["wk"][:, 0], K["wv"][:, 0])):
                act.wait_ge(s_w[i], 16)
                nc.scalar.activation(dst, raw[:, i], ACT.Copy, scale=SW).then_inc(s_hi, 1)
            for i in range(DC):
                act.wait_ge(s_m, i + 1)
                nc.scalar.activation(M["m"][:, 0, i, :], ps[:, i, :], ACT.Copy, scale=1.0 / SW).then_inc(s_mh, 1)

        @block.vector
        def _(dve):
            for i, (hi, lo) in enumerate(((spl[:, 0, 0], spl[:, 0, 1]), (spl[:, 1, 0], spl[:, 1, 1]),
                                          (K["wk"][:, 0], K["wk"][:, 1]), (K["wv"][:, 0], K["wv"][:, 1]))):
                if i == 2:
                    dve.wait_ge(s_xin, 16)
                    layer_norm_stats(nc, dve, Chain(dve, s_ch), K, M["stats"], s_var, s_pow)
                dve.wait_ge(s_hi, i + 1)
                nc.vector.scalar_tensor_tensor(lo.rearrange("p c n -> p (c n)"), raw[:, i].rearrange("p c n -> p (c n)"),
                                               SW, hi.rearrange("p c n -> p (c n)"),
                                               ALU.mult, ALU.subtract).then_inc(s_lo, 1)
            for i in range(DC):
                dve.wait_ge(s_mh, i + 1)
                nc.vector.scalar_tensor_tensor(M["m"][:, 1, i, :], ps[:, i, :], 1.0 / SW, M["m"][:, 0, i, :],
                                               ALU.mult, ALU.subtract).then_inc(s_ml, 1)
            f0 = SQ / math.sqrt(D)
            dve.wait_ge(s_col, 1)
            nc.vector.tensor_scalar(M["qb"][:, :], ps[:, 4, 0:DC], f0, None, ALU.mult)
            nc.vector.tensor_scalar(M["c0"][:, :], ps[:, 6, 0:1], SX * f0, None, ALU.mult)
            nc.vector.tensor_scalar(wb32[:, :], ps[:, 5, 0:DC], SX, None, ALU.mult).then_inc(s_wb, 1)
            dve.wait_ge(s_wb, 1)
            nc.vector.tensor_copy(M["wb"][:, 0, :], wb32[:, :]).then_inc(s_wb, 1)
            dve.wait_ge(s_wb, 2)
            nc.vector.tensor_tensor(M["wb"][:, 1, :], wb32[:, :], M["wb"][:, 0, :], ALU.subtract)

        @block.tensor
        def _(pe):
            pe.wait_ge(s_lo, 2)
            for i in range(DC):
                for d in range(DC):
                    last = mm3(nc, ps[:, i, :], [spl[:, 0, h, d, i * 128:(i + 1) * 128] for h in range(2)],
                               [spl[:, 1, h, d, :] for h in range(2)], d == 0, d == DC - 1)
                last.then_inc(s_m, 1)
            pe.wait_ge(s_b, 32)
            for bank, w, v in ((4, 1, 0), (5, 0, 1)):
                for i in range(DC):
                    for d in range(DC):
                        nc.tensor.matmul(ps[:, bank, i:i + 1], raw[:, w, d, i * 128:(i + 1) * 128],
                                         bcol[:, v, d:d + 1], start=(d == 0), stop=(d == DC - 1))
            for d in range(DC):
                last = nc.tensor.matmul(ps[:, 6, 0:1], bcol[:, 0, d:d + 1].to_broadcast([128, 128]),
                                        bcol[:, 1, d:d + 1], start=(d == 0), stop=(d == DC - 1))
            last.then_inc(s_col, 1)



def attention0(nc, ps, K, M, ctx4, Wq1, Wo1, Wup, Wdn, k_scr, v_scr, wq_scr, wo_scr):
    with ExitStack() as c:
        def sb(name, shape, dt):
            return c.enter_context(nc.sbuf_tensor(name, shape, dt))

        def sem(name):
            return c.enter_context(nc.semaphore("a_" + name))

        raw = M["ctx"]
        nat = sb("ctx_nat", [128, 2, KT0, D], fp16)
        ctT = sb("ctx_T", [128, 2, DC, NCP], fp16)
        prob = sb("prob0", [128, NC], fp32)
        pT = sb("probT0", [128, 2, KT0, 128], fp16)
        kst = sb("k_stage", [128, 2, 2, NCP], fp16)
        vst = sb("v_stage", [128, KVH, KT0, 2, HD], fp16)
        xln = sb("xln0", [128, QT, D], fp32)
        xT = sb("xT0", [128, 2, DC, NTOK], fp16)
        q32 = sb("q32", [128, DC, NTOK], fp32)
        qT = sb("qT0", [128, 2, DC, NTOK], fp16)
        wraw = sb("wp_raw", [128, 2, 512], fp32)
        wspl = sb("wp_spl", [128, 2, 2, 512], fp16)
        fraw = sb("fp_raw", [128, 2, 512], fp32)
        _, mv, _, yh = M["stats"]
        cc = sb("cc0", [128, QT], fp32)
        mx = sb("mx0", [128, QT, 8], fp32)
        rs = sb("rs0", [128, QT, 4], fp32)

        TB, PB = 4, 6
        NG = -(-KT0 // 4)
        t_order = [("ln", q) for q in range(QT)] + [("p", q, g) for q in range(QT) for g in range(NG)]
        tj = {name: n for n, name in enumerate(t_order)}
        TJ = len(tj)
        p_order = [("k", 0, j) for j in range(4)] + [("q", i) for i in range(DC)] + [("c", 0)]
        p_order += [("k", h, j) for h in (1, 2, 3) for j in range(4)] + [("pv", 0)]
        p_order += [("v", kt) for kt in range(KT0)] + [("pv", 1)]
        pj = {name: n for n, name in enumerate(p_order)}
        PJ = len(pj)
        assert TJ % 2 == 0 and PJ % 2 == 0
        t_split = [x for x in t_order if x[0] in ("ln", "p")]
        p_split = [x for x in p_order if x[0] in ("k", "v")]
        assert NFP == NB * KVH
        NP = 16
        CH = 3 * QT + 3 * QT

        ctx_loaded, nat_hi, nat_lo = M["loaded"], sem("nat_hi"), sem("nat_lo")
        f_loaded, f_clamped, f_summed = sem("f_loaded"), sem("f_clamped"), sem("f_summed")
        c_ready, c_free = [sem(f"c_ready{s}") for s in range(2)], [sem(f"c_free{s}") for s in range(2)]
        t_ready, t_hi, t_free = sem("t_ready"), sem("t_hi"), [sem(f"t_free{i}") for i in range(2)]
        p_ready, p_hi, p_free = sem("p_ready"), sem("p_hi"), [sem(f"p_free{i}") for i in range(2)]
        xln_ready, chain_s = sem("xln_ready"), sem("chain")
        q32_ready, q_hi, q_lo = sem("q32_ready"), sem("q_hi"), sem("q_lo")
        s_ready, s_free, bias_ready = sem("s_ready"), sem("s_free"), sem("bias_ready")
        k_staged, v_staged = sem("k_staged"), sem("v_staged")
        k_stored, v_stored = [sem(f"k_stored{i}") for i in range(2)], sem("v_stored")
        w_hi, w_lo, padded = sem("w_hi"), sem("w_lo"), sem("padded")
        w_loaded, w_stored = [sem(f"w_loaded{i}") for i in range(2)], [sem(f"w_stored{i}") for i in range(2)]
        block = c.enter_context(nc.Block())

        def tbank(n):
            return ps[:, TB + n % 2, :]

        def pbank(n):
            return ps[:, PB + n % 2, :]

        def rows(kt):
            return 128 if kt < KT0 - 1 else REST

        def t_at(b, *job):
            return b * TJ + tj[job] + 1

        def p_at(b, *job):
            return b * PJ + pj[job] + 1

        def t_hi_at(b, *job):
            return b * len(t_split) + t_split.index(job) + 1

        def p_hi_at(b, *job):
            return b * len(p_split) + p_split.index(job) + 1

        def piece(b, i):
            if i < 8:
                return Wq1[i // 2 * 128:(i // 2 + 1) * 128, bass.ds(b * 1024 + i % 2 * 512, 512)], wq_scr[bass.ds(b, 1), i]
            return Wo1[bass.ds(b * 1024 + (i - 8) * 128, 128), :], wo_scr[bass.ds(b, 1), i - 8]

        @block.sync
        def _(sp):
            def ffn_pieces(n):
                sp.wait_ge(f_summed, 2 * n + 2)
                sp.dma_start(fraw[:, 0, :], Wup[bass.ds(n * 128, 128), :]).then_inc(f_loaded, 16)
                sp.dma_start(fraw[:, 1, :], Wdn.rearrange("h (q n) -> (h q) n", n=512)[bass.ds(n * 128, 128), :]
                             ).then_inc(f_loaded, 16)

            def stores(b):
                for h in range(KVH):
                    sp.wait_ge(k_staged, b * KVH + h + 1)
                    sp.dma_start(k_scr[bass.ds(b, 1), h].rearrange("a p n -> p (a n)"),
                                 kst[:, h % 2].rearrange("p s n -> p (s n)")).then_inc(k_stored[h % 2], 16)
                    ffn_pieces(b * KVH + h)
                sp.wait_ge(v_staged, b + 1)
                for h in range(KVH):
                    sp.dma_start(v_scr[bass.ds(b, 1), h].rearrange("a p n -> p (a n)"),
                                 vst[:, h].rearrange("p t s n -> p (t s n)")).then_inc(v_stored, 16)

            sp.sem_inc(f_summed, 2)
            with sp.Fori(0, NB - 1) as b:
                sp.wait_ge(nat_lo, (b + 1) * KT0)
                load_context(sp, M, ctx4, b + 1)
                stores(b)
            stores(NB - 1)
            for s in k_stored:
                sp.wait_ge(s, 16 * (2 * NB + 1))
            sp.wait_ge(v_stored, 16 * KVH * (NB + 1))
            for s in w_stored:
                sp.wait_ge(s, 16 * (NP // 2 * NB + 1))

        @block.gpsimd
        def _(pool):
            nc.gpsimd.memset(kst[:, :, :, NC - 1:NCP], 0.0).then_inc(padded, 1)
            nc.gpsimd.memset(vst[:, :, KT0 - 1], 0.0).then_inc(padded, 1)

        @block.scalar
        def _(act):
            for s in k_stored:
                act.sem_inc(s, 16)
            act.sem_inc(v_stored, 16 * KVH)
            for s in w_stored:
                act.sem_inc(s, 16)
            act.wait_ge(padded, 2)

            def natural_hi(kt):
                nc.scalar.activation(nat[0:rows(kt), 0, kt, :], raw[0:rows(kt), kt, :], ACT.Copy,
                                     scale=SX).then_inc(nat_hi, 1)

            def load_piece(b, i):
                act.dma_start(wraw[:, i % 2, :], piece(b, i)[0]).then_inc(w_loaded[i % 2], 16)

            def store_piece(b, i):
                act.wait_ge(w_lo, b * NP + i + 1)
                act.dma_start(piece(b, i)[1].rearrange("a p n -> p (a n)"),
                              wspl[:, i % 2].rearrange("p s n -> p (s n)")).then_inc(w_stored[i % 2], 16)

            def weights_hi(b, i):
                if i:
                    store_piece(b, i - 1)
                if i + 1 < NP:
                    load_piece(b, i + 1)
                act.wait_ge(w_loaded[i % 2], 16 * (b * (NP // 2) + i // 2 + 1))
                act.wait_ge(w_stored[i % 2], 16 * (b * (NP // 2) + i // 2 + 1))
                nc.scalar.activation(wspl[:, i % 2, 0, :], wraw[:, i % 2, :], ACT.Copy, scale=SW).then_inc(w_hi, 1)

            def exps(b, q):
                act.wait_ge(bias_ready, b * QT + q + 1)
                for j, (o, w) in enumerate(CUT0):
                    nc.scalar.activation(prob[:, o:o + w], ps[:, j, 0:w], ACT.Exp, bias=mx[:, q, 6:7],
                                         scale=1.0 / (SQ * SX), accum_out=rs[:, q, j:j + 1]).then_inc(s_free, 1)

            def keys_hi(b, h):
                act.wait_ge(k_stored[h % 2], 16 * (2 * b + h // 2 + 1))
                for j, (o, w) in enumerate(CUT0):
                    act.wait_ge(p_ready, p_at(b, "k", h, j))
                    nc.scalar.activation(kst[:, h % 2, 0, o:o + w], pbank(pj["k", h, j])[:, 0:w], ACT.Copy,
                                         scale=1.0 / SW).then_inc(p_hi, 1)

            def probs_hi(b, q, groups=range(NG)):
                for g in groups:
                    t = min(4, KT0 - 4 * g)
                    r = rows(4 * g)
                    act.wait_ge(t_ready, t_at(b, "p", q, g))
                    nc.scalar.activation(pT[0:r, 0, 4 * g:4 * g + t, :],
                                         tbank(tj["p", q, g])[0:r, 0:t * 128].rearrange("p (t n) -> p t n", t=t),
                                         ACT.Copy, scale=SP_).then_inc(t_hi, 1)

            with act.Fori(0, NB) as b:
                load_piece(b, 0)
                act.wait_ge(ctx_loaded, (b + 1) * 32)
                natural_hi(0)
                for kt in range(KT0):
                    if kt + 1 < KT0:
                        natural_hi(kt + 1)
                    act.wait_ge(c_ready[1], b * KT0 + kt + 1)
                    nc.scalar.activation(ctT[:, 1, :, kt * 128:kt * 128 + rows(kt)],
                                         ps[:, 2 + kt % 2, 0:256].bitcast(fp16).rearrange("p (c n) -> p c n", c=DC)
                                         [:, :, 0:rows(kt)], ACT.Copy).then_inc(c_free[1], 1)
                for q in range(QT):
                    act.wait_ge(t_ready, t_at(b, "ln", q))
                    nc.scalar.activation(xT[:, 0, :, q * 128:(q + 1) * 128],
                                         tbank(tj["ln", q]).rearrange("p (c n) -> p c n", c=DC), ACT.Copy,
                                         scale=SX).then_inc(t_hi, 1)
                keys_hi(b, 0)
                for i in range(DC):
                    n = pj["q", i]
                    act.wait_ge(p_ready, p_at(b, "q", i))
                    nc.scalar.activation(q32[:, i, :], pbank(n)[:, 0:NTOK], ACT.Identity, bias=M["qb"][:, i:i + 1],
                                         scale=SQ / math.sqrt(D) / (SX * SW)).then_inc(p_free[n % 2], 1)
                for i in range(DC):
                    n = pj["q", i]
                    act.wait_ge(p_free[n % 2], b * (PJ // 2) + n // 2 + 2)
                    nc.scalar.activation(qT[:, 0, i, :], q32[:, i, :], ACT.Copy).then_inc(q_hi, 1)
                keys_hi(b, 1)
                weights_hi(b, 0)
                exps(b, 0)
                keys_hi(b, 2)
                weights_hi(b, 1)
                probs_hi(b, 0)
                exps(b, 1)
                keys_hi(b, 3)
                weights_hi(b, 2)
                act.wait_ge(v_stored, 16 * KVH * (b + 1))
                for kt in range(KT0):
                    act.wait_ge(p_ready, p_at(b, "v", kt))
                    nc.scalar.activation(vst[0:rows(kt), :, kt, 0, :],
                                         pbank(pj["v", kt])[0:rows(kt), :].rearrange("p (h n) -> p h n", h=KVH),
                                         ACT.Copy, scale=1.0 / SW).then_inc(p_hi, 1)
                    if kt < NG:
                        probs_hi(b, 1, (kt,))
                    weights_hi(b, kt + NP - KT0)
                store_piece(b, NP - 1)
                act.wait_ge(p_ready, p_at(b, "pv", 1))

        @block.vector
        def _(dve):
            def lo(dst, src, scale, hi, done):
                nc.vector.scalar_tensor_tensor(dst, src, scale, hi, ALU.mult, ALU.subtract).then_inc(done, 1)

            def bias(b, q, chain):
                dve.wait_ge(s_ready, b * QT + q + 1)
                for j, (o, w) in enumerate(CUT0):
                    last = nc.vector.reduce_max(mx[:, q, j:j + 1], ps[:, j, 0:w], AX.X)
                chain(last)
                chain(nc.vector.reduce_max(mx[:, q, 4:5], mx[:, q, 0:4], AX.X))
                chain(nc.vector.tensor_scalar(mx[:, q, 5:6], mx[:, q, 4:5], cc[:, q:q + 1], None, ALU.add))
                nc.vector.tensor_scalar(mx[:, q, 6:7], mx[:, q, 5:6], cc[:, q:q + 1], -1.0 / (SQ * SX),
                                        ALU.subtract, ALU.mult).then_inc(bias_ready, 1)

            def keys_lo(b, h):
                for j, (o, w) in enumerate(CUT0):
                    n = pj["k", h, j]
                    dve.wait_ge(p_hi, p_hi_at(b, "k", h, j))
                    lo(kst[:, h % 2, 1, o:o + w], pbank(n)[:, 0:w], 1.0 / SW, kst[:, h % 2, 0, o:o + w], p_free[n % 2])
                dve.wait_ge(p_free[n % 2], b * (PJ // 2) + n // 2 + 2)
                dve.sem_inc(k_staged, 1)

            def probs_lo(b, q, groups=range(NG)):
                for g in groups:
                    t = min(4, KT0 - 4 * g)
                    n, r = tj["p", q, g], rows(4 * g)
                    dve.wait_ge(t_hi, t_hi_at(b, "p", q, g))
                    lo(pT[0:r, 1, 4 * g:4 * g + t, :].rearrange("p t n -> p (t n)"), tbank(n)[0:r, 0:t * 128], SP_,
                       pT[0:r, 0, 4 * g:4 * g + t, :].rearrange("p t n -> p (t n)"), t_free[n % 2])

            def weights_lo(b, i):
                dve.wait_ge(w_hi, b * NP + i + 1)
                lo(wspl[:, i % 2, 1, :], wraw[:, i % 2, :], SW, wspl[:, i % 2, 0, :], w_lo)

            def magnitudes(b, h):
                n = b * KVH + h
                dve.wait_ge(f_loaded, 32 * n + 32)
                for i in range(2):
                    nc.vector.tensor_scalar(fraw[:, i, :], fraw[:, i, :], 1.0, -1.0, ALU.min, ALU.max).then_inc(f_clamped, 1)
                for i in range(2):
                    dve.wait_ge(f_clamped, 2 * n + i + 1)
                    nc.vector.tensor_reduce(K["part"][:, i, bass.ds(n, 1)], fraw[:, i, :], AX.X, ALU.add,
                                            apply_absolute_value=True).then_inc(f_summed, 1)

            def row_sum(b, q, chain):
                dve.wait_ge(s_free, 4 * (b * QT + q + 1) + 4)
                chain(nc.vector.reduce_sum(mx[:, q, 7:8], rs[:, q, :], AX.X))
                chain(nc.vector.reciprocal(mx[:, q, 7:8], mx[:, q, 7:8]))
                chain(nc.vector.tensor_scalar(mx[:, q, 7:8], mx[:, q, 7:8], 1.0 / (SP_ * SX), None, ALU.mult))

            def attended(b, q):
                n = pj["pv", q]
                xs = K["x"][:, bass.ds(b * QT + q, 1), :].rearrange("p a d -> p (a d)")
                dve.wait_ge(p_ready, p_at(b, "pv", q))
                nc.vector.scalar_tensor_tensor(xs, pbank(n), mx[:, q, 7:8], xs, ALU.mult,
                                               ALU.add).then_inc(p_free[n % 2], 1)

            with dve.Fori(0, NB) as b:
                chain = Chain(dve, chain_s, b * CH)
                for q in range(QT):
                    nc.vector.tensor_scalar(xln[:, q, :],
                                            K["x"][:, bass.ds(b * QT + q, 1), :].rearrange("p a d -> p (a d)"),
                                            mv[:, bass.ds(b * QT + q, 1), 0:1].rearrange("p a c -> p (a c)"),
                                            yh[:, 2, bass.ds(b * QT + q, 1)], ALU.subtract,
                                            ALU.mult).then_inc(xln_ready, 1)
                for kt in range(KT0):
                    r = rows(kt)
                    dve.wait_ge(nat_hi, b * KT0 + kt + 1)
                    lo(nat[0:r, 1, kt, :], raw[0:r, kt, :], SX, nat[0:r, 0, kt, :], nat_lo)
                    dve.wait_ge(c_ready[0], b * KT0 + kt + 1)
                    nc.vector.tensor_copy(ctT[:, 0, :, kt * 128:kt * 128 + r],
                                          ps[:, kt % 2, 0:256].bitcast(fp16).rearrange("p (c n) -> p c n", c=DC)
                                          [:, :, 0:r]).then_inc(c_free[0], 1)
                for q in range(QT):
                    n = tj["ln", q]
                    dve.wait_ge(t_hi, t_hi_at(b, "ln", q))
                    lo(xT[:, 1, :, q * 128:(q + 1) * 128], tbank(n).rearrange("p (c n) -> p c n", c=DC), SX,
                       xT[:, 0, :, q * 128:(q + 1) * 128], t_free[n % 2])
                keys_lo(b, 0)
                for i in range(DC):
                    dve.wait_ge(q_hi, b * DC + i + 1)
                    nc.vector.tensor_tensor(qT[:, 1, i, :], q32[:, i, :], qT[:, 0, i, :],
                                            ALU.subtract).then_inc(q_lo, 1)
                n = pj["c", 0]
                dve.wait_ge(p_ready, p_at(b, "c", 0))
                nc.vector.tensor_scalar(cc[:, :], pbank(n)[:, 0:QT], SQ / math.sqrt(D) / SX, M["c0"][:, 0:1],
                                        ALU.mult, ALU.add).then_inc(p_free[n % 2], 1)
                keys_lo(b, 1)
                weights_lo(b, 0)
                bias(b, 0, chain)
                keys_lo(b, 2)
                weights_lo(b, 1)
                magnitudes(b, 0)
                probs_lo(b, 0)
                row_sum(b, 0, chain)
                bias(b, 1, chain)
                keys_lo(b, 3)
                weights_lo(b, 2)
                magnitudes(b, 1)
                attended(b, 0)
                for kt in range(KT0):
                    n, r = pj["v", kt], rows(kt)
                    dve.wait_ge(p_hi, p_hi_at(b, "v", kt))
                    lo(vst[0:r, :, kt, 1, :], pbank(n)[0:r, :].rearrange("p (h n) -> p h n", h=KVH), 1.0 / SW,
                       vst[0:r, :, kt, 0, :], p_free[n % 2])
                    if kt < NG:
                        probs_lo(b, 1, (kt,))
                    weights_lo(b, kt + NP - KT0)
                    if kt in (5, 9):
                        magnitudes(b, 2 + kt // 9)
                row_sum(b, 1, chain)
                n = pj["v", KT0 - 1]
                dve.wait_ge(p_free[n % 2], b * (PJ // 2) + n // 2 + 2)
                dve.sem_inc(v_staged, 1)
                attended(b, 1)
                assert chain.n == CH, chain.n

        @block.tensor
        def _(pe):
            for s in t_free + p_free:
                pe.sem_inc(s, 1)
            for s in c_free:
                pe.sem_inc(s, 2)
            pe.sem_inc(s_free, 4)

            def take(b, ring, free, per, n):
                pe.wait_ge(free[n % 2], b * (per // 2) + n // 2 + 1)
                return ring(n)

            def t_take(b, *job):
                return take(b, tbank, t_free, TJ, tj[job])

            def p_take(b, *job):
                return take(b, pbank, p_free, PJ, pj[job])

            def scores(b, q, some=range(4)):
                for j in some:
                    o, w = CUT0[j]
                    pe.wait_ge(s_free, 4 * (b * QT + q) + j + 1)
                    for i in range(DC):
                        last = mm3(nc, ps[:, j, 0:w], [qT[:, s, i, q * 128:(q + 1) * 128] for s in range(2)],
                                   [ctT[:, s, i, o:o + w] for s in range(2)], i == 0, i == DC - 1)
                if j == 3:
                    last.then_inc(s_ready, 1)

            def keys(b, h):
                for j, (o, w) in enumerate(CUT0):
                    out = p_take(b, "k", h, j)
                    for i in range(DC):
                        last = mm3(nc, out[:, 0:w], [K["wk"][:, s, i, h * 128:(h + 1) * 128] for s in range(2)],
                                   [ctT[:, s, i, o:o + w] for s in range(2)], i == 0, i == DC - 1)
                    last.then_inc(p_ready, 1)

            def turn(b, q, groups):
                for g in groups:
                    if g == 0:
                        pe.wait_ge(s_free, 4 * (b * QT + q + 1) + 4)
                    out = t_take(b, "p", q, g)
                    for kt in range(4 * g, min(4 * g + 4, KT0)):
                        o = (kt - 4 * g) * 128
                        last = nc.tensor.transpose(out[0:rows(kt), o:o + 128], prob[:, kt * 128:kt * 128 + rows(kt)],
                                                   K["id32"][:, :])
                    last.then_inc(t_ready, 1)

            def attend(b, q):
                out = p_take(b, "pv", q)
                n = tj["p", q, NG - 1]
                pe.wait_ge(t_free[n % 2], b * (TJ // 2) + n // 2 + 2)
                n = tj["p", q, NG - 2]
                pe.wait_ge(t_free[n % 2], b * (TJ // 2) + n // 2 + 2)
                for kt in range(KT0):
                    r = rows(kt)
                    last = mm3(nc, out, [pT[0:r, s, kt, :] for s in range(2)], [nat[0:r, s, kt, :] for s in range(2)],
                               kt == 0, kt == KT0 - 1)
                last.then_inc(p_ready, 1)

            with pe.Fori(0, NB) as b:
                pe.wait_ge(s_free, 4 * b * QT + 4)
                for kt in range(KT0):
                    r = rows(kt)
                    for s, sm in enumerate((nat_hi, nat_lo)):
                        pe.wait_ge(sm, b * KT0 + kt + 1)
                        pe.wait_ge(c_free[s], b * KT0 + kt + 1)
                        out = ps[:, 2 * s + kt % 2, 0:256].bitcast(fp16)
                        for i in range(DC):
                            last = nc.tensor.transpose(out[:, i * 128:i * 128 + r], nat[0:r, s, kt, i * 128:(i + 1) * 128],
                                                       K["id16"][0:r, 0:r])
                        last.then_inc(c_ready[s], 1)
                for q in range(QT):
                    pe.wait_ge(xln_ready, b * QT + q + 1)
                    out = t_take(b, "ln", q)
                    for i in range(DC):
                        last = nc.tensor.transpose(out[:, i * 128:(i + 1) * 128], xln[:, q, i * 128:(i + 1) * 128],
                                                   K["id32"][:, :])
                    last.then_inc(t_ready, 1)
                for s in range(2):
                    pe.wait_ge(c_free[s], b * KT0 + KT0 + 2)
                keys(b, 0)
                for q in range(QT):
                    n = tj["ln", q]
                    pe.wait_ge(t_free[n % 2], b * (TJ // 2) + n // 2 + 2)
                for i in range(DC):
                    out = p_take(b, "q", i)
                    for j in range(DC):
                        last = mm3(nc, out[:, 0:NTOK], [M["m"][:, s, j, i * 128:(i + 1) * 128] for s in range(2)],
                                   [xT[:, s, j, :] for s in range(2)], j == 0, j == DC - 1)
                    last.then_inc(p_ready, 1)
                out = p_take(b, "c", 0)
                for q in range(QT):
                    for j in range(DC):
                        last = mm3(nc, out[:, q:q + 1], [xT[:, s, j, q * 128:(q + 1) * 128] for s in range(2)],
                                   [M["wb"][:, s, j:j + 1] for s in range(2)], j == 0, j == DC - 1)
                last.then_inc(p_ready, 1)
                keys(b, 1)
                pe.wait_ge(q_lo, (b + 1) * DC)
                scores(b, 0)
                keys(b, 2)
                for j in range(4):
                    scores(b, 1, (j,))
                    turn(b, 0, (j,))
                keys(b, 3)
                attend(b, 0)
                for kt in range(KT0):
                    r = rows(kt)
                    out = p_take(b, "v", kt)
                    for i in range(DC):
                        last = mm3(nc, out[0:r, :], [ctT[:, s, i, kt * 128:kt * 128 + r] for s in range(2)],
                                   [K["wv"][:, s, i, :] for s in range(2)], i == 0, i == DC - 1)
                    last.then_inc(p_ready, 1)
                    if kt < NG:
                        turn(b, 1, (kt,))
                attend(b, 1)


def ffn0(nc, ps, K, Wup, Wdn):
    with ExitStack() as c:
        def sb(name, shape, dt):
            return c.enter_context(nc.sbuf_tensor(name, shape, dt))

        def sem(name):
            return c.enter_context(nc.semaphore("f_" + name))

        upT = sb("up_T", [128, DC, F], bf16)
        dnT = sb("down_T", [128, FC, D], bf16)
        id_b = sb("id_b", [128, 128], bf16)
        ones = sb("ones", [128, 128], fp32)
        tot = sb("tot", [128, 2, 6], fp32)
        stats = stats_tiles(sb, "f")
        _, mv, ve, yh = stats
        var_ready, pow_ready, stats_s = sem("var_ready"), sem("pow_ready"), sem("stats")
        with ExitStack() as w:
            NWT = F * D // 128 // 2048
            raw = w.enter_context(nc.sbuf_tensor("ffn_raw", [128, 2, NWT, 2048], fp32))
            gt = w.enter_context(nc.sbuf_tensor("ffn_gt", [128, 2, 2048], bf16))
            tern = w.enter_context(nc.sbuf_tensor("ffn_tern", [128, 2, NWT, 2048], bf16))

            def semw(name):
                return w.enter_context(nc.semaphore("fw_" + name))

            loaded = [[semw(f"loaded{i}_{t}") for t in range(NWT)] for i in range(2)]
            ones_s, sum_s, tot_s, thr_s, tern_s, tr_s, ev_s, ch_s, idb_s = (
                semw(n) for n in ("ones", "sum", "tot", "thr", "tern", "tr", "ev", "ch", "idb"))
            block = w.enter_context(nc.Block())

            @block.sync
            def _(sp):
                for t in range(NWT):
                    sp.dma_start(raw[:, 0, t, :].rearrange("p (a n) -> p a n", a=4),
                                 Wup[t * 512:(t + 1) * 512, :].rearrange("(a p) n -> p a n", p=128)
                                 ).then_inc(loaded[0][t], 16)
                for t in range(NWT):
                    sp.dma_start(raw[:, 1, t, :], Wdn[t * 128:(t + 1) * 128, :]).then_inc(loaded[1][t], 16)

            @block.gpsimd
            def _(pool):
                nc.gpsimd.memset(ones[:, :], 1.0).then_inc(ones_s, 1)
                nc.gpsimd.tensor_copy(id_b[:, :], K["id16"][:, :]).then_inc(idb_s, 1)
                pool.wait_ge(var_ready, 1)
                nc.gpsimd.tensor_tensor(yh[:, 0, :], ve[:, :], K["mhalf"][:, :], ALU.pow).then_inc(pow_ready, 1)

            @block.vector
            def _(dve):
                chain = Chain(dve, ch_s)
                for i in range(2):
                    nc.vector.reduce_sum(tot[:, i, 0:1], K["part"][:, i, :], AX.X).then_inc(sum_s, 1)
                layer_norm_stats(nc, dve, Chain(dve, stats_s), K, stats, var_ready, pow_ready)
                for i in range(2):
                    dve.wait_ge(tot_s, i + 1)
                    chain(nc.vector.tensor_scalar(tot[:, i, 1:2], ps[:, 6 + i, 0:1], 1.0 / (F * D), EPS, ALU.mult, ALU.add))
                    nc.vector.tensor_scalar(tot[:, i, 2:3], tot[:, i, 1:2], 0.5, None, ALU.mult)
                    chain(nc.vector.tensor_scalar(tot[:, i, 3:4], tot[:, i, 1:2], -0.5, None, ALU.mult))
                    for t in range(NWT):
                        dve.wait_ge(loaded[i][t], 16)
                        chain(nc.vector.tensor_scalar(gt[:, t % 2, :], raw[:, i, t, :], tot[:, i, 2:3], None, ALU.is_gt))
                        nc.vector.scalar_tensor_tensor(tern[:, i, t, :], raw[:, i, t, :], tot[:, i, 3:4], gt[:, t % 2, :],
                                                       ALU.is_lt, ALU.subtract).then_inc(tern_s, 1)

            @block.tensor
            def _(pe):
                pe.wait_ge(ones_s, 1)
                for i in range(2):
                    pe.wait_ge(sum_s, i + 1)
                    nc.tensor.matmul(ps[:, 6 + i, 0:1], ones[:, :], tot[:, i, 0:1], start=True, stop=True).then_inc(tot_s, 1)
                pe.wait_ge(idb_s, 1)
                n = 0
                for t in range(NWT):
                    pe.wait_ge(tern_s, t + 1)
                    for i in range(DC):
                        if n >= 4:
                            pe.wait_ge(ev_s, n - 3)
                        for a in range(4):
                            last = nc.tensor.transpose(ps[:, n % 4, 0:256].bitcast(bf16)[:, a * 128:(a + 1) * 128],
                                                       tern[:, 0, t, a * 512 + i * 128:a * 512 + (i + 1) * 128], id_b[:, :])
                        last.then_inc(tr_s, 1)
                        n += 1
                for t in range(FC):
                    if t == 0:
                        pe.wait_ge(tern_s, 2 * NWT)
                    pe.wait_ge(ev_s, n - 3)
                    for a in range(DC):
                        last = nc.tensor.transpose(ps[:, n % 4, 0:256].bitcast(bf16)[:, a * 128:(a + 1) * 128],
                                                   tern[:, 1, a, t * 128:(t + 1) * 128], id_b[:, :])
                    last.then_inc(tr_s, 1)
                    n += 1

            @block.scalar
            def _(act):
                n = 0
                for t in range(NWT):
                    for i in range(DC):
                        act.wait_ge(tr_s, n + 1)
                        nc.scalar.activation(upT[:, i, t * 512:(t + 1) * 512], ps[:, n % 4, 0:256].bitcast(bf16),
                                             ACT.Copy, scale=-1.0).then_inc(ev_s, 1)
                        n += 1
                for t in range(FC):
                    act.wait_ge(tr_s, n + 1)
                    nc.scalar.activation(dnT[:, t, :], ps[:, n % 4, 0:256].bitcast(bf16), ACT.Copy,
                                         scale=-1.0).then_inc(ev_s, 1)
                    n += 1

        hr = sb("h_relu", [128, QT, F], fp32)
        hq = sb("h32", [128, F], fp32)
        hb = sb("h_int", [128, QT, F], bf16)
        hT = sb("h_intT", [128, FC, 128], bf16)
        xln = sb("xlnf", [128, QT, D], fp32)
        xq = sb("xq", [128, QT, D], bf16)
        xqT = sb("xqT", [128, QT, DC, 128], bf16)
        sx = sb("sxf", [128, QT, 3], fp32)
        unit = sb("unit", [128, QT], fp32)
        sh = sb("shf", [128, QT, 4], fp32)
        (chain_s, xq_ready, xt_ready, xt_done, up_ready, relu_done,
         hb_ready, ht_ready, ht_done, dn_ready, dn_done, unit_ready) = (sem(n) for n in (
             "chain", "xq_ready", "xt_ready", "xt_done", "up_ready", "relu_done",
             "hb_ready", "ht_ready", "ht_done", "dn_ready", "dn_done", "unit_ready"))
        CHX, CHH = 1 + QT * 5, 5
        CHF = CHX + QT * CHH
        block = c.enter_context(nc.Block())

        @block.tensor
        def _(pe):
            pe.sem_inc(xt_done, 1)
            pe.sem_inc(dn_done, 1)
            pe.sem_inc(ht_done, 2)
            pe.sem_inc(relu_done, 4)

            def turn_tokens(n, q):
                pe.wait_ge(xq_ready, n + 1)
                pe.wait_ge(xt_done, n + 1)
                for i in range(DC):
                    last = nc.tensor.transpose(ps[:, 6, 0:256].bitcast(bf16)[:, i * 128:(i + 1) * 128],
                                               xq[:, q, i * 128:(i + 1) * 128], id_b[:, :])
                last.then_inc(xt_ready, 1)

            def up(n, q):
                pe.wait_ge(xt_done, n + 2)
                for j in range(4):
                    pe.wait_ge(relu_done, 4 * n + j + 1)
                    for i in range(DC):
                        last = nc.tensor.matmul(ps[:, j, :], xqT[:, q, i, :], upT[:, i, j * 512:(j + 1) * 512],
                                                start=(i == 0), stop=(i == DC - 1))
                    last.then_inc(up_ready, 1)

            def down(n, q):
                pe.wait_ge(hb_ready, n + 1)
                for g in range(4):
                    pe.wait_ge(ht_done, 4 * n + g + 1)
                    for a in range(4):
                        t = 4 * g + a
                        last = nc.tensor.transpose(ps[:, 4 + g % 2, 0:256].bitcast(bf16)[:, a * 128:(a + 1) * 128],
                                                   hb[:, q, t * 128:(t + 1) * 128], id_b[:, :])
                    last.then_inc(ht_ready, 1)
                pe.wait_ge(dn_done, n + 1)
                pe.wait_ge(ht_done, 4 * n + 4 + 2)
                for t in range(FC):
                    last = nc.tensor.matmul(ps[:, 7, :], hT[:, t, :], dnT[:, t, :], start=(t == 0), stop=(t == FC - 1))
                last.then_inc(dn_ready, 1)

            def body(b, more):
                up(b * QT + 1, 1)
                down(b * QT, 0)
                if more:
                    turn_tokens(b * QT + 2, 0)
                    turn_tokens(b * QT + 3, 1)
                    up(b * QT + 2, 0)
                down(b * QT + 1, 1)

            turn_tokens(0, 0)
            turn_tokens(1, 1)
            up(0, 0)
            with pe.Fori(0, NB - 1) as b:
                body(b, True)
            body(NB - 1, False)

        @block.scalar
        def _(act):
            def tokens(n, q):
                act.wait_ge(xt_ready, n + 1)
                nc.scalar.activation(xqT[:, q].rearrange("p c n -> p (c n)"), ps[:, 6, 0:256].bitcast(bf16),
                                     ACT.Copy).then_inc(xt_done, 1)

            def relu(n, q):
                act.wait_ge(unit_ready, n + 1)
                for j in range(4):
                    act.wait_ge(up_ready, 4 * n + j + 1)
                    nc.scalar.activation(hr[:, q, j * 512:(j + 1) * 512], ps[:, j, :], ACT.Relu,
                                         scale=unit[:, q:q + 1]).then_inc(relu_done, 1)

            def hidden(n):
                for g in range(4):
                    act.wait_ge(ht_ready, 4 * n + g + 1)
                    nc.scalar.activation(hT[:, 4 * g:4 * g + 4, :].rearrange("p t n -> p (t n)"),
                                         ps[:, 4 + g % 2, 0:256].bitcast(bf16), ACT.Copy).then_inc(ht_done, 1)

            def body(b, more):
                relu(b * QT + 1, 1)
                hidden(b * QT)
                if more:
                    tokens(b * QT + 2, 0)
                    tokens(b * QT + 3, 1)
                    relu(b * QT + 2, 0)
                hidden(b * QT + 1)

            tokens(0, 0)
            tokens(1, 1)
            relu(0, 0)
            with act.Fori(0, NB - 1) as b:
                body(b, True)
            body(NB - 1, False)

        @block.vector
        def _(dve):
            def xs(n):
                return K["x"][:, n, :] if isinstance(n, int) else K["x"][:, bass.ds(n, 1), :].rearrange("p a d -> p (a d)")

            def unit_of(q):
                nc.vector.tensor_scalar(unit[:, q:q + 1], sx[:, q, 0:1], tot[:, 0, 1:2], 1.0 / 127.0, ALU.mult,
                                        ALU.mult).then_inc(unit_ready, 1)

            def quantised_tokens(b, chain):
                for q in range(QT):
                    n = b * QT + q
                    last = nc.vector.tensor_scalar(xln[:, q, :], xs(n),
                                                   mv[:, bass.ds(n, 1), 0:1].rearrange("p a c -> p (a c)"),
                                                   yh[:, 2, bass.ds(n, 1)], ALU.subtract, ALU.mult)
                chain(last)
                for q in range(QT):
                    chain(nc.vector.tensor_reduce(sx[:, q, 0:1], xln[:, q, :], AX.X, ALU.max, apply_absolute_value=True))
                    chain(nc.vector.tensor_scalar(sx[:, q, 0:1], sx[:, q, 0:1], EPS, None, ALU.max))
                    chain(nc.vector.reciprocal(sx[:, q, 1:2], sx[:, q, 0:1]))
                    chain(nc.vector.tensor_scalar(sx[:, q, 1:2], sx[:, q, 1:2], 127.0, None, ALU.mult))
                    if q == 0:
                        unit_of(0)
                    chain(nc.vector.tensor_scalar(xln[:, q, :], xln[:, q, :], sx[:, q, 1:2], MAGIC, ALU.mult, ALU.add))
                    nc.vector.tensor_scalar(xq[:, q, :], xln[:, q, :], MAGIC, 127.0, ALU.subtract,
                                            ALU.min).then_inc(xq_ready, 1)

            def quantised_hidden(n, q, chain):
                if q:
                    dve.wait_ge(hb_ready, n)
                dve.wait_ge(relu_done, 4 * n + 4 + 4)
                nc.vector.memset(sh[:, q, 3:4], EPS)
                chain(nc.vector.tensor_tensor_reduce(out=hq[:, :], in0=hr[:, q, :], in1=hr[:, q, :], scale=1.0, scalar=0.0,
                                                     op0=ALU.mult, op1=ALU.max, accum_out=sh[:, q, 0:1]))
                chain(nc.vector.tensor_scalar(sh[:, q, 0:1], sh[:, q, 0:1], sh[:, q, 3:4], None, ALU.max))
                chain(nc.vector.reciprocal(sh[:, q, 1:2], sh[:, q, 0:1]))
                chain(nc.vector.tensor_scalar(sh[:, q, 1:2], sh[:, q, 1:2], 127.0, None, ALU.mult))
                nc.vector.tensor_scalar(sh[:, q, 2:3], sh[:, q, 0:1], tot[:, 1, 1:2], 1.0 / 127.0, ALU.mult, ALU.mult)
                chain(nc.vector.tensor_scalar(hq[:, :], hq[:, :], sh[:, q, 1:2], MAGIC, ALU.mult, ALU.add))
                nc.vector.tensor_scalar(hb[:, q, :], hq[:, :], MAGIC, 127.0, ALU.subtract, ALU.min).then_inc(hb_ready, 1)

            def result(n, q):
                dve.wait_ge(dn_ready, n + 1)
                nc.vector.scalar_tensor_tensor(xs(n), ps[:, 7, :], sh[:, q, 2:3], xs(n), ALU.mult,
                                               ALU.add).then_inc(dn_done, 1)

            def body(b, more):
                chain = Chain(dve, chain_s, b * CHF + CHX)
                quantised_hidden(b * QT, 0, chain)
                if more:
                    quantised_tokens(b + 1, chain)
                quantised_hidden(b * QT + 1, 1, chain)
                if more:
                    unit_of(1)
                result(b * QT, 0)
                result(b * QT + 1, 1)
                assert chain.n == (CHF if more else CHF - CHX), chain.n

            quantised_tokens(0, Chain(dve, chain_s))
            unit_of(1)
            with dve.Fori(0, NB - 1) as b:
                body(b, True)
            body(NB - 1, False)


def attention1(nc, ps, K, k_scr, v_scr, wq_scr, wo_scr):
    NTL = GRP * QT
    OB = 7
    with ExitStack() as c:
        def sb(name, shape, dt):
            return c.enter_context(nc.sbuf_tensor(name, shape, dt))

        xT = sb("xT1", [128, 2, DC, NB * NTOK], fp16)

        def sem(name):
            return c.enter_context(nc.semaphore("c_" + name))

        wq = sb("wq_s", [128, DC, 2, 2, 512], fp16)
        wo = sb("wo_s", [128, GRP, 2, 512], fp16)
        kb = sb("keys", [128, 2, NKP], fp16)
        vb = sb("values", [128, KT1, 2, HD], fp16)
        wq_loaded, wo_loaded, k_loaded, v_loaded = sem("wq_loaded"), sem("wo_loaded"), sem("k_loaded"), sem("v_loaded")

        def load_wq(sp, kv):
            sp.dma_start(wq[:, :, :, :, :].rearrange("p i c s n -> p (i c) (s n)"),
                         wq_scr[bass.ds(kv, 1)].rearrange("a i p n -> p (a i) n")).then_inc(wq_loaded, 16)

        def load_wo(sp, kv):
            sp.dma_start(wo[:, :, :, :].rearrange("p i s n -> p i (s n)"),
                         wo_scr[bass.ds(kv, 1)].rearrange("a i p n -> p (a i) n")).then_inc(wo_loaded, 16)

        def load_keys(sp, kv, b):
            sp.dma_start(kb[:, :, NTOK:NKP], k_scr[bass.ds(b, 1), bass.ds(kv, 1)].rearrange(
                "a h p (s n) -> p (a h s) n", s=2)).then_inc(k_loaded, 16)

        def load_values(sp, kv, b):
            sp.dma_start(vb[:, 2:KT1], v_scr[bass.ds(b, 1), bass.ds(kv, 1)].rearrange(
                "a h p n -> p (a h n)")).then_inc(v_loaded, 16)

        def first_loads(sp):
            load_wq(sp, 0)
            load_keys(sp, 0, 0)
            load_values(sp, 0, 0)
            load_wo(sp, 0)

        layer_norm_turned(nc, ps, K, xT, SX, "c", first_loads)
        qT = sb("qT1", [128, 2, GRP, NTOK], fp16)
        prob = sb("prob1", [128, 2, NK], fp32)
        pT = sb("probT1", [128, 2, 2, KT1, NTOK], fp16)
        rb = sb("rb", [128, 2, NTOK], fp32)
        o32 = sb("o32", [128, 2, NTOK], fp32)
        oT = sb("oT", [128, 2, GRP, NTOK], fp16)
        mx = sb("mx1", [128, 4, 6], fp32)
        rs = sb("rs1", [128, 4, 4], fp32)

        def turns(h, q):
            return [(("p", h, q, g), (4, 5, 6, 4)[g]) for g in range(4)]

        order = [(("kl",), 4), (("q", 0), 5), (("vl",), 6), (("q", 1), 4), (("q", 2), 5), (("q", 3), 6)] + turns(0, 0)
        order += [(("q", 4), 5), (("q", 5), 6)] + turns(0, 1) + [(("q", 6), 5), (("q", 7), 6)]
        order += [x for h in range(1, GRP) for q in range(QT) for x in turns(h, q)]
        order += [(("wo", 0), 4), (("wo", 1), 5)]
        jobs = {name: n for n, (name, _) in enumerate(order)}
        bank_of = dict(order)
        PER = {k: sum(x == k for _, x in order) for k in (4, 5, 6)}
        at_bank = {name: sum(x == k for _, x in order[:n]) for n, (name, k) in enumerate(order)}
        TJ = len(order)
        SPLIT = TJ - QT

        t_ready, t_hi, t_free = sem("t_ready"), sem("t_hi"), {k: sem(f"t_free{k}") for k in PER}
        s_ready, max_done, bias_ready, s_free = sem("s_ready"), sem("max_done"), sem("bias_ready"), sem("s_free")
        sum_done, r_ready = sem("sum_done"), sem("r_ready")
        o_ready, rb_ready, o_free = sem("o_ready"), sem("rb_ready"), sem("o_free")
        ot_hi, ot_lo = sem("ot_hi"), sem("ot_lo")
        block = c.enter_context(nc.Block())

        def job(h, q, g):
            if isinstance(h, int):
                return jobs["p", h, q, g]
            return (h - 1) * 8 + (jobs["p", 1, 0, 0] + 4 * q + g)

        def bank(*name):
            return ps[:, bank_of[name], :]

        def freed(u, name, h=None):
            k = bank_of[name]
            n = at_bank[name] + 2
            if h is None:
                return u * PER[k] + n
            return u * PER[k] + (h - 1) * (4 if k == 4 else 2) + n

        def turn_name(h, q, g):
            return (("p", h, q, g), None) if isinstance(h, int) else (("p", 1, q, g), h)

        def flat(p):
            return ps[:, 2 * p:2 * p + 2, :].rearrange("p b n -> p (b n)")

        HALF = [(0, 1024), (1024, NK - 1024)]

        def heads(eng, body):
            with eng.Fori(0, (GRP - 2) // 2) as i:
                for e in range(2):
                    body(i * 2 + (1 + e), (1 + e) % 2)

        @block.sync
        def _(sp):
            def scores_done(u):
                sp.wait_ge(s_ready, (u + 1) * (4 * NTL) + 1)

            def values_done(u):
                sp.wait_ge(o_ready, (u + 1) * GRP + 1)

            def inner(kv):
                with sp.Fori(0, NB - 1) as b:
                    scores_done(kv * NB + b)
                    load_keys(sp, kv, b + 1)
                    values_done(kv * NB + b)
                    load_values(sp, kv, b + 1)

            with sp.Fori(0, KVH - 1) as kv:
                inner(kv)
                sp.wait_ge(t_ready, kv * (NB * TJ) + (NB - 1) * TJ + jobs["q", 7] + 2)
                load_wq(sp, kv + 1)
                scores_done(kv * NB + (NB - 1))
                load_keys(sp, kv + 1, 0)
                values_done(kv * NB + (NB - 1))
                load_values(sp, kv + 1, 0)
                sp.wait_ge(t_ready, (kv + 1) * (NB * TJ) + 1)
                load_wo(sp, kv + 1)
            inner(KVH - 1)

        @block.gpsimd
        def _(pool):
            with pool.Fori(0, KVH * NB) as u:
                def post(h, p):
                    G = u * GRP + h
                    pool.wait_ge(o_free, G + 2)
                    dst = [oT[:, s, bass.ds(h, 1), :].rearrange("p a n -> p (a n)") for s in range(2)]
                    nc.gpsimd.tensor_copy(dst[0], o32[:, p, :]).then_inc(ot_hi, 1)
                    pool.wait_ge(ot_hi, G + 1)
                    nc.gpsimd.tensor_tensor(dst[1], o32[:, p, :], dst[0], ALU.subtract).then_inc(ot_lo, 1)

                with pool.Fori(0, GRP // 2) as i:
                    for e in range(2):
                        post(i * 2 + e, e)

        @block.scalar
        def _(act):
            with act.Fori(0, KVH * NB) as u:
                def hi(n, dst, src, scale):
                    act.wait_ge(t_ready, u * TJ + n + 2)
                    nc.scalar.activation(dst, src, ACT.Copy, scale=scale).then_inc(t_hi, 1)

                def query_hi(h):
                    hi(jobs["q", h], qT[:, 0, h, :], bank("q", h)[:, 0:NTOK], SQ / math.sqrt(HD) / (SX * SW))

                def exps(h, q, p):
                    s = 2 * p + q
                    act.wait_ge(bias_ready, u * NTL + h * QT + q + 1)
                    for k, (o, w) in enumerate(HALF):
                        nc.scalar.activation(prob[:, q, o:o + w], flat(k)[:, 0:w], ACT.Exp, bias=mx[:, s, 5:6],
                                             scale=1.0 / (SQ * SX), accum_out=rs[:, s, k:k + 1]).then_inc(s_free, 1)

                def turned_hi(h, q, p, groups=range(4)):
                    for g in groups:
                        t = min(4, KT1 - 4 * g)
                        hi(job(h, q, g), pT[:, p, 0, 4 * g:4 * g + t, q * 128:(q + 1) * 128],
                           bank("p", 1, q, g)[:, 0:t * 128].rearrange("p (t n) -> p t n", t=t), SP_)

                def recip(h, p):
                    act.wait_ge(o_ready, u * GRP + h + 2)
                    nc.scalar.activation(rb[:, p, :], ps[:, OB, NTOK:2 * NTOK], ACT.Copy,
                                         scale=1.0 / SP_).then_inc(rb_ready, 1)

                hi(jobs["kl",], kb[:, 0, 0:NTOK], bank("kl")[:, 0:NTOK], 1.0 / SW)
                query_hi(0)
                hi(jobs["vl",], vb[:, 0:QT, 0, :], bank("vl")[:, 0:NTOK].rearrange("p (t n) -> p t n", t=QT), 1.0 / SW)
                query_hi(1)
                exps(0, 0, 0)
                query_hi(2)
                query_hi(3)
                turned_hi(0, 0, 0)
                exps(0, 1, 0)
                query_hi(4)
                query_hi(5)
                turned_hi(0, 1, 0)
                exps(1, 0, 1)
                query_hi(6)
                query_hi(7)

                def body(h, p):
                    turned_hi(h, 0, p)
                    exps(h, 1, p)
                    turned_hi(h, 1, p)
                    exps(h + 1, 0, 1 - p)
                    recip(h - 1, 1 - p)

                heads(act, body)
                h = GRP - 1
                turned_hi(h, 0, h % 2)
                exps(h, 1, h % 2)
                turned_hi(h, 1, h % 2, (0, 1))
                recip(h - 1, 1 - h % 2)
                turned_hi(h, 1, h % 2, (2, 3))
                recip(h, h % 2)

        @block.vector
        def _(dve):
            with dve.Fori(0, KVH * NB) as u:
                def lo(n, k, dst, src, scale, hi):
                    dve.wait_ge(t_hi, u * SPLIT + n + 1)
                    nc.vector.scalar_tensor_tensor(dst, src, scale, hi, ALU.mult, ALU.subtract).then_inc(t_free[k], 1)

                def query_lo(h):
                    lo(jobs["q", h], bank_of["q", h], qT[:, 1, h, :], bank("q", h)[:, 0:NTOK],
                       SQ / math.sqrt(HD) / (SX * SW), qT[:, 0, h, :])

                def bank_max(h, q, p, k):
                    T = u * NTL + h * QT + q
                    s = 2 * p + q
                    if k == 3:
                        dve.wait_ge(max_done, 5 * T + 3)
                        nc.vector.reduce_max(mx[:, s, 4:5], mx[:, s, 0:3], AX.X).then_inc(max_done, 1)
                    dve.wait_ge(s_ready, 4 * T + k + 2)
                    nc.vector.reduce_max(mx[:, s, k:k + 1], ps[:, k, 0:CUT1[k][1]], AX.X).then_inc(max_done, 1)

                def bias(h, q, p):
                    s = 2 * p + q
                    dve.wait_ge(max_done, (u * NTL + h * QT + q) * 5 + 5)
                    nc.vector.tensor_scalar(mx[:, s, 5:6], mx[:, s, 3:4], mx[:, s, 4:5], -1.0 / (SQ * SX), ALU.max,
                                            ALU.mult).then_inc(bias_ready, 1)

                def turned_lo(h, q, p, g):
                    t = min(4, KT1 - 4 * g)
                    dst = [pT[:, p, s, 4 * g:4 * g + t, q * 128:(q + 1) * 128] for s in range(2)]
                    lo(job(h, q, g), bank_of["p", 1, q, g], dst[1],
                       bank("p", 1, q, g)[:, 0:t * 128].rearrange("p (t n) -> p t n", t=t), SP_, dst[0])

                def sums(h, q, p):
                    s = 2 * p + q
                    T = u * NTL + h * QT + q
                    dve.wait_ge(s_free, 2 * T + 4)
                    nc.vector.tensor_tensor(rs[:, s, 2:3], rs[:, s, 0:1], rs[:, s, 1:2], ALU.add).then_inc(sum_done, 1)
                    dve.wait_ge(sum_done, T + 1)
                    nc.vector.reciprocal(rs[:, s, 3:4], rs[:, s, 2:3]).then_inc(r_ready, 1)

                def normalise(h, p):
                    G = u * GRP + h
                    dve.wait_ge(rb_ready, G + 1)
                    dve.wait_ge(ot_lo, G + 1)
                    nc.vector.tensor_tensor(o32[:, p, :], ps[:, OB, 0:NTOK], rb[:, p, :],
                                            ALU.mult).then_inc(o_free, 1)

                def step(h, q, p, nxt):
                    if nxt:
                        bank_max(*nxt, 0)
                    turned_lo(h, q, p, 0)
                    if nxt:
                        bank_max(*nxt, 1)
                    turned_lo(h, q, p, 1)
                    if nxt:
                        bank_max(*nxt, 2)
                        bank_max(*nxt, 3)
                        bias(*nxt)
                    turned_lo(h, q, p, 2)
                    turned_lo(h, q, p, 3)
                    sums(h, q, p)

                lo(jobs["kl",], bank_of["kl",], kb[:, 1, 0:NTOK], bank("kl")[:, 0:NTOK], 1.0 / SW, kb[:, 0, 0:NTOK])
                query_lo(0)
                lo(jobs["vl",], bank_of["vl",], vb[:, 0:QT, 1, :],
                   bank("vl")[:, 0:NTOK].rearrange("p (t n) -> p t n", t=QT), 1.0 / SW, vb[:, 0:QT, 0, :])
                for k in range(4):
                    bank_max(0, 0, 0, k)
                bias(0, 0, 0)
                for h in range(1, 4):
                    query_lo(h)
                step(0, 0, 0, (0, 1, 0))
                query_lo(4)
                query_lo(5)
                step(0, 1, 0, (1, 0, 1))
                query_lo(6)
                query_lo(7)

                def body(h, p):
                    step(h, 0, p, (h, 1, p))
                    step(h, 1, p, (h + 1, 0, 1 - p))
                    normalise(h - 1, 1 - p)

                heads(dve, body)
                h = GRP - 1
                step(h, 0, h % 2, (h, 1, h % 2))
                turned_lo(h, 1, h % 2, 0)
                turned_lo(h, 1, h % 2, 1)
                normalise(h - 1, 1 - h % 2)
                turned_lo(h, 1, h % 2, 2)
                turned_lo(h, 1, h % 2, 3)
                sums(h, 1, h % 2)
                normalise(h, h % 2)
                b = u % NB
                for q in range(QT):
                    dve.wait_ge(t_ready, u * TJ + jobs["wo", q] + 2)
                    xs = K["x"][:, bass.ds(b * QT + q, 1), :].rearrange("p a d -> p (a d)")
                    nc.vector.scalar_tensor_tensor(xs, bank("wo", q), 1.0 / (SX * SW), xs, ALU.mult,
                                                   ALU.add).then_inc(t_free[bank_of["wo", q]], 1)

        @block.tensor
        def _(pe):
            for s in (s_free, ot_lo):
                pe.sem_inc(s, 2)
            for s in (s_ready, o_ready, t_ready, o_free, *t_free.values()):
                pe.sem_inc(s, 1)

            def unit(kv, b):
                u = kv * NB + b

                def take(name, h=None):
                    pe.wait_ge(t_free[bank_of[name]], freed(u, name, h) - 1)
                    return bank(*name)

                def read(*name):
                    pe.wait_ge(t_free[bank_of[name]], freed(u, name))

                tok = [xT[:, s, :, bass.ds(b * NTOK, NTOK)] for s in range(2)]

                def keys_of_latents():
                    out = take(("kl",))
                    for i in range(DC):
                        last = mm3(nc, out[:, 0:NTOK], [K["wk"][:, s, i, bass.ds(kv * HD, HD)] for s in range(2)],
                                   [tok[s][:, i, :] for s in range(2)], i == 0, i == DC - 1)
                    last.then_inc(t_ready, 1)

                def values_of_latents():
                    out = take(("vl",))
                    for q in range(QT):
                        for i in range(DC):
                            last = mm3(nc, out[:, q * 128:(q + 1) * 128],
                                       [xT[:, s, i, bass.ds(b * NTOK + q * 128, 128)] for s in range(2)],
                                       [K["wv"][:, s, i, bass.ds(kv * HD, HD)] for s in range(2)], i == 0, i == DC - 1)
                    last.then_inc(t_ready, 1)

                def query(h):
                    out = take(("q", h))
                    for i in range(DC):
                        last = mm3(nc, out[:, 0:NTOK], [wq[:, i, h // 4, s, h % 4 * HD:(h % 4 + 1) * HD] for s in range(2)],
                                   [tok[s][:, i, :] for s in range(2)], i == 0, i == DC - 1)
                    last.then_inc(t_ready, 1)

                def scores(h, q, j):
                    T = u * NTL + h * QT + q
                    if j % 2 == 0:
                        pe.wait_ge(s_free, 2 * T + j // 2 + 1)
                    o, w = CUT1[j]
                    qs = [qT[:, s, bass.ds(h, 1), q * 128:(q + 1) * 128].rearrange("p a n -> p (a n)") for s in range(2)]
                    last = mm3(nc, ps[:, j, 0:w], qs, [kb[:, s, o:o + w] for s in range(2)], True, True)
                    last.then_inc(s_ready, 1)

                def turn(h, q, g):
                    T = u * NTL + h * QT + q
                    if g % 2 == 0:
                        pe.wait_ge(s_free, 2 * T + g // 2 + 3)
                    out = take(*turn_name(h, q, g))
                    for kt in range(4 * g, min(4 * g + 4, KT1)):
                        r = min(128, NK - kt * 128)
                        o = (kt - 4 * g) * 128
                        last = nc.tensor.transpose(out[0:r, o:o + 128], prob[:, q, kt * 128:kt * 128 + r],
                                                   K["id32"][:, :])
                    last.then_inc(t_ready, 1)

                def step(h, q, nxt):
                    for g in range(4):
                        if nxt:
                            scores(*nxt, g)
                        turn(h, q, g)

                def attend(h, p, k0, k1):
                    if k0 == 0:
                        pe.wait_ge(o_free, u * GRP + h + 1)
                    out = ps[:, OB, 0:NTOK]
                    for kt in range(k0, k1):
                        r = min(128, NK - kt * 128)
                        last = mm3(nc, out, [vb[0:r, kt, s, :] for s in range(2)], [pT[0:r, p, s, kt, :] for s in range(2)],
                                   kt == 0, kt == KT1 - 1)

                def spread(h, p):
                    pe.wait_ge(r_ready, u * NTL + h * QT + 2)
                    for q in range(QT):
                        last = nc.tensor.transpose(ps[:, OB, NTOK + q * 128:NTOK + (q + 1) * 128],
                                                   rs[:, 2 * p + q, 3:4].to_broadcast([128, 128]), K["id32"][:, :])
                    last.then_inc(o_ready, 1)

                KM = 8
                pe.wait_ge(wq_loaded, (kv + 1) * 16)
                keys_of_latents()
                query(0)
                values_of_latents()
                pe.wait_ge(v_loaded, (u + 1) * 16)
                pe.wait_ge(k_loaded, (u + 1) * 16)
                read("kl")
                read("q", 0)
                for j in range(4):
                    scores(0, 0, j)
                for h in range(1, 4):
                    query(h)
                step(0, 0, (0, 1))
                query(4)
                query(5)
                read("q", 1)
                step(0, 1, (1, 0))
                query(6)
                query(7)

                def body(h, p):
                    step(h, 0, (h, 1))
                    attend(h - 1, 1 - p, 0, KM)
                    step(h, 1, (h + 1, 0))
                    attend(h - 1, 1 - p, KM, KT1)
                    spread(h - 1, 1 - p)

                heads(pe, body)
                h = GRP - 1
                p = h % 2
                step(h, 0, (h, 1))
                attend(h - 1, 1 - p, 0, KM)
                turn(h, 1, 0)
                turn(h, 1, 1)
                attend(h - 1, 1 - p, KM, KT1)
                spread(h - 1, 1 - p)
                turn(h, 1, 2)
                turn(h, 1, 3)

                def project(q, hs):
                    for hh in hs:
                        last = mm3(nc, bank("wo", q), [oT[:, s, hh, q * 128:(q + 1) * 128] for s in range(2)],
                                   [wo[:, hh, s, :] for s in range(2)], hh == 0, hh == GRP - 1)
                    return last

                pe.wait_ge(wo_loaded, (kv + 1) * 16)
                pe.wait_ge(ot_lo, u * GRP + 4 + 2)
                for q in range(QT):
                    take(("wo", q))
                    project(q, range(4))
                for g in (1, 2, 3):
                    read("p", h, 1, g)
                attend(h, p, 0, KT1)
                spread(h, p)
                pe.wait_ge(ot_lo, u * GRP + (GRP - 1) + 2)
                project(0, (4, 5, 6))
                project(1, (4, 5))
                pe.wait_ge(ot_lo, u * GRP + GRP + 2)
                project(0, (7,)).then_inc(t_ready, 1)
                project(1, (6, 7)).then_inc(t_ready, 1)

            with pe.Fori(0, KVH) as kv:
                with pe.Fori(0, NB) as b:
                    unit(kv, b)


def layer_norm_turned(nc, ps, K, xT, scale, tag, loads):
    with ExitStack() as c:
        def sb(name, shape, dt):
            return c.enter_context(nc.sbuf_tensor(name + tag, shape, dt))

        def sem(name):
            return c.enter_context(nc.semaphore(tag + "n_" + name))

        xln = sb("xlnn", [128, NT, D], fp32)
        stats = stats_tiles(sb, "n")
        _, mv, ve, yh = stats
        var_ready, pow_ready, chain_s, xln_ready, t_ready, t_hi, t_lo = (
            sem(n) for n in ("var_ready", "pow_ready", "chain", "xln_ready", "t_ready", "t_hi", "t_lo"))
        block = c.enter_context(nc.Block())

        @block.sync
        def _(sp):
            loads(sp)

        @block.gpsimd
        def _(pool):
            pool.wait_ge(var_ready, 1)
            nc.gpsimd.tensor_tensor(yh[:, 0, :], ve[:, :], K["mhalf"][:, :], ALU.pow).then_inc(pow_ready, 1)

        @block.vector
        def _(dve):
            def low(n):
                dve.wait_ge(t_hi, n + 1)
                nc.vector.scalar_tensor_tensor(xT[:, 1, :, n * 128:(n + 1) * 128],
                                               ps[:, n % 4, :].rearrange("p (c n) -> p c n", c=DC), scale,
                                               xT[:, 0, :, n * 128:(n + 1) * 128], ALU.mult,
                                               ALU.subtract).then_inc(t_lo, 1)

            layer_norm_stats(nc, dve, Chain(dve, chain_s), K, stats, var_ready, pow_ready)
            for n in range(NT):
                nc.vector.tensor_scalar(xln[:, n, :], K["x"][:, n, :], mv[:, n, 0:1], yh[:, 2, n:n + 1],
                                        ALU.subtract, ALU.mult).then_inc(xln_ready, 1)
                if n >= 3:
                    low(n - 3)
            for n in range(NT - 3, NT):
                low(n)

        @block.tensor
        def _(pe):
            for n in range(NT):
                pe.wait_ge(xln_ready, n + 1)
                if n >= 4:
                    pe.wait_ge(t_lo, n - 3)
                for i in range(DC):
                    last = nc.tensor.transpose(ps[:, n % 4, i * 128:(i + 1) * 128],
                                               xln[:, n, i * 128:(i + 1) * 128], K["id32"][:, :])
                last.then_inc(t_ready, 1)

        @block.scalar
        def _(act):
            for n in range(NT):
                act.wait_ge(t_ready, n + 1)
                nc.scalar.activation(xT[:, 0, :, n * 128:(n + 1) * 128],
                                     ps[:, n % 4, :].rearrange("p (c n) -> p c n", c=DC), ACT.Copy,
                                     scale=scale).then_inc(t_hi, 1)


def ffn1(nc, ps, K, baseW, gateW, loraA, loraB, out):
    GA = NE + NR
    HR = NR // 2
    with ExitStack() as c:
        def sb(name, shape, dt):
            return c.enter_context(nc.sbuf_tensor(name, shape, dt))

        def sem(name):
            return c.enter_context(nc.semaphore("d_" + name))

        xT = sb("xT2", [128, 2, DC, NB * NTOK], fp16)
        braw = sb("base_raw", [128, DC, D], fp32)
        graw = sb("gate_raw", [NE, D], fp32)
        araw = sb("a_raw", [HR, 2, D], fp32)
        lraw = sb("b_raw", [128, DC, NE, RANK], fp32)
        bT = sb("base_T", [128, 2, DC, D], fp16)
        gaT = sb("ga_T", [128, 2, DC, GA], fp16)
        lT = sb("b_T", [HR, 2, 2, D], fp16)
        iota = sb("iota", [128, NE], fp32)
        ga = sb("ga", [128, 2, GA], fp32)
        top = sb("top", [128, 2, 8], fp32)
        topi = sb("topi", [128, 2, 8], u32)
        tf = sb("tf", [128, 2, 8], fp32)
        gate = sb("gate", [128, 2, 2, NE], fp32)
        hg = sb("hg", [128, 2, NR], fp32)
        hgT = sb("hgT", [HR, 2, 2, 2, 128], fp16)
        y = sb("y", [128, 2, D], fp32)
        loaded = [sem(f"loaded{i}") for i in range(4)]

        def loads(sp):
            sp.dma_start(braw[:, :, :], baseW.rearrange("(c p) n -> p c n", p=128)).then_inc(loaded[0], 16)
            sp.dma_start(graw[:, :], gateW).then_inc(loaded[1], 16)
            sp.dma_start(araw[:, :, :], loraA.rearrange("e r n -> (e r) n").rearrange("(c p) n -> p c n", p=HR)
                         ).then_inc(loaded[2], 16)
            for i in range(DC):
                sp.dma_start(lraw[:, i], loraB[:, i * 128:(i + 1) * 128, :].rearrange("e p r -> p e r")
                             ).then_inc(loaded[3], 16)

        layer_norm_turned(nc, ps, K, xT, SX, "d", loads)
        (iota_s, w_ready, w_hi, w_lo, ga_ready, ga_free, top_s, ex_ready, pr_ready, hg_ready, ht_ready, ht_hi, ht_lo,
         y_ready, y_free, chain_s) = (sem(n) for n in (
             "iota", "w_ready", "w_hi", "w_lo", "ga_ready", "ga_free", "top", "ex_ready", "pr_ready", "hg_ready",
             "ht_ready", "ht_hi", "ht_lo", "y_ready", "y_free", "chain"))
        stored = [sem(f"stored{i}") for i in range(2)]
        block = c.enter_context(nc.Block())

        prep = []
        for i in range(DC):
            prep.append(([bT[:, s, i, :] for s in range(2)], D, 128))
        for i in range(DC):
            prep.append(([gaT[:, s, i, :] for s in range(2)], GA, 128))
        for r in range(2):
            prep.append(([lT[:, s, r, :] for s in range(2)], D, HR))

        @block.sync
        def _(sp):
            for n in range(NT):
                sp.wait_ge(y_free, n + 1)
                sp.dma_start(out[n // QT, (n % QT) * 128:(n % QT + 1) * 128, :], y[:, n % 2, :]).then_inc(stored[n % 2], 16)
            for s in stored:
                sp.wait_ge(s, 16 * NT // 2)

        @block.gpsimd
        def _(pool):
            nc.gpsimd.iota(iota[:, :], pattern=[[1, NE]], base=0, channel_multiplier=0,
                           allow_small_or_imprecise_dtypes=True).then_inc(iota_s, 1)

        @block.tensor
        def _(pe):
            for n in range(len(prep)):
                if n >= 4:
                    pe.wait_ge(w_lo, n - 3)
                o = ps[:, n % 4, :]
                if n < DC:
                    pe.wait_ge(loaded[0], 16)
                    for a in range(DC):
                        last = nc.tensor.transpose(o[:, a * 128:(a + 1) * 128], braw[:, a, n * 128:(n + 1) * 128],
                                                   K["id32"][:, :])
                elif n < 2 * DC:
                    i = n - DC
                    pe.wait_ge(loaded[1], 16)
                    pe.wait_ge(loaded[2], 16)
                    nc.tensor.transpose(o[:, 0:NE], graw[:, i * 128:(i + 1) * 128], K["id32"][0:NE, 0:NE])
                    for a in range(2):
                        last = nc.tensor.transpose(o[:, NE + a * HR:NE + (a + 1) * HR], araw[:, a, i * 128:(i + 1) * 128],
                                                   K["id32"][0:HR, 0:HR])
                else:
                    r = n - 2 * DC
                    pe.wait_ge(loaded[3], 16 * DC)
                    for a in range(DC):
                        last = nc.tensor.transpose(o[0:HR, a * 128:(a + 1) * 128],
                                                   lraw[:, a].rearrange("p e r -> p (e r)")[:, r * HR:(r + 1) * HR],
                                                   K["id32"][:, :])
                last.then_inc(w_ready, 1)
            pe.wait_ge(w_lo, len(prep))

            def gates(n):
                if n >= 2:
                    pe.wait_ge(ga_free, n - 1)
                for i in range(DC):
                    last = mm3(nc, ps[:, 4 + n % 2, 0:GA], [xT[:, s, i, n * 128:(n + 1) * 128] for s in range(2)],
                               [gaT[:, s, i, :] for s in range(2)], i == 0, i == DC - 1)
                last.then_inc(ga_ready, 1)

            def base(n):
                if n >= 2:
                    pe.wait_ge(y_free, n - 1)
                for i in range(DC):
                    mm3(nc, ps[:, 6 + n % 2, :], [xT[:, s, i, n * 128:(n + 1) * 128] for s in range(2)],
                        [bT[:, s, i, :] for s in range(2)], i == 0, False)

            gates(0)
            base(0)
            gates(1)
            for n in range(NT):
                pe.wait_ge(hg_ready, n + 1)
                if n >= 2:
                    pe.wait_ge(ht_lo, n - 1)
                for r in range(2):
                    last = nc.tensor.transpose(ps[0:HR, n % 2, r * 128:(r + 1) * 128],
                                               hg[:, n % 2, r * HR:(r + 1) * HR], K["id32"][:, :])
                last.then_inc(ht_ready, 1)
                if n + 1 < NT:
                    base(n + 1)
                pe.wait_ge(ht_lo, n + 1)
                for r in range(2):
                    last = mm3(nc, ps[:, 6 + n % 2, :], [hgT[:, n % 2, s, r, :] for s in range(2)],
                               [lT[:, s, r, :] for s in range(2)], False, r == 1)
                last.then_inc(y_ready, 1)
                if n + 2 < NT:
                    gates(n + 2)

        @block.scalar
        def _(act):
            for n, (dst, w, r) in enumerate(prep):
                act.wait_ge(w_ready, n + 1)
                nc.scalar.activation(dst[0], ps[0:r, n % 4, 0:w], ACT.Copy, scale=SW).then_inc(w_hi, 1)
            def exp_gap(n):
                act.wait_ge(top_s, n + 1)
                nc.scalar.activation(tf[:, n % 2, 3:4], tf[:, n % 2, 2:3], ACT.Exp).then_inc(ex_ready, 1)

            exp_gap(0)
            for n in range(NT):
                act.wait_ge(ht_ready, n + 1)
                nc.scalar.activation(hgT[:, n % 2, 0], ps[0:HR, n % 2, 0:256].rearrange("p (r n) -> p r n", r=2),
                                     ACT.Copy, scale=SX).then_inc(ht_hi, 1)
                if n + 1 < NT:
                    exp_gap(n + 1)

        @block.vector
        def _(dve):
            chain = Chain(dve, chain_s)
            for n, (dst, w, r) in enumerate(prep):
                dve.wait_ge(w_hi, n + 1)
                nc.vector.scalar_tensor_tensor(dst[1], ps[0:r, n % 4, 0:w], SW, dst[0], ALU.mult,
                                               ALU.subtract).then_inc(w_lo, 1)
            dve.wait_ge(iota_s, 1)
            def gated(n):
                p = n % 2
                dve.wait_ge(ga_ready, n + 1)
                nc.vector.tensor_scalar(ga[:, p, :], ps[:, 4 + p, 0:GA], 1.0 / (SX * SW), None,
                                        ALU.mult).then_inc(ga_free, 1)
                dve.wait_ge(ga_free, n + 1)
                chain(nc.vector.max(top[:, p, :], ga[:, p, 0:NE]))
                chain(nc.vector.max_index(topi[:, p, :], top[:, p, :], ga[:, p, 0:NE]))
                nc.vector.tensor_tensor(tf[:, p, 2:3], top[:, p, 1:2], top[:, p, 0:1], ALU.subtract).then_inc(top_s, 1)
                chain(nc.vector.tensor_copy(tf[:, p, 0:2], topi[:, p, 0:2]))
                dve.wait_ge(ex_ready, n + 1)
                chain(nc.vector.tensor_scalar(tf[:, p, 4:5], tf[:, p, 3:4], 1.0, None, ALU.add))
                chain(nc.vector.reciprocal(tf[:, p, 5:6], tf[:, p, 4:5]))
                chain(nc.vector.tensor_scalar(tf[:, p, 6:7], tf[:, p, 5:6], TOPK_SCALE, None, ALU.mult))
                chain(nc.vector.tensor_scalar(tf[:, p, 7:8], tf[:, p, 6:7], tf[:, p, 3:4], None, ALU.mult))
                nc.vector.tensor_scalar(gate[:, p, 0, :], iota[:, :], tf[:, p, 0:1], tf[:, p, 6:7], ALU.is_equal, ALU.mult)
                chain(nc.vector.tensor_scalar(gate[:, p, 1, :], iota[:, :], tf[:, p, 1:2], tf[:, p, 7:8], ALU.is_equal,
                                              ALU.mult))
                chain(nc.vector.tensor_tensor(gate[:, p, 0, :], gate[:, p, 0, :], gate[:, p, 1, :], ALU.add))
                nc.vector.tensor_tensor(hg[:, p, :].rearrange("p (e r) -> p e r", r=RANK),
                                        ga[:, p, NE:GA].rearrange("p (e r) -> p e r", r=RANK),
                                        gate[:, p, 0, :].rearrange("p (e a) -> p e a", a=1).to_broadcast([128, NE, RANK]),
                                        ALU.mult).then_inc(hg_ready, 1)

            gated(0)
            for n in range(NT):
                p = n % 2
                dve.wait_ge(ht_hi, n + 1)
                nc.vector.scalar_tensor_tensor(hgT[:, p, 1], ps[0:HR, p, 0:256].rearrange("p (r n) -> p r n", r=2), SX,
                                               hgT[:, p, 0], ALU.mult, ALU.subtract).then_inc(ht_lo, 1)
                if n + 1 < NT:
                    gated(n + 1)
                dve.wait_ge(y_ready, n + 1)
                if n >= 2:
                    dve.wait_ge(stored[p], 16 * (n // 2))
                nc.vector.scalar_tensor_tensor(y[:, p, :], ps[:, 6 + p, :], 1.0 / (SX * SW), K["x"][:, n, :], ALU.mult,
                                               ALU.add).then_inc(y_free, 1)


_INS = ['x', 'ctx_4096', 'L0_xattn_Wq', 'L0_xattn_bq', 'L0_xattn_Wk', 'L0_xattn_bk', 'L0_ffn_w_up', 'L0_ffn_w_down',
        'L1_xattn_Wq', 'L1_xattn_Wk', 'L1_xattn_Wv', 'L1_xattn_Wo', 'L1_ffn_base_W', 'L1_ffn_gate_W', 'L1_ffn_lora_A',
        'L1_ffn_lora_B']
_OUTS = [((4, 256, 512), 'float32')]


def kernel(**inputs):
    import numpy as _np
    import concourse.bacc as _bacc
    from concourse import mybir as _mybir
    from concourse.bass_utils import run_bass_kernel_spmd as _run

    nc = _bacc.Bacc("TRN2", target_bir_lowering=False, num_devices=1)
    arrays, args = {}, []
    for name in _INS:
        a = _np.ascontiguousarray(inputs[name])
        arrays[f"in_{name}_dram"] = a
        args.append(nc.dram_tensor(f"in_{name}_dram", a.shape, _mybir.dt.from_np(a.dtype), kind="ExternalInput").ap())
    for i, (shape, dtype) in enumerate(_OUTS):
        dt = _mybir.dt.from_np(_np.dtype(dtype))
        args.append(nc.dram_tensor(f"out_{i}_dram", shape, dt, kind="ExternalOutput").ap())
    build(nc, *args)
    r = _run(nc, [arrays], core_ids=[0])
    got = tuple(r.results[0][f"out_{i}_dram"] for i in range(len(_OUTS)))
    return got[0]
```

```python
import concourse.bass as bass
from concourse import mybir
from contextlib import ExitStack
import math

fp32 = mybir.dt.float32
fp16 = mybir.dt.float16
bf16 = mybir.dt.bfloat16
u32 = mybir.dt.uint32
ALU = mybir.AluOpType
ACT = mybir.ActivationFunctionType
AX = mybir.AxisListType

NB = 4
NTOK = 256
QT = NTOK // 128
NT = NB * QT
D = 512
DC = D // 128
NC = 1601
KT0 = -(-NC // 128)
REST = NC - (KT0 - 1) * 128
F = 2048
FC = F // 128
NFP = F // 128
KVH = 4
GRP = 8
HD = 128
NK = NTOK + NC
KT1 = -(-NK // 128)
NCP = NC + NC % 2
NKP = NTOK + NCP
NE, RANK, TOPK_SCALE = 28, 8, 2.0
NR = NE * RANK
EPS = 1e-5
MAGIC = 1.5 * 2.0 ** 23

SX = 64.0
SW = 1024.0
SQ = 512.0
SP_ = 4096.0


def banks(n):
    return [(o, min(512, n - o)) for o in range(0, n, 512)]


CUT0 = banks(NC)


def mm3(nc, out, a, b, start, stop):
    nc.tensor.matmul(out, a[0], b[0], start=start, stop=False)
    nc.tensor.matmul(out, a[0], b[1], start=False, stop=False)
    return nc.tensor.matmul(out, a[1], b[0], start=False, stop=stop)


class Chain:

    def __init__(self, eng, sem, base=0):
        self.eng, self.sem, self.base, self.n = eng, sem, base, 0

    def __call__(self, ins):
        self.n += 1
        ins.then_inc(self.sem, 1)
        self.eng.wait_ge(self.sem, self.base + self.n)


def row_moments(nc, K, n):
    return nc.vector.bn_stats(K["st"][:, bass.ds(n, 1), :].rearrange("p a c -> p (a c)"),
                              K["x"][:, bass.ds(n, 1), :].rearrange("p a d -> p (a d)"))


def layer_norm_stats(nc, dve, chain, K, stats, s_var, s_pow, moments):
    mv, ve, yh = stats
    for n in moments:
        last = row_moments(nc, K, n)
    chain(last)
    for n in range(NT):
        last = nc.vector.bn_aggr(mv[:, n, :], K["st"][:, n, :])
    chain(last)
    nc.vector.tensor_scalar(ve[:, :], mv[:, :, 1], EPS, None, ALU.add).then_inc(s_var, 1)
    dve.wait_ge(s_var, 1)
    dve.wait_ge(s_pow, 1)
    chain(nc.vector.tensor_tensor(yh[:, 1, :], yh[:, 0, :], yh[:, 0, :], ALU.mult))
    chain(nc.vector.tensor_tensor(yh[:, 1, :], yh[:, 1, :], ve[:, :], ALU.mult))
    chain(nc.vector.tensor_scalar(yh[:, 1, :], yh[:, 1, :], -0.5, 1.5, ALU.mult, ALU.add))
    nc.vector.tensor_tensor(yh[:, 2, :], yh[:, 0, :], yh[:, 1, :], ALU.mult).then_inc(s_var, 1)
    dve.wait_ge(s_var, 2)


def stats_tiles(sb, tag):
    return sb("mv" + tag, [128, NT, 2], fp32), sb("ve" + tag, [128, NT], fp32), sb("yh" + tag, [128, 3, NT], fp32)


def build(nc, x, ctx4, Wq0, bq0, Wk0, bk0, Wup, Wdn, Wq1, Wk1, Wv1, Wo1, baseW, gateW, loraA, loraB, out):
    k_scr = nc.dram_tensor("k_scr", (NB, KVH, 128, 2 * NCP), fp16, kind="Internal").ap()
    v_scr = nc.dram_tensor("v_scr", (NB, KVH, 128, KT0 * 2 * HD), fp16, kind="Internal").ap()
    wq_scr = nc.dram_tensor("wq_scr", (KVH, 8, 128, 2 * 512), fp16, kind="Internal").ap()
    wo_scr = nc.dram_tensor("wo_scr", (KVH, 8, 128, 2 * 512), fp16, kind="Internal").ap()

    with ExitStack() as keep:
        def sbk(name, shape, dt):
            return keep.enter_context(nc.sbuf_tensor(name, shape, dt))

        ps = keep.enter_context(nc.psum_tensor("ps", [128, 8, 512], fp32))
        K = {
            "id32": sbk("id32", [128, 128], fp32),
            "id16": sbk("id16", [128, 128], fp16),
            "x": sbk("x_all", [128, NT, D], fp32),
            "wk": sbk("wk_split", [128, 2, DC, 512], fp16),
            "wv": sbk("wv_split", [128, 2, DC, 512], fp16),
            "mhalf": sbk("mhalf", [128, NT], fp32),
            "st": sbk("row_moments", [128, NT, 6], fp32),
            "part": sbk("ffn_part", [128, 2, NFP], fp32),
        }
        with ExitStack() as a:
            M = {
                "m": a.enter_context(nc.sbuf_tensor("m_split", [128, 2, DC, 512], fp16)),
                "qb": a.enter_context(nc.sbuf_tensor("q_bias", [128, DC], fp32)),
                "wb": a.enter_context(nc.sbuf_tensor("wb_split", [128, 2, DC], fp16)),
                "c0": a.enter_context(nc.sbuf_tensor("c0", [128, 1], fp32)),
                "ctx": a.enter_context(nc.sbuf_tensor("ctx_raw", [128, KT0, D], fp32)),
                "loaded": a.enter_context(nc.semaphore("ctx_loaded")),
                "stats": stats_tiles(lambda name, shape, dt: a.enter_context(nc.sbuf_tensor(name, shape, dt)), "0"),
            }
            prepare(nc, ps, K, M, x, ctx4, Wq0, bq0, Wk0, bk0, Wk1, Wv1)
            attention0(nc, ps, K, M, ctx4, Wq1, Wo1, Wup, Wdn, k_scr, v_scr, wq_scr, wo_scr)
        ffn0(nc, ps, K, Wup, Wdn)
        attention1(nc, ps, K, k_scr, v_scr, wq_scr, wo_scr)
        ffn1(nc, ps, K, baseW, gateW, loraA, loraB, out)


def load_context(sp, M, ctx4, b):
    sp.dma_start(M["ctx"][:, 0:KT0 - 1, :],
                 ctx4[bass.ds(b, 1), 0:(KT0 - 1) * 128, :].rearrange("a (t p) d -> p (a t) d", p=128)
                 ).then_inc(M["loaded"], 16)
    sp.dma_start(M["ctx"][0:REST, KT0 - 1, :],
                 ctx4[bass.ds(b, 1), (KT0 - 1) * 128:NC, :].rearrange("a p d -> p (a d)")
                 ).then_inc(M["loaded"], 16)


def prepare(nc, ps, K, M, x, ctx4, Wq0, bq0, Wk0, bk0, Wk1, Wv1):
    with ExitStack() as c:
        def sb(name, shape, dt):
            return c.enter_context(nc.sbuf_tensor(name, shape, dt))

        def sem(name):
            return c.enter_context(nc.semaphore(name))

        raw = sb("w_raw", [128, 4, DC, 512], fp32)
        spl = sb("w_spl", [128, 2, 2, DC, 512], fp16)
        bcol = sb("b_col", [128, 2, DC], fp32)
        wb32 = sb("wb32", [128, DC], fp32)
        s_w = [sem(f"p_w{i}") for i in range(4)]
        s_var, s_pow, s_ch = sem("p_var"), sem("p_pow"), sem("p_ch")
        s_b, s_xin, s_id, s_hi, s_lo, s_m, s_mh, s_ml, s_col, s_wb = (
            sem(n) for n in ("p_b", "p_x", "p_id", "p_hi", "p_lo", "p_m", "p_mh", "p_ml", "p_col", "p_wb"))
        block = c.enter_context(nc.Block())

        @block.sync
        def _(sp):
            for i, w in enumerate((Wq0, Wk0, Wk1, Wv1)):
                if i == 2:
                    sp.dma_start(K["x"][:, :, :], x.rearrange("b (q p) d -> p (b q) d", p=128)).then_inc(s_xin, 16)
                sp.dma_start(raw[:, i], w.rearrange("(c p) n -> p c n", p=128)).then_inc(s_w[i], 16)
            load_context(sp, M, ctx4, 0)
            sp.wait_ge(s_xin, 16)

        @block.gpsimd
        def _(pool):
            nc.gpsimd.memset(K["id32"][:, :], 0.0).then_inc(s_id, 1)
            nc.gpsimd.memset(K["id16"][:, :], 0.0).then_inc(s_id, 1)
            nc.gpsimd.memset(K["mhalf"][:, :], -0.5).then_inc(s_id, 1)
            pool.wait_ge(s_id, 3)
            for m in (K["id32"], K["id16"]):
                nc.gpsimd.affine_select(out=m[:, :], in_=m[:, :], compare_op=ALU.not_equal, fill=1.0, base=0,
                                        pattern=[[-1, 128]], channel_multiplier=1).then_inc(s_id, 1)
            pool.wait_ge(s_var, 1)
            nc.gpsimd.tensor_tensor(M["stats"][2][:, 0, :], M["stats"][1][:, :], K["mhalf"][:, :], ALU.pow).then_inc(s_pow, 1)

        @block.scalar
        def _(act):
            act.dma_start(bcol[:, 0, :], bq0.rearrange("(c p) -> p c", p=128), allow_slow_non_contiguous=True).then_inc(s_b, 16)
            act.dma_start(bcol[:, 1, :], bk0.rearrange("(c p) -> p c", p=128), allow_slow_non_contiguous=True).then_inc(s_b, 16)
            for i, dst in enumerate((spl[:, 0, 0], spl[:, 1, 0], K["wk"][:, 0], K["wv"][:, 0])):
                act.wait_ge(s_w[i], 16)
                nc.scalar.activation(dst, raw[:, i], ACT.Copy, scale=SW).then_inc(s_hi, 1)
            for i in range(DC):
                act.wait_ge(s_m, i + 1)
                nc.scalar.activation(M["m"][:, 0, i, :], ps[:, i, :], ACT.Copy, scale=1.0 / SW).then_inc(s_mh, 1)

        @block.vector
        def _(dve):
            for i, (hi, lo) in enumerate(((spl[:, 0, 0], spl[:, 0, 1]), (spl[:, 1, 0], spl[:, 1, 1]),
                                          (K["wk"][:, 0], K["wk"][:, 1]), (K["wv"][:, 0], K["wv"][:, 1]))):
                if i == 2:
                    dve.wait_ge(s_xin, 16)
                    layer_norm_stats(nc, dve, Chain(dve, s_ch), K, M["stats"], s_var, s_pow, range(NT))
                dve.wait_ge(s_hi, i + 1)
                nc.vector.scalar_tensor_tensor(lo.rearrange("p c n -> p (c n)"), raw[:, i].rearrange("p c n -> p (c n)"),
                                               SW, hi.rearrange("p c n -> p (c n)"),
                                               ALU.mult, ALU.subtract).then_inc(s_lo, 1)
            for i in range(DC):
                dve.wait_ge(s_mh, i + 1)
                nc.vector.scalar_tensor_tensor(M["m"][:, 1, i, :], ps[:, i, :], 1.0 / SW, M["m"][:, 0, i, :],
                                               ALU.mult, ALU.subtract).then_inc(s_ml, 1)
            f0 = SQ / math.sqrt(D)
            dve.wait_ge(s_col, 1)
            nc.vector.tensor_scalar(M["qb"][:, :], ps[:, 4, 0:DC], f0, None, ALU.mult)
            nc.vector.tensor_scalar(M["c0"][:, :], ps[:, 6, 0:1], SX * f0, None, ALU.mult)
            nc.vector.tensor_scalar(wb32[:, :], ps[:, 5, 0:DC], SX, None, ALU.mult).then_inc(s_wb, 1)
            dve.wait_ge(s_wb, 1)
            nc.vector.tensor_copy(M["wb"][:, 0, :], wb32[:, :]).then_inc(s_wb, 1)
            dve.wait_ge(s_wb, 2)
            nc.vector.tensor_tensor(M["wb"][:, 1, :], wb32[:, :], M["wb"][:, 0, :], ALU.subtract)

        @block.tensor
        def _(pe):
            pe.wait_ge(s_lo, 2)
            for i in range(DC):
                for d in range(DC):
                    last = mm3(nc, ps[:, i, :], [spl[:, 0, h, d, i * 128:(i + 1) * 128] for h in range(2)],
                               [spl[:, 1, h, d, :] for h in range(2)], d == 0, d == DC - 1)
                last.then_inc(s_m, 1)
            pe.wait_ge(s_b, 32)
            for bank, w, v in ((4, 1, 0), (5, 0, 1)):
                for i in range(DC):
                    for d in range(DC):
                        nc.tensor.matmul(ps[:, bank, i:i + 1], raw[:, w, d, i * 128:(i + 1) * 128],
                                         bcol[:, v, d:d + 1], start=(d == 0), stop=(d == DC - 1))
            for d in range(DC):
                last = nc.tensor.matmul(ps[:, 6, 0:1], bcol[:, 0, d:d + 1].to_broadcast([128, 128]),
                                        bcol[:, 1, d:d + 1], start=(d == 0), stop=(d == DC - 1))
            last.then_inc(s_col, 1)



def attention0(nc, ps, K, M, ctx4, Wq1, Wo1, Wup, Wdn, k_scr, v_scr, wq_scr, wo_scr):
    with ExitStack() as c:
        def sb(name, shape, dt):
            return c.enter_context(nc.sbuf_tensor(name, shape, dt))

        def sem(name):
            return c.enter_context(nc.semaphore("a_" + name))

        raw = M["ctx"]
        nat = sb("ctx_nat", [128, 2, KT0, D], fp16)
        ctT = sb("ctx_T", [128, 2, DC, NCP], fp16)
        prob = sb("prob0", [128, NC], fp32)
        pT = sb("probT0", [128, 2, KT0, 128], fp16)
        kst = sb("k_stage", [128, 2, 2, NCP], fp16)
        vst = sb("v_stage", [128, KVH, KT0, 2, HD], fp16)
        xln = sb("xln0", [128, QT, D], fp32)
        xT = sb("xT0", [128, 2, DC, NTOK], fp16)
        q32 = sb("q32", [128, DC, NTOK], fp32)
        qT = sb("qT0", [128, 2, DC, NTOK], fp16)
        wraw = sb("wp_raw", [128, 2, 512], fp32)
        wspl = sb("wp_spl", [128, 2, 2, 512], fp16)
        fraw = sb("fp_raw", [128, 2, 512], fp32)
        mv, _, yh = M["stats"]
        cc = sb("cc0", [128, QT], fp32)
        mx = sb("mx0", [128, QT, 8], fp32)
        rs = sb("rs0", [128, QT, 4], fp32)

        TB, PB = 4, 6
        NG = -(-KT0 // 4)
        t_order = [("ln", q) for q in range(QT)] + [("p", q, g) for q in range(QT) for g in range(NG)]
        tj = {name: n for n, name in enumerate(t_order)}
        TJ = len(tj)
        p_order = [("k", 0, j) for j in range(4)] + [("q", i) for i in range(DC)] + [("c", 0)]
        p_order += [("k", h, j) for h in (1, 2, 3) for j in range(4)] + [("pv", 0)]
        p_order += [("v", kt) for kt in range(KT0)] + [("pv", 1)]
        pj = {name: n for n, name in enumerate(p_order)}
        PJ = len(pj)
        assert TJ % 2 == 0 and PJ % 2 == 0
        t_split = [x for x in t_order if x[0] in ("ln", "p")]
        p_split = [x for x in p_order if x[0] in ("k", "v")]
        assert NFP == NB * KVH
        VPARTS = [(0, 8), (8, KT0)]
        NP = 16
        CH = 3 * QT + 3 * QT

        ctx_loaded, nat_hi, nat_lo = M["loaded"], sem("nat_hi"), sem("nat_lo")
        f_loaded, f_clamped, f_summed = sem("f_loaded"), sem("f_clamped"), sem("f_summed")
        c_ready, c_free = [sem(f"c_ready{s}") for s in range(2)], [sem(f"c_free{s}") for s in range(2)]
        t_ready, t_hi, t_free = sem("t_ready"), sem("t_hi"), [sem(f"t_free{i}") for i in range(2)]
        p_ready, p_hi, p_free = sem("p_ready"), sem("p_hi"), [sem(f"p_free{i}") for i in range(2)]
        xln_ready, chain_s = sem("xln_ready"), sem("chain")
        q_hi, q_lo = sem("q_hi"), sem("q_lo")
        s_ready, s_free, bias_ready = sem("s_ready"), sem("s_free"), sem("bias_ready")
        k_staged, v_staged = sem("k_staged"), sem("v_staged")
        k_stored, v_stored = [sem(f"k_stored{i}") for i in range(2)], sem("v_stored")
        w_hi, w_lo, padded = sem("w_hi"), sem("w_lo"), sem("padded")
        w_loaded, w_stored = [sem(f"w_loaded{i}") for i in range(2)], [sem(f"w_stored{i}") for i in range(2)]
        block = c.enter_context(nc.Block())

        def tbank(n):
            return ps[:, TB + n % 2, :]

        def pbank(n):
            return ps[:, PB + n % 2, :]

        def rows(kt):
            return 128 if kt < KT0 - 1 else REST

        def t_at(b, *job):
            return b * TJ + tj[job] + 1

        def p_at(b, *job):
            return b * PJ + pj[job] + 1

        def t_hi_at(b, *job):
            return b * len(t_split) + t_split.index(job) + 1

        def p_hi_at(b, *job):
            return b * len(p_split) + p_split.index(job) + 1

        def piece(b, i):
            if i < 8:
                return Wq1[i // 2 * 128:(i // 2 + 1) * 128, bass.ds(b * 1024 + i % 2 * 512, 512)], wq_scr[bass.ds(b, 1), i]
            return Wo1[bass.ds(b * 1024 + (i - 8) * 128, 128), :], wo_scr[bass.ds(b, 1), i - 8]

        @block.sync
        def _(sp):
            def ffn_pieces(n):
                sp.wait_ge(f_summed, 2 * n + 2)
                sp.dma_start(fraw[:, 0, :], Wup[bass.ds(n * 128, 128), :]).then_inc(f_loaded, 16)
                sp.dma_start(fraw[:, 1, :], Wdn.rearrange("h (q n) -> (h q) n", n=512)[bass.ds(n * 128, 128), :]
                             ).then_inc(f_loaded, 16)

            def stores(b):
                for h in range(KVH):
                    sp.wait_ge(k_staged, b * KVH + h + 1)
                    sp.dma_start(k_scr[bass.ds(b, 1), h].rearrange("a p n -> p (a n)"),
                                 kst[:, h % 2].rearrange("p s n -> p (s n)")).then_inc(k_stored[h % 2], 16)
                    ffn_pieces(b * KVH + h)
                for k, (t0, t1) in enumerate(VPARTS):
                    sp.wait_ge(v_staged, b * 2 + k + 1)
                    for h in range(KVH):
                        sp.dma_start(v_scr[bass.ds(b, 1), h, :, t0 * 2 * HD:t1 * 2 * HD].rearrange("a p n -> p (a n)"),
                                     vst[:, h, t0:t1].rearrange("p t s n -> p (t s n)")).then_inc(v_stored, 16)

            sp.sem_inc(f_summed, 2)
            with sp.Fori(0, NB - 1) as b:
                sp.wait_ge(nat_lo, (b + 1) * KT0)
                load_context(sp, M, ctx4, b + 1)
                stores(b)
            stores(NB - 1)
            for s in k_stored:
                sp.wait_ge(s, 16 * (2 * NB + 1))
            sp.wait_ge(v_stored, 32 * KVH * (NB + 1))
            for s in w_stored:
                sp.wait_ge(s, 16 * (NP // 2 * NB + 1))

        @block.gpsimd
        def _(pool):
            nc.gpsimd.memset(kst[:, :, :, NC - 1:NCP], 0.0).then_inc(padded, 1)
            nc.gpsimd.memset(vst[:, :, KT0 - 1], 0.0).then_inc(padded, 1)

        @block.scalar
        def _(act):
            for s in k_stored:
                act.sem_inc(s, 16)
            act.sem_inc(v_stored, 32 * KVH)
            for s in w_stored:
                act.sem_inc(s, 16)
            act.wait_ge(padded, 2)

            def natural_hi(kt):
                nc.scalar.activation(nat[0:rows(kt), 0, kt, :], raw[0:rows(kt), kt, :], ACT.Copy,
                                     scale=SX).then_inc(nat_hi, 1)

            def load_piece(b, i):
                act.dma_start(wraw[:, i % 2, :], piece(b, i)[0]).then_inc(w_loaded[i % 2], 16)

            def store_piece(b, i):
                act.wait_ge(w_lo, b * NP + i + 1)
                act.dma_start(piece(b, i)[1].rearrange("a p n -> p (a n)"),
                              wspl[:, i % 2].rearrange("p s n -> p (s n)")).then_inc(w_stored[i % 2], 16)

            def weights_hi(b, i):
                if i:
                    store_piece(b, i - 1)
                if i + 1 < NP:
                    load_piece(b, i + 1)
                act.wait_ge(w_loaded[i % 2], 16 * (b * (NP // 2) + i // 2 + 1))
                act.wait_ge(w_stored[i % 2], 16 * (b * (NP // 2) + i // 2 + 1))
                nc.scalar.activation(wspl[:, i % 2, 0, :], wraw[:, i % 2, :], ACT.Copy, scale=SW).then_inc(w_hi, 1)

            def exps(b, q, some):
                if some[0] == 0:
                    act.wait_ge(bias_ready, b * QT + q + 1)
                for j in some:
                    o, w = CUT0[j]
                    nc.scalar.activation(prob[:, o:o + w], ps[:, j, 0:w], ACT.Exp, bias=mx[:, q, 6:7],
                                         scale=1.0 / (SQ * SX), accum_out=rs[:, q, j:j + 1]).then_inc(s_free, 1)

            def keys_hi(b, h, some=range(4)):
                if some[0] == 0:
                    act.wait_ge(k_stored[h % 2], 16 * (2 * b + h // 2 + 1))
                for j in some:
                    o, w = CUT0[j]
                    act.wait_ge(p_ready, p_at(b, "k", h, j))
                    nc.scalar.activation(kst[:, h % 2, 0, o:o + w], pbank(pj["k", h, j])[:, 0:w], ACT.Copy,
                                         scale=1.0 / SW).then_inc(p_hi, 1)

            def keys_and_exps(b, h, q):
                keys_hi(b, h, (0,))
                exps(b, q, (0, 1))
                keys_hi(b, h, (1,))
                exps(b, q, (2, 3))
                keys_hi(b, h, (2, 3))

            def probs_hi(b, q, groups=range(NG)):
                for g in groups:
                    t = min(4, KT0 - 4 * g)
                    r = rows(4 * g)
                    act.wait_ge(t_ready, t_at(b, "p", q, g))
                    nc.scalar.activation(pT[0:r, 0, 4 * g:4 * g + t, :],
                                         tbank(tj["p", q, g])[0:r, 0:t * 128].rearrange("p (t n) -> p t n", t=t),
                                         ACT.Copy, scale=SP_).then_inc(t_hi, 1)

            with act.Fori(0, NB) as b:
                load_piece(b, 0)
                act.wait_ge(ctx_loaded, (b + 1) * 32)
                natural_hi(0)
                for kt in range(KT0):
                    if kt + 1 < KT0:
                        natural_hi(kt + 1)
                    act.wait_ge(c_ready[1], b * KT0 + kt + 1)
                    nc.scalar.activation(ctT[:, 1, :, kt * 128:kt * 128 + rows(kt)],
                                         ps[:, 2 + kt % 2, 0:256].bitcast(fp16).rearrange("p (c n) -> p c n", c=DC)
                                         [:, :, 0:rows(kt)], ACT.Copy).then_inc(c_free[1], 1)
                for q in range(QT):
                    act.wait_ge(t_ready, t_at(b, "ln", q))
                    nc.scalar.activation(xT[:, 0, :, q * 128:(q + 1) * 128],
                                         tbank(tj["ln", q]).rearrange("p (c n) -> p c n", c=DC), ACT.Copy,
                                         scale=SX).then_inc(t_hi, 1)
                keys_hi(b, 0)
                for i in range(DC):
                    n = pj["q", i]
                    act.wait_ge(p_ready, p_at(b, "q", i))
                    nc.scalar.activation(q32[:, i, :], pbank(n)[:, 0:NTOK], ACT.Identity, bias=M["qb"][:, i:i + 1],
                                         scale=SQ / math.sqrt(D) / (SX * SW)).then_inc(p_free[n % 2], 1)
                for i in range(DC):
                    n = pj["q", i]
                    act.wait_ge(p_free[n % 2], b * (PJ // 2) + n // 2 + 2)
                    nc.scalar.activation(qT[:, 0, i, :], q32[:, i, :], ACT.Copy).then_inc(q_hi, 1)
                keys_hi(b, 1)
                weights_hi(b, 0)
                keys_and_exps(b, 2, 0)
                weights_hi(b, 1)
                probs_hi(b, 0)
                keys_and_exps(b, 3, 1)
                weights_hi(b, 2)
                act.wait_ge(v_stored, 32 * KVH * (b + 1))
                for kt in range(KT0):
                    act.wait_ge(p_ready, p_at(b, "v", kt))
                    nc.scalar.activation(vst[0:rows(kt), :, kt, 1, :],
                                         pbank(pj["v", kt])[0:rows(kt), :].rearrange("p (h n) -> p h n", h=KVH),
                                         ACT.Copy, scale=1.0 / SW).then_inc(p_hi, 1)
                    if kt < NG:
                        probs_hi(b, 1, (kt,))
                    weights_hi(b, kt + NP - KT0)
                store_piece(b, NP - 1)
                act.wait_ge(p_ready, p_at(b, "pv", 1))

        @block.vector
        def _(dve):
            def lo(dst, src, scale, hi, done):
                nc.vector.scalar_tensor_tensor(dst, src, scale, hi, ALU.mult, ALU.subtract).then_inc(done, 1)

            def bias(b, q, h, chain):
                dve.wait_ge(s_ready, b * QT + q + 1)
                for j, (o, w) in enumerate(CUT0):
                    last = nc.vector.reduce_max(mx[:, q, j:j + 1], ps[:, j, 0:w], AX.X)
                chain(last)
                keys_lo(b, h, (0,))
                chain(nc.vector.reduce_max(mx[:, q, 4:5], mx[:, q, 0:4], AX.X))
                chain(nc.vector.tensor_scalar(mx[:, q, 5:6], mx[:, q, 4:5], cc[:, q:q + 1], None, ALU.add))
                nc.vector.tensor_scalar(mx[:, q, 6:7], mx[:, q, 5:6], cc[:, q:q + 1], -1.0 / (SQ * SX),
                                        ALU.subtract, ALU.mult).then_inc(bias_ready, 1)

            def keys_lo(b, h, some=range(4)):
                for j in some:
                    o, w = CUT0[j]
                    n = pj["k", h, j]
                    dve.wait_ge(p_hi, p_hi_at(b, "k", h, j))
                    lo(kst[:, h % 2, 1, o:o + w], pbank(n)[:, 0:w], 1.0 / SW, kst[:, h % 2, 0, o:o + w], p_free[n % 2])
                if j == 3:
                    dve.wait_ge(p_free[n % 2], b * (PJ // 2) + n // 2 + 2)
                    dve.sem_inc(k_staged, 1)

            def probs_lo(b, q, groups=range(NG)):
                for g in groups:
                    t = min(4, KT0 - 4 * g)
                    n, r = tj["p", q, g], rows(4 * g)
                    dve.wait_ge(t_hi, t_hi_at(b, "p", q, g))
                    lo(pT[0:r, 1, 4 * g:4 * g + t, :].rearrange("p t n -> p (t n)"), tbank(n)[0:r, 0:t * 128], SP_,
                       pT[0:r, 0, 4 * g:4 * g + t, :].rearrange("p t n -> p (t n)"), t_free[n % 2])

            def weights_lo(b, i):
                dve.wait_ge(w_hi, b * NP + i + 1)
                lo(wspl[:, i % 2, 1, :], wraw[:, i % 2, :], SW, wspl[:, i % 2, 0, :], w_lo)

            def magnitudes(b, h):
                n = b * KVH + h
                dve.wait_ge(f_loaded, 32 * n + 32)
                for i in range(2):
                    nc.vector.tensor_scalar(fraw[:, i, :], fraw[:, i, :], 1.0, -1.0, ALU.min, ALU.max).then_inc(f_clamped, 1)
                for i in range(2):
                    dve.wait_ge(f_clamped, 2 * n + i + 1)
                    nc.vector.tensor_reduce(K["part"][:, i, bass.ds(n, 1)], fraw[:, i, :], AX.X, ALU.add,
                                            apply_absolute_value=True).then_inc(f_summed, 1)

            def row_sum(b, q, chain):
                dve.wait_ge(s_free, 4 * (b * QT + q + 1) + 4)
                chain(nc.vector.reduce_sum(mx[:, q, 7:8], rs[:, q, :], AX.X))
                chain(nc.vector.reciprocal(mx[:, q, 7:8], mx[:, q, 7:8]))
                chain(nc.vector.tensor_scalar(mx[:, q, 7:8], mx[:, q, 7:8], 1.0 / (SP_ * SX), None, ALU.mult))

            def attended(b, q):
                n = pj["pv", q]
                xs = K["x"][:, bass.ds(b * QT + q, 1), :].rearrange("p a d -> p (a d)")
                dve.wait_ge(p_ready, p_at(b, "pv", q))
                nc.vector.scalar_tensor_tensor(xs, pbank(n), mx[:, q, 7:8], xs, ALU.mult,
                                               ALU.add).then_inc(p_free[n % 2], 1)
                if q < QT - 1:
                    dve.wait_ge(p_free[n % 2], b * (PJ // 2) + n // 2 + 2)
                    row_moments(nc, K, b * QT + q)

            with dve.Fori(0, NB) as b:
                chain = Chain(dve, chain_s, b * CH)
                for q in range(QT):
                    nc.vector.tensor_scalar(xln[:, q, :],
                                            K["x"][:, bass.ds(b * QT + q, 1), :].rearrange("p a d -> p (a d)"),
                                            mv[:, bass.ds(b * QT + q, 1), 0:1].rearrange("p a c -> p (a c)"),
                                            yh[:, 2, bass.ds(b * QT + q, 1)], ALU.subtract,
                                            ALU.mult).then_inc(xln_ready, 1)
                for kt in range(KT0):
                    r = rows(kt)
                    dve.wait_ge(nat_hi, b * KT0 + kt + 1)
                    lo(nat[0:r, 1, kt, :], raw[0:r, kt, :], SX, nat[0:r, 0, kt, :], nat_lo)
                    dve.wait_ge(c_ready[0], b * KT0 + kt + 1)
                    nc.vector.tensor_copy(ctT[:, 0, :, kt * 128:kt * 128 + r],
                                          ps[:, kt % 2, 0:256].bitcast(fp16).rearrange("p (c n) -> p c n", c=DC)
                                          [:, :, 0:r]).then_inc(c_free[0], 1)
                for q in range(QT):
                    n = tj["ln", q]
                    dve.wait_ge(t_hi, t_hi_at(b, "ln", q))
                    lo(xT[:, 1, :, q * 128:(q + 1) * 128], tbank(n).rearrange("p (c n) -> p c n", c=DC), SX,
                       xT[:, 0, :, q * 128:(q + 1) * 128], t_free[n % 2])
                keys_lo(b, 0)
                for i in range(DC):
                    dve.wait_ge(q_hi, b * DC + i + 1)
                    nc.vector.tensor_tensor(qT[:, 1, i, :], q32[:, i, :], qT[:, 0, i, :],
                                            ALU.subtract).then_inc(q_lo, 1)
                n = pj["c", 0]
                dve.wait_ge(p_ready, p_at(b, "c", 0))
                nc.vector.tensor_scalar(cc[:, :], pbank(n)[:, 0:QT], SQ / math.sqrt(D) / SX, M["c0"][:, 0:1],
                                        ALU.mult, ALU.add).then_inc(p_free[n % 2], 1)
                keys_lo(b, 1)
                weights_lo(b, 0)
                bias(b, 0, 2, chain)
                keys_lo(b, 2, (1, 2, 3))
                weights_lo(b, 1)
                magnitudes(b, 0)
                probs_lo(b, 0)
                row_sum(b, 0, chain)
                bias(b, 1, 3, chain)
                keys_lo(b, 3, (1, 2, 3))
                weights_lo(b, 2)
                magnitudes(b, 1)
                attended(b, 0)
                for kt in range(KT0):
                    n, r = pj["v", kt], rows(kt)
                    dve.wait_ge(p_hi, p_hi_at(b, "v", kt))
                    lo(vst[0:r, :, kt, 0, :], pbank(n)[0:r, :].rearrange("p (h n) -> p h n", h=KVH), 1.0 / SW,
                       vst[0:r, :, kt, 1, :], p_free[n % 2])
                    if kt < NG:
                        probs_lo(b, 1, (kt,))
                    weights_lo(b, kt + NP - KT0)
                    if kt == VPARTS[0][1]:
                        m = pj["v", kt - 1]
                        dve.wait_ge(p_free[m % 2], b * (PJ // 2) + m // 2 + 2)
                        dve.sem_inc(v_staged, 1)
                    if kt in (5, 9):
                        magnitudes(b, 2 + kt // 9)
                row_sum(b, 1, chain)
                n = pj["v", KT0 - 1]
                dve.wait_ge(p_free[n % 2], b * (PJ // 2) + n // 2 + 2)
                dve.sem_inc(v_staged, 1)
                attended(b, 1)
                assert chain.n == CH, chain.n

        @block.tensor
        def _(pe):
            for s in t_free + p_free:
                pe.sem_inc(s, 1)
            for s in c_free:
                pe.sem_inc(s, 2)
            pe.sem_inc(s_free, 4)

            def take(b, ring, free, per, n):
                pe.wait_ge(free[n % 2], b * (per // 2) + n // 2 + 1)
                return ring(n)

            def t_take(b, *job):
                return take(b, tbank, t_free, TJ, tj[job])

            def p_take(b, *job):
                return take(b, pbank, p_free, PJ, pj[job])

            def scores(b, q, some=range(4)):
                for j in some:
                    o, w = CUT0[j]
                    pe.wait_ge(s_free, 4 * (b * QT + q) + j + 1)
                    for i in range(DC):
                        last = mm3(nc, ps[:, j, 0:w], [qT[:, s, i, q * 128:(q + 1) * 128] for s in range(2)],
                                   [ctT[:, s, i, o:o + w] for s in range(2)], i == 0, i == DC - 1)
                if j == 3:
                    last.then_inc(s_ready, 1)

            def keys(b, h):
                for j, (o, w) in enumerate(CUT0):
                    out = p_take(b, "k", h, j)
                    for i in range(DC):
                        last = mm3(nc, out[:, 0:w], [K["wk"][:, s, i, h * 128:(h + 1) * 128] for s in range(2)],
                                   [ctT[:, s, i, o:o + w] for s in range(2)], i == 0, i == DC - 1)
                    last.then_inc(p_ready, 1)

            def turn(b, q, groups):
                for g in groups:
                    if g == 0:
                        pe.wait_ge(s_free, 4 * (b * QT + q + 1) + 4)
                    out = t_take(b, "p", q, g)
                    for kt in range(4 * g, min(4 * g + 4, KT0)):
                        o = (kt - 4 * g) * 128
                        last = nc.tensor.transpose(out[0:rows(kt), o:o + 128], prob[:, kt * 128:kt * 128 + rows(kt)],
                                                   K["id32"][:, :])
                    last.then_inc(t_ready, 1)

            def attend(b, q):
                out = p_take(b, "pv", q)
                n = tj["p", q, NG - 1]
                pe.wait_ge(t_free[n % 2], b * (TJ // 2) + n // 2 + 2)
                n = tj["p", q, NG - 2]
                pe.wait_ge(t_free[n % 2], b * (TJ // 2) + n // 2 + 2)
                for kt in range(KT0):
                    r = rows(kt)
                    last = mm3(nc, out, [pT[0:r, s, kt, :] for s in range(2)], [nat[0:r, s, kt, :] for s in range(2)],
                               kt == 0, kt == KT0 - 1)
                last.then_inc(p_ready, 1)

            with pe.Fori(0, NB) as b:
                for q in range(QT):
                    pe.wait_ge(xln_ready, b * QT + q + 1)
                    out = t_take(b, "ln", q)
                    for i in range(DC):
                        last = nc.tensor.transpose(out[:, i * 128:(i + 1) * 128], xln[:, q, i * 128:(i + 1) * 128],
                                                   K["id32"][:, :])
                    last.then_inc(t_ready, 1)
                pe.wait_ge(s_free, 4 * b * QT + 4)
                for kt in range(KT0):
                    r = rows(kt)
                    for s, sm in enumerate((nat_hi, nat_lo)):
                        pe.wait_ge(sm, b * KT0 + kt + 1)
                        pe.wait_ge(c_free[s], b * KT0 + kt + 1)
                        out = ps[:, 2 * s + kt % 2, 0:256].bitcast(fp16)
                        for i in range(DC):
                            last = nc.tensor.transpose(out[:, i * 128:i * 128 + r], nat[0:r, s, kt, i * 128:(i + 1) * 128],
                                                       K["id16"][0:r, 0:r])
                        last.then_inc(c_ready[s], 1)
                for s in range(2):
                    pe.wait_ge(c_free[s], b * KT0 + KT0 + 2)
                keys(b, 0)
                for q in range(QT):
                    n = tj["ln", q]
                    pe.wait_ge(t_free[n % 2], b * (TJ // 2) + n // 2 + 2)
                for i in range(DC):
                    out = p_take(b, "q", i)
                    for j in range(DC):
                        last = mm3(nc, out[:, 0:NTOK], [M["m"][:, s, j, i * 128:(i + 1) * 128] for s in range(2)],
                                   [xT[:, s, j, :] for s in range(2)], j == 0, j == DC - 1)
                    last.then_inc(p_ready, 1)
                out = p_take(b, "c", 0)
                for q in range(QT):
                    for j in range(DC):
                        last = mm3(nc, out[:, q:q + 1], [xT[:, s, j, q * 128:(q + 1) * 128] for s in range(2)],
                                   [M["wb"][:, s, j:j + 1] for s in range(2)], j == 0, j == DC - 1)
                last.then_inc(p_ready, 1)
                keys(b, 1)
                pe.wait_ge(q_lo, (b + 1) * DC)
                scores(b, 0)
                keys(b, 2)
                for j in range(4):
                    scores(b, 1, (j,))
                    turn(b, 0, (j,))
                keys(b, 3)
                attend(b, 0)
                for kt in range(KT0):
                    r = rows(kt)
                    out = p_take(b, "v", kt)
                    for i in range(DC):
                        last = mm3(nc, out[0:r, :], [ctT[:, s, i, kt * 128:kt * 128 + r] for s in range(2)],
                                   [K["wv"][:, s, i, :] for s in range(2)], i == 0, i == DC - 1)
                    last.then_inc(p_ready, 1)
                    if kt < NG:
                        turn(b, 1, (kt,))
                attend(b, 1)


def ffn0(nc, ps, K, Wup, Wdn):
    with ExitStack() as c:
        def sb(name, shape, dt):
            return c.enter_context(nc.sbuf_tensor(name, shape, dt))

        def sem(name):
            return c.enter_context(nc.semaphore("f_" + name))

        upT = sb("up_T", [128, DC, F], bf16)
        dnT = sb("down_T", [128, FC, D], bf16)
        id_b = sb("id_b", [128, 128], bf16)
        ones = sb("ones", [128, 128], fp32)
        tot = sb("tot", [128, 2, 6], fp32)
        stats = stats_tiles(sb, "f")
        mv, ve, yh = stats
        var_ready, pow_ready, stats_s = sem("var_ready"), sem("pow_ready"), sem("stats")
        with ExitStack() as w:
            NWT = F * D // 128 // 2048
            raw = w.enter_context(nc.sbuf_tensor("ffn_raw", [128, 2, NWT, 2048], fp32))
            gt = w.enter_context(nc.sbuf_tensor("ffn_gt", [128, 2, 2048], bf16))
            tern = w.enter_context(nc.sbuf_tensor("ffn_tern", [128, 2, NWT, 2048], bf16))

            def semw(name):
                return w.enter_context(nc.semaphore("fw_" + name))

            loaded = [[semw(f"loaded{i}_{t}") for t in range(NWT)] for i in range(2)]
            ones_s, sum_s, tot_s, tern_s, tr_s, ev_s, ch_s, idb_s = (
                semw(n) for n in ("ones", "sum", "tot", "tern", "tr", "ev", "ch", "idb"))
            block = w.enter_context(nc.Block())

            @block.sync
            def _(sp):
                for t in range(NWT):
                    sp.dma_start(raw[:, 0, t, :].rearrange("p (a n) -> p a n", a=4),
                                 Wup[t * 512:(t + 1) * 512, :].rearrange("(a p) n -> p a n", p=128)
                                 ).then_inc(loaded[0][t], 16)
                for t in range(NWT):
                    sp.dma_start(raw[:, 1, t, :], Wdn[t * 128:(t + 1) * 128, :]).then_inc(loaded[1][t], 16)

            @block.gpsimd
            def _(pool):
                nc.gpsimd.memset(ones[:, :], 1.0).then_inc(ones_s, 1)
                nc.gpsimd.tensor_copy(id_b[:, :], K["id16"][:, :]).then_inc(idb_s, 1)
                pool.wait_ge(var_ready, 1)
                nc.gpsimd.tensor_tensor(yh[:, 0, :], ve[:, :], K["mhalf"][:, :], ALU.pow).then_inc(pow_ready, 1)

            @block.vector
            def _(dve):
                chain = Chain(dve, ch_s)
                for i in range(2):
                    nc.vector.reduce_sum(tot[:, i, 0:1], K["part"][:, i, :], AX.X).then_inc(sum_s, 1)
                layer_norm_stats(nc, dve, Chain(dve, stats_s), K, stats, var_ready, pow_ready,
                                 range(QT - 1, NT, QT))
                for i in range(2):
                    dve.wait_ge(tot_s, i + 1)
                    chain(nc.vector.tensor_scalar(tot[:, i, 1:2], ps[:, 6 + i, 0:1], 1.0 / (F * D), EPS, ALU.mult, ALU.add))
                    nc.vector.tensor_scalar(tot[:, i, 2:3], tot[:, i, 1:2], 0.5, None, ALU.mult)
                    chain(nc.vector.tensor_scalar(tot[:, i, 3:4], tot[:, i, 1:2], -0.5, None, ALU.mult))
                    for t in range(NWT):
                        dve.wait_ge(loaded[i][t], 16)
                        chain(nc.vector.tensor_scalar(gt[:, t % 2, :], raw[:, i, t, :], tot[:, i, 2:3], None, ALU.is_gt))
                        nc.vector.scalar_tensor_tensor(tern[:, i, t, :], raw[:, i, t, :], tot[:, i, 3:4], gt[:, t % 2, :],
                                                       ALU.is_lt, ALU.subtract).then_inc(tern_s, 1)

            @block.tensor
            def _(pe):
                pe.wait_ge(ones_s, 1)
                for i in range(2):
                    pe.wait_ge(sum_s, i + 1)
                    nc.tensor.matmul(ps[:, 6 + i, 0:1], ones[:, :], tot[:, i, 0:1], start=True, stop=True).then_inc(tot_s, 1)
                pe.wait_ge(idb_s, 1)
                n = 0
                for t in range(NWT):
                    pe.wait_ge(tern_s, t + 1)
                    for i in range(DC):
                        if n >= 4:
                            pe.wait_ge(ev_s, n - 3)
                        for a in range(4):
                            last = nc.tensor.transpose(ps[:, n % 4, 0:256].bitcast(bf16)[:, a * 128:(a + 1) * 128],
                                                       tern[:, 0, t, a * 512 + i * 128:a * 512 + (i + 1) * 128], id_b[:, :])
                        last.then_inc(tr_s, 1)
                        n += 1
                for t in range(NWT):
                    pe.wait_ge(tern_s, NWT + t + 1)
                    for i in range(FC // 4):
                        pe.wait_ge(ev_s, n - 3)
                        for a in range(4):
                            f = 4 * i + a
                            last = nc.tensor.transpose(ps[:, n % 4, 0:256].bitcast(bf16)[:, a * 128:(a + 1) * 128],
                                                       tern[:, 1, t, f * 128:(f + 1) * 128], id_b[:, :])
                        last.then_inc(tr_s, 1)
                        n += 1

            @block.scalar
            def _(act):
                n = 0
                for t in range(NWT):
                    for i in range(DC):
                        act.wait_ge(tr_s, n + 1)
                        nc.scalar.activation(upT[:, i, t * 512:(t + 1) * 512], ps[:, n % 4, 0:256].bitcast(bf16),
                                             ACT.Copy, scale=-1.0).then_inc(ev_s, 1)
                        n += 1
                for t in range(NWT):
                    for i in range(FC // 4):
                        act.wait_ge(tr_s, n + 1)
                        nc.scalar.activation(dnT[:, 4 * i:4 * i + 4, t * 128:(t + 1) * 128],
                                             ps[:, n % 4, 0:256].bitcast(bf16).rearrange("p (f n) -> p f n", f=4),
                                             ACT.Copy, scale=-1.0).then_inc(ev_s, 1)
                        n += 1

        hr = sb("h_relu", [128, QT, F], fp32)
        hq = sb("h32", [128, F], fp32)
        hb = sb("h_int", [128, QT, F], bf16)
        hT = sb("h_intT", [128, FC, 128], bf16)
        xln = sb("xlnf", [128, QT, D], fp32)
        xq = sb("xq", [128, QT, D], bf16)
        xqT = sb("xqT", [128, QT, DC, 128], bf16)
        sx = sb("sxf", [128, QT, 3], fp32)
        unit = sb("unit", [128, QT], fp32)
        sh = sb("shf", [128, QT, 4], fp32)
        (chain_s, xq_ready, xt_ready, xt_done, up_ready, relu_done,
         hb_ready, ht_ready, ht_done, dn_ready, dn_done, unit_ready) = (sem(n) for n in (
             "chain", "xq_ready", "xt_ready", "xt_done", "up_ready", "relu_done",
             "hb_ready", "ht_ready", "ht_done", "dn_ready", "dn_done", "unit_ready"))
        CHX, CHH = 1 + QT * 5, 5
        CHF = CHX + QT * CHH
        block = c.enter_context(nc.Block())

        @block.tensor
        def _(pe):
            pe.sem_inc(xt_done, 1)
            pe.sem_inc(dn_done, 1)
            pe.sem_inc(ht_done, 2)
            pe.sem_inc(relu_done, 4)

            def turn_tokens(n, q):
                pe.wait_ge(xq_ready, n + 1)
                pe.wait_ge(xt_done, n + 1)
                for i in range(DC):
                    last = nc.tensor.transpose(ps[:, 6, 0:256].bitcast(bf16)[:, i * 128:(i + 1) * 128],
                                               xq[:, q, i * 128:(i + 1) * 128], id_b[:, :])
                last.then_inc(xt_ready, 1)

            def up(n, q):
                pe.wait_ge(xt_done, n + 2)
                for j in range(4):
                    pe.wait_ge(relu_done, 4 * n + j + 1)
                    for i in range(DC):
                        last = nc.tensor.matmul(ps[:, j, :], xqT[:, q, i, :], upT[:, i, j * 512:(j + 1) * 512],
                                                start=(i == 0), stop=(i == DC - 1))
                    last.then_inc(up_ready, 1)

            def down(n, q):
                pe.wait_ge(hb_ready, n + 1)
                for g in range(4):
                    pe.wait_ge(ht_done, 4 * n + g + 1)
                    for a in range(4):
                        t = 4 * g + a
                        last = nc.tensor.transpose(ps[:, 4 + g % 2, 0:256].bitcast(bf16)[:, a * 128:(a + 1) * 128],
                                                   hb[:, q, t * 128:(t + 1) * 128], id_b[:, :])
                    last.then_inc(ht_ready, 1)
                pe.wait_ge(dn_done, n + 1)
                pe.wait_ge(ht_done, 4 * n + 4 + 2)
                for t in range(FC):
                    last = nc.tensor.matmul(ps[:, 7, :], hT[:, t, :], dnT[:, t, :], start=(t == 0), stop=(t == FC - 1))
                last.then_inc(dn_ready, 1)

            def body(b, more):
                up(b * QT + 1, 1)
                down(b * QT, 0)
                if more:
                    turn_tokens(b * QT + 2, 0)
                    turn_tokens(b * QT + 3, 1)
                    up(b * QT + 2, 0)
                down(b * QT + 1, 1)

            turn_tokens(0, 0)
            turn_tokens(1, 1)
            up(0, 0)
            with pe.Fori(0, NB - 1) as b:
                body(b, True)
            body(NB - 1, False)

        @block.scalar
        def _(act):
            def tokens(n, q):
                act.wait_ge(xt_ready, n + 1)
                nc.scalar.activation(xqT[:, q].rearrange("p c n -> p (c n)"), ps[:, 6, 0:256].bitcast(bf16),
                                     ACT.Copy).then_inc(xt_done, 1)

            def relu(n, q):
                act.wait_ge(unit_ready, n + 1)
                for j in range(4):
                    act.wait_ge(up_ready, 4 * n + j + 1)
                    nc.scalar.activation(hr[:, q, j * 512:(j + 1) * 512], ps[:, j, :], ACT.Relu,
                                         scale=unit[:, q:q + 1]).then_inc(relu_done, 1)

            def hidden(n):
                for g in range(4):
                    act.wait_ge(ht_ready, 4 * n + g + 1)
                    nc.scalar.activation(hT[:, 4 * g:4 * g + 4, :].rearrange("p t n -> p (t n)"),
                                         ps[:, 4 + g % 2, 0:256].bitcast(bf16), ACT.Copy).then_inc(ht_done, 1)

            def body(b, more):
                relu(b * QT + 1, 1)
                hidden(b * QT)
                if more:
                    tokens(b * QT + 2, 0)
                    tokens(b * QT + 3, 1)
                    relu(b * QT + 2, 0)
                hidden(b * QT + 1)

            tokens(0, 0)
            tokens(1, 1)
            relu(0, 0)
            with act.Fori(0, NB - 1) as b:
                body(b, True)
            body(NB - 1, False)

        @block.vector
        def _(dve):
            def xs(n):
                return K["x"][:, n, :] if isinstance(n, int) else K["x"][:, bass.ds(n, 1), :].rearrange("p a d -> p (a d)")

            def unit_of(q):
                nc.vector.tensor_scalar(unit[:, q:q + 1], sx[:, q, 0:1], tot[:, 0, 1:2], 1.0 / 127.0, ALU.mult,
                                        ALU.mult).then_inc(unit_ready, 1)

            def quantised_tokens(b, chain):
                for q in range(QT):
                    n = b * QT + q
                    last = nc.vector.tensor_scalar(xln[:, q, :], xs(n),
                                                   mv[:, bass.ds(n, 1), 0:1].rearrange("p a c -> p (a c)"),
                                                   yh[:, 2, bass.ds(n, 1)], ALU.subtract, ALU.mult)
                chain(last)
                for q in range(QT):
                    chain(nc.vector.tensor_reduce(sx[:, q, 0:1], xln[:, q, :], AX.X, ALU.max, apply_absolute_value=True))
                    chain(nc.vector.tensor_scalar(sx[:, q, 0:1], sx[:, q, 0:1], EPS, None, ALU.max))
                    chain(nc.vector.reciprocal(sx[:, q, 1:2], sx[:, q, 0:1]))
                    chain(nc.vector.tensor_scalar(sx[:, q, 1:2], sx[:, q, 1:2], 127.0, None, ALU.mult))
                    if q == 0:
                        unit_of(0)
                    chain(nc.vector.tensor_scalar(xln[:, q, :], xln[:, q, :], sx[:, q, 1:2], MAGIC, ALU.mult, ALU.add))
                    nc.vector.tensor_scalar(xq[:, q, :], xln[:, q, :], MAGIC, 127.0, ALU.subtract,
                                            ALU.min).then_inc(xq_ready, 1)

            def quantised_hidden(n, q, chain, first=False):
                if not first:
                    dve.wait_ge(hb_ready, n)
                dve.wait_ge(relu_done, 4 * n + 4 + 4)
                nc.vector.memset(sh[:, q, 3:4], EPS)
                chain(nc.vector.tensor_tensor_reduce(out=hq[:, :], in0=hr[:, q, :], in1=hr[:, q, :], scale=1.0, scalar=0.0,
                                                     op0=ALU.mult, op1=ALU.max, accum_out=sh[:, q, 0:1]))
                chain(nc.vector.tensor_scalar(sh[:, q, 0:1], sh[:, q, 0:1], sh[:, q, 3:4], None, ALU.max))
                chain(nc.vector.reciprocal(sh[:, q, 1:2], sh[:, q, 0:1]))
                chain(nc.vector.tensor_scalar(sh[:, q, 1:2], sh[:, q, 1:2], 127.0, None, ALU.mult))
                nc.vector.tensor_scalar(sh[:, q, 2:3], sh[:, q, 0:1], tot[:, 1, 1:2], 1.0 / 127.0, ALU.mult, ALU.mult)
                chain(nc.vector.tensor_scalar(hq[:, :], hq[:, :], sh[:, q, 1:2], MAGIC, ALU.mult, ALU.add))
                nc.vector.tensor_scalar(hb[:, q, :], hq[:, :], MAGIC, 127.0, ALU.subtract, ALU.min).then_inc(hb_ready, 1)

            def result(n, q):
                dve.wait_ge(dn_ready, n + 1)
                nc.vector.scalar_tensor_tensor(xs(n), ps[:, 7, :], sh[:, q, 2:3], xs(n), ALU.mult,
                                               ALU.add).then_inc(dn_done, 1)

            def body(b, more):
                chain = Chain(dve, chain_s, b * CHF + CHX + CHH)
                if more:
                    quantised_tokens(b + 1, chain)
                quantised_hidden(b * QT + 1, 1, chain)
                if more:
                    unit_of(1)
                result(b * QT, 0)
                if more:
                    quantised_hidden(b * QT + 2, 0, chain)
                result(b * QT + 1, 1)
                assert chain.n == (CHF if more else CHH), chain.n

            chain = Chain(dve, chain_s)
            quantised_tokens(0, chain)
            unit_of(1)
            quantised_hidden(0, 0, chain, first=True)
            with dve.Fori(0, NB - 1) as b:
                body(b, True)
            body(NB - 1, False)


def attention1(nc, ps, K, k_scr, v_scr, wq_scr, wo_scr):
    NKA = KT1 * 128
    LAST = NK - (KT1 - 1) * 128
    CHK = [(k, min(4, KT1 - k)) for k in range(0, KT1, 4)]
    NCK = len(CHK)
    NU = KVH * NB
    PAIR = [(k, min(2, KT1 - k)) for k in range(0, KT1, 2)]
    NP = len(PAIR)
    OB, WB = 4, 6
    VW = 2 * HD + 2
    OW = HD + 2
    with ExitStack() as c:
        def sb(name, shape, dt):
            return c.enter_context(nc.sbuf_tensor(name, shape, dt))

        def sem(name):
            return c.enter_context(nc.semaphore("c_" + name))

        xT = sb("xT1", [128, 2, DC, NB * NTOK], fp16)
        wq = sb("wq_s", [128, DC, 2, 2, 512], fp16)
        wo = sb("wo_s", [128, GRP, 2, 512], fp16)
        kb = sb("keys", [128, 2, 2, NKA], fp16)
        vb = sb("values", [128, 2, KT1, VW], fp16)
        wq_loaded, wo_loaded = sem("wq_loaded"), sem("wo_loaded")
        k_loaded, v_loaded = [sem(f"k_loaded{e}") for e in range(2)], [sem(f"v_loaded{e}") for e in range(2)]

        def load_wq(sp, kv):
            sp.dma_start(wq[:, :, :, :, :].rearrange("p i c s n -> p (i c) (s n)"),
                         wq_scr[bass.ds(kv, 1)].rearrange("a i p n -> p (a i) n")).then_inc(wq_loaded, 16)

        def load_wo(sp, kv):
            sp.dma_start(wo[:, :, :, :].rearrange("p i s n -> p i (s n)"),
                         wo_scr[bass.ds(kv, 1)].rearrange("a i p n -> p (a i) n")).then_inc(wo_loaded, 16)

        def load_keys(sp, kv, b):
            sp.dma_start(kb[:, b % 2, :, NTOK:NKP],
                         k_scr[b, bass.ds(kv, 1)].rearrange("h p (s n) -> p (h s) n", s=2)
                         ).then_inc(k_loaded[b % 2], 16)

        def load_values(sp, kv, b):
            sp.dma_start(vb[:, b % 2, QT:KT1, 0:2 * HD], v_scr[b, bass.ds(kv, 1)].rearrange(
                "h p (t n) -> p (h t) n", t=KT0)).then_inc(v_loaded[b % 2], 16)

        def first_loads(sp):
            load_wq(sp, 0)
            load_keys(sp, 0, 0)
            load_values(sp, 0, 0)
            load_wo(sp, 0)

        layer_norm_turned(nc, ps, K, xT, SX, "c", first_loads)

        qT = sb("qT1", [128, 2, 2, NTOK], fp16)
        s32 = sb("scores", [128, 2, KT1, NTOK], fp32)
        pT = sb("probT1", [128, 2, 2, KT1, NTOK], fp16)
        acc = sb("acc", [128, 4, NTOK], fp32)
        rm = sb("row_max", [128, NTOK], fp32)
        mcol = sb("max_col", [128, QT], fp32)
        mrow = sb("max_row", [128, NTOK], fp32)
        rs = sb("rs1", [128, QT], fp32)
        o32 = sb("o32", [128, QT, HD], fp32)
        oT = sb("oT", [128, 2, 2, NTOK], fp16)
        lnp = sb("ln_p", [128, 1], fp32)

        s_ready, s_copied, sub_done, e_done, h_done, lo_done = (
            sem(n) for n in ("s_ready", "s_copied", "sub_done", "e_done", "h_done", "lo_done"))
        q_ready, q_hi, q_lo, rm_ready, mt_ready, mc_ready, mb_ready, mb_done = (
            sem(n) for n in ("q_ready", "q_hi", "q_lo", "rm_ready", "mt_ready", "mc_ready", "mb_ready", "mb_done"))
        pv_done, o_done, ot_ready, ot_hi, ot_lo, chain_s = (
            sem(n) for n in ("pv_done", "o_done", "ot_ready", "ot_hi", "ot_lo", "chain"))
        l_ready, l_hi, l_lo, wo_ready, wo_taken, consts = (
            sem(n) for n in ("l_ready", "l_hi", "l_lo", "wo_ready", "wo_taken", "consts"))
        block = c.enter_context(nc.Block())
        small = [ps[:, 3, 0:NTOK], ps[:, 5, 0:NTOK]]

        def scores_of(j):
            return ps[:, j % 3, 0:PAIR[j][1] * NTOK]

        def tiles(t, k, n):
            return t[:, k:k + n, :].rearrange("p t n -> p (t n)")

        def chunk(t, g):
            return tiles(t, *CHK[g])

        def units(eng, first, rest):
            first()
            with eng.Fori(0, NU // 2 - 1) as i:
                for e in range(2):
                    rest(i * 2 + e, e, True)
            rest(NU - 2, 0, True)
            rest(NU - 1, 1, False)

        @block.sync
        def _(sp):
            def keys_and_values(u, kv, b):
                sp.wait_ge(s_ready, u * (GRP * NP) + 1)
                load_keys(sp, kv, b)
                sp.wait_ge(pv_done, u * GRP + 2)
                load_values(sp, kv, b)

            with sp.Fori(0, KVH - 1) as kv:
                for b in range(NB - 1):
                    keys_and_values(kv * NB + b, kv, b + 1)
                u = kv * NB + (NB - 1)
                keys_and_values(u, kv + 1, 0)
                sp.wait_ge(q_ready, (u + 1) * GRP)
                load_wq(sp, kv + 1)
                sp.wait_ge(wo_ready, (u + 1) * QT)
                load_wo(sp, kv + 1)
            for b in range(NB - 1):
                keys_and_values((KVH - 1) * NB + b, KVH - 1, b + 1)

        @block.gpsimd
        def _(pool):
            nc.gpsimd.memset(kb[:, :, :, NKP:NKA], 0.0).then_inc(consts, 1)
            nc.gpsimd.memset(vb[:, :, :, 2 * HD:VW], 1.0).then_inc(consts, 1)
            nc.gpsimd.memset(lnp[:, :], math.log(SP_)).then_inc(consts, 1)
            with pool.Fori(0, NU) as u:
                for h in range(GRP):
                    for g in range(NCK):
                        pool.wait_ge(h_done, (u * GRP + h) * NCK + g + 1)
                        nc.gpsimd.tensor_tensor(chunk(pT[:, h % 2, 1], g), chunk(s32[:, h % 2], g),
                                                chunk(pT[:, h % 2, 0], g), ALU.subtract).then_inc(lo_done, 1)

        @block.scalar
        def _(act):
            def query(G, h):
                act.wait_ge(q_ready, G + 1)
                nc.scalar.activation(qT[:, h % 2, 0, :], small[1], ACT.Copy,
                                     scale=SQ / math.sqrt(HD) / (SX * SW)).then_inc(q_hi, 1)

            def latent_keys(u, e):
                act.wait_ge(l_ready, 2 * u + 1)
                nc.scalar.activation(kb[:, e, 0, 0:NTOK], small[0], ACT.Copy,
                                     scale=1.0 / SW).then_inc(l_hi, 1)

            def latent_values(u, e):
                act.wait_ge(l_ready, 2 * u + 2)
                nc.scalar.activation(vb[:, e, 0:QT, HD:2 * HD], small[0].rearrange("p (t n) -> p t n", t=QT), ACT.Copy,
                                     scale=1.0 / SW).then_inc(l_hi, 1)

            def copy(G, h, g):
                for j in (2 * g, 2 * g + 1):
                    act.wait_ge(s_ready, G * NP + j + 2)
                    if j % 2 == 0:
                        act.wait_ge(lo_done, G * NCK + g + 1)
                    nc.scalar.activation(tiles(s32[:, h % 2], *PAIR[j]), scores_of(j), ACT.Copy).then_inc(s_copied, 1)

            def exp(G, h, g):
                act.wait_ge(sub_done, G * NCK + g + 1)
                nc.scalar.activation(chunk(s32[:, h % 2], g), chunk(s32[:, h % 2], g), ACT.Exp, bias=lnp[:, 0:1],
                                     scale=1.0 / (SQ * SX)).then_inc(e_done, 1)

            def hi(G, h, g):
                act.wait_ge(e_done, G * NCK + g + 1)
                if g == 0:
                    act.wait_ge(pv_done, G + 1)
                nc.scalar.activation(chunk(pT[:, h % 2, 0], g), chunk(s32[:, h % 2], g), ACT.Copy).then_inc(h_done, 1)

            def turned_out(G, h):
                act.wait_ge(ot_ready, G + 1)
                nc.scalar.activation(oT[:, h % 2, 0, :], small[0], ACT.Copy).then_inc(ot_hi, 1)

            def maxima(G):
                act.wait_ge(mb_ready, G + 1)
                nc.scalar.activation(mrow[:, :], small[1], ACT.Copy).then_inc(mb_done, 1)

            def step(u, e, h, lags, more):
                G = u * GRP + h
                copy(G, h, 0)
                if lags >= 1:
                    maxima(G - 1)
                if lags >= 2:
                    hi(G - 2, h - 2, 3)
                if lags >= 1:
                    exp(G - 1, h - 1, 0)
                copy(G, h, 1)
                if lags >= 1:
                    exp(G - 1, h - 1, 1)
                    hi(G - 1, h - 1, 0)
                copy(G, h, 2)
                if h == GRP - 2 and more:
                    latent_keys(u + 1, 1 - e)
                if h == GRP - 1 and more:
                    latent_values(u + 1, 1 - e)
                if lags >= 1:
                    exp(G - 1, h - 1, 2)
                copy(G, h, 3)
                if lags >= 1:
                    hi(G - 1, h - 1, 1)
                    exp(G - 1, h - 1, 3)
                    hi(G - 1, h - 1, 2)
                if lags >= 2:
                    turned_out(G - 2, h - 2)
                if h < GRP - 2 or more:
                    query(G + 2, h)

            def finish(G, h):
                hi(G - 1, h - 1, 3)
                maxima(G)
                for g in range(NCK):
                    exp(G, h, g)
                    hi(G, h, g)
                turned_out(G - 1, h - 1)
                turned_out(G, h)

            def first():
                act.wait_ge(consts, 3)
                latent_keys(0, 0)
                query(0, 0)
                latent_values(0, 0)
                query(1, 1)
                for h in range(3):
                    step(0, 0, h, h, True)

            def rest(u, e, more):
                for h in range(3, GRP):
                    step(u, e, h, 3, more)
                for h in range(3 if more else 0):
                    step(u + 1, 1 - e, h, 3, True)

            units(act, first, rest)
            finish(NU * GRP - 1, GRP - 1)

        @block.vector
        def _(dve):
            CHN = 3 + 1

            def low(dst, src, scale, hi, wait, n, done):
                dve.wait_ge(wait, n)
                nc.vector.scalar_tensor_tensor(dst, src, scale, hi, ALU.mult, ALU.subtract).then_inc(done, 1)

            def query(G, h):
                low(qT[:, h % 2, 1, :], small[1], SQ / math.sqrt(HD) / (SX * SW), qT[:, h % 2, 0, :], q_hi, G + 1, q_lo)

            def latent_keys(u, e):
                low(kb[:, e, 1, 0:NTOK], small[0], 1.0 / SW, kb[:, e, 0, 0:NTOK], l_hi, 2 * u + 1, l_lo)

            def latent_values(u, e):
                low(vb[:, e, 0:QT, 0:HD], small[0].rearrange("p (t n) -> p t n", t=QT), 1.0 / SW, vb[:, e, 0:QT, HD:2 * HD],
                    l_hi, 2 * u + 2, l_lo)

            def turned_out(G, h):
                low(oT[:, h % 2, 1, :], small[0], 1.0, oT[:, h % 2, 0, :], ot_hi, G + 1, ot_lo)

            flat = acc[:, :, :].rearrange("p t n -> p (t n)")

            def largest(G, h, g, chain):
                sc = s32[:, h % 2]
                dve.wait_ge(s_copied, G * NP + 2 * g + 4)
                if g < NCK - 1:
                    chain(nc.vector.tensor_tensor(flat, chunk(sc, 0) if g == 1 else flat, chunk(sc, g), ALU.max))
                else:
                    nc.vector.tensor_tensor(acc[:, 0:2, :], acc[:, 0:2, :], sc[:, KT1 - 3:KT1 - 1, :], ALU.max)
                    chain(nc.vector.tensor_tensor(acc[0:LAST, 2, :], acc[0:LAST, 2, :], sc[0:LAST, KT1 - 1, :], ALU.max))

            def partition_maxima():
                nc.vector.tensor_reduce(rm[:, :], acc[:, :, :].rearrange("p t n -> p n t"), AX.X,
                                        ALU.max).then_inc(rm_ready, 1)

            def maxima(G):
                dve.wait_ge(mt_ready, G + 1)
                nc.vector.tensor_reduce(mcol[:, :], small[0].rearrange("p (q n) -> p q n", q=QT), AX.X,
                                        ALU.max).then_inc(mc_ready, 1)

            def sub(G, h, g):
                t = s32[:, h % 2, CHK[g][0]:CHK[g][0] + CHK[g][1], :]
                m = mrow[:, :].rearrange("p (a n) -> p a n", a=1).to_broadcast([128, CHK[g][1], NTOK])
                if g == 0:
                    dve.wait_ge(mb_done, G + 1)
                nc.vector.tensor_tensor(t, t, m, ALU.subtract).then_inc(sub_done, 1)

            def normalise(G, chain):
                dve.wait_ge(pv_done, G + 3)
                o = ps[:, OB, 0:QT * OW].rearrange("p (q n) -> p q n", q=QT)
                chain(nc.vector.reciprocal(rs[:, :], o[:, :, HD]))
                nc.vector.tensor_tensor(o32[:, :, :], o[:, :, 0:HD],
                                        rs[:, :].rearrange("p (q a) -> p q a", a=1).to_broadcast([128, QT, HD]),
                                        ALU.mult).then_inc(o_done, 1)

            def output(u, q):
                dve.wait_ge(wo_ready, u * QT + q + 1)
                xs = K["x"][:, bass.ds(u % NB * QT + q, 1), :].rearrange("p a d -> p (a d)")
                nc.vector.scalar_tensor_tensor(xs, ps[:, WB + q, :], 1.0 / (SX * SW), xs, ALU.mult,
                                               ALU.add).then_inc(wo_taken, 1)

            def step(u, e, h, lags, more):
                G = u * GRP + h
                chain = Chain(dve, chain_s, G * CHN - min(lags, 2))
                if lags >= 1:
                    maxima(G - 1)
                    sub(G - 1, h - 1, 0)
                    sub(G - 1, h - 1, 1)
                largest(G, h, 1, chain)
                if lags >= 1:
                    sub(G - 1, h - 1, 2)
                    sub(G - 1, h - 1, 3)
                largest(G, h, 2, chain)
                if h == GRP - 2 and more:
                    latent_keys(u + 1, 1 - e)
                if h == GRP - 1 and more:
                    latent_values(u + 1, 1 - e)
                if lags >= 2:
                    normalise(G - 2, chain)
                largest(G, h, 3, chain)
                partition_maxima()
                if h == 2 and lags >= 3:
                    output(u - 1, 0)
                if lags >= 2:
                    turned_out(G - 2, h - 2)
                if h < GRP - 2 or more:
                    query(G + 2, h)
                if h == 2 and lags >= 3:
                    output(u - 1, 1)

            def first():
                latent_keys(0, 0)
                query(0, 0)
                latent_values(0, 0)
                query(1, 1)
                for h in range(3):
                    step(0, 0, h, h, True)

            def rest(u, e, more):
                for h in range(3, GRP):
                    step(u, e, h, 3, more)
                for h in range(3 if more else 0):
                    step(u + 1, 1 - e, h, 3, True)

            units(dve, first, rest)
            G = NU * GRP
            chain = Chain(dve, chain_s, G * CHN - 2)
            maxima(G - 1)
            for g in range(NCK):
                sub(G - 1, GRP - 1, g)
            for n in (2, 1):
                normalise(G - n, chain)
                turned_out(G - n, GRP - n)
            for q in range(QT):
                output(NU - 1, q)

        @block.tensor
        def _(pe):
            pe.sem_inc(s_ready, 1)
            pe.sem_inc(s_copied, 2)
            pe.sem_inc(lo_done, 2 * NCK)
            pe.sem_inc(pv_done, 2)
            pe.sem_inc(o_done, 1)
            pe.sem_inc(ot_lo, 2)
            pe.sem_inc(wo_taken, QT)

            def tokens(u):
                return [xT[:, s, :, bass.ds(u % NB * NTOK, NTOK)] for s in range(2)]

            def latent_keys(u):
                kv, tok = u // NB, tokens(u)
                for i in range(DC):
                    last = mm3(nc, small[0], [K["wk"][:, s, i, bass.ds(kv * HD, HD)] for s in range(2)],
                               [tok[s][:, i, :] for s in range(2)], i == 0, i == DC - 1)
                last.then_inc(l_ready, 1)

            def latent_values(u):
                kv = u // NB
                for q in range(QT):
                    for i in range(DC):
                        last = mm3(nc, small[0][:, q * 128:(q + 1) * 128],
                                   [xT[:, s, i, bass.ds(u % NB * NTOK + q * 128, 128)] for s in range(2)],
                                   [K["wv"][:, s, i, bass.ds(kv * HD, HD)] for s in range(2)], i == 0, i == DC - 1)
                last.then_inc(l_ready, 1)

            def query(u, h):
                tok = tokens(u)
                if h == 0:
                    pe.wait_ge(wq_loaded, (u // NB + 1) * 16)
                for i in range(DC):
                    last = mm3(nc, small[1], [wq[:, i, h // 4, s, h % 4 * HD:(h % 4 + 1) * HD] for s in range(2)],
                               [tok[s][:, i, :] for s in range(2)], i == 0, i == DC - 1)
                last.then_inc(q_ready, 1)

            def scores(u, e, h, j):
                n = (u * GRP + h) * NP + j
                pe.wait_ge(s_copied, n + 1 if j < 2 else n)
                k0, w = PAIR[j]
                for kt in range(k0, k0 + w):
                    last = mm3(nc, scores_of(j)[:, (kt - k0) * NTOK:(kt - k0 + 1) * NTOK],
                               [kb[:, e, s, kt * 128:(kt + 1) * 128] for s in range(2)],
                               [qT[:, h % 2, s, :] for s in range(2)], True, True)
                last.then_inc(s_ready, 1)

            def attend(G, e, h, g):
                pe.wait_ge(lo_done, (G + 2) * NCK + g + 1)
                if g == 0:
                    pe.wait_ge(o_done, G + 1)
                k0, n = CHK[g]
                for kt in range(k0, k0 + n):
                    r = 128 if kt < KT1 - 1 else LAST
                    for q in range(QT):
                        o = ps[:, OB, q * OW:(q + 1) * OW]
                        p = [pT[0:r, h % 2, s, kt, q * 128:(q + 1) * 128] for s in range(2)]
                        nc.tensor.matmul(o, p[0], vb[0:r, e, kt, HD:VW], start=(kt == 0 and q == 0), stop=False)
                        nc.tensor.matmul(o[:, 0:HD], p[0], vb[0:r, e, kt, 0:HD], start=False, stop=False)
                        last = nc.tensor.matmul(o, p[1], vb[0:r, e, kt, HD:VW], start=False, stop=(kt == KT1 - 1 and q == QT - 1))
                if g == NCK - 1:
                    last.then_inc(pv_done, 1)

            def turn_maxima(G):
                pe.wait_ge(rm_ready, G + 1)
                pe.wait_ge(ot_lo, G + 1)
                for q in range(QT):
                    last = nc.tensor.transpose(small[0][:, q * 128:(q + 1) * 128], rm[:, q * 128:(q + 1) * 128],
                                               K["id32"][:, :])
                last.then_inc(mt_ready, 1)

            def spread_maxima(G):
                pe.wait_ge(mc_ready, G + 1)
                for q in range(QT):
                    last = nc.tensor.transpose(small[1][:, q * 128:(q + 1) * 128],
                                               mcol[:, q:q + 1].to_broadcast([128, 128]), K["id32"][:, :])
                last.then_inc(mb_ready, 1)

            def turn_out(G):
                pe.wait_ge(o_done, G + 2)
                pe.wait_ge(mc_ready, G + 2)
                for q in range(QT):
                    last = nc.tensor.transpose(small[0][:, q * 128:(q + 1) * 128], o32[:, q, :], K["id32"][:, :])
                last.then_inc(ot_ready, 1)

            def project(u, h):
                pe.wait_ge(ot_lo, u * GRP + h + 3)
                if h == 0:
                    pe.wait_ge(wo_loaded, (u // NB + 1) * 16)
                for q in range(QT):
                    if h == 0:
                        pe.wait_ge(wo_taken, u * QT + q + 1)
                    last = mm3(nc, ps[:, WB + q, :], [oT[:, h % 2, s, q * 128:(q + 1) * 128] for s in range(2)],
                               [wo[:, h, s, :] for s in range(2)], h == 0, h == GRP - 1)
                    if h == GRP - 1:
                        last.then_inc(wo_ready, 1)

            def step(u, e, h, lags, more):
                G = u * GRP + h
                pe.wait_ge(q_lo, G + 1)
                if h == 0:
                    pe.wait_ge(l_lo, 2 * u + 1)
                    pe.wait_ge(k_loaded[e], (u // 2 + 1) * 16)
                scores(u, e, h, 0)
                if lags >= 1:
                    turn_maxima(G - 1)
                scores(u, e, h, 1)
                if lags >= 1:
                    if h < GRP - 1 or more:
                        pe.wait_ge(q_lo, G + 2)
                    spread_maxima(G - 1)
                for g in range(NCK):
                    if g:
                        scores(u, e, h, 2 * g)
                        scores(u, e, h, 2 * g + 1)
                    if lags >= 2:
                        if h == 2 and g == 0:
                            pe.wait_ge(l_lo, 2 * u + 2)
                            pe.wait_ge(v_loaded[e], (u // 2 + 1) * 16)
                        attend(G - 2, e if h >= 2 else 1 - e, h - 2, g)
                    if g == 1 and h >= GRP - 2 and more:
                        pe.wait_ge(mc_ready, G)
                        if h == GRP - 2:
                            latent_keys(u + 1)
                        else:
                            latent_values(u + 1)
                if lags >= 3:
                    project(u if h >= 3 else u - 1, (h - 3) % GRP)
                if h == GRP - 2 and more:
                    pe.wait_ge(l_lo, 2 * u + 3)
                if h == GRP - 1 and more:
                    pe.wait_ge(l_lo, 2 * u + 4)
                if lags >= 2:
                    turn_out(G - 2)
                if h < GRP - 2 or more:
                    if lags >= 1:
                        pe.wait_ge(mb_done, G)
                    else:
                        pe.wait_ge(q_lo, 2)
                    query(u if h < GRP - 2 else u + 1, (h + 2) % GRP)

            def first():
                pe.wait_ge(consts, 3)
                latent_keys(0)
                query(0, 0)
                pe.wait_ge(l_lo, 1)
                latent_values(0)
                pe.wait_ge(q_lo, 1)
                query(0, 1)
                pe.wait_ge(l_lo, 2)
                for h in range(3):
                    step(0, 0, h, h, True)

            def rest(u, e, more):
                for h in range(3, GRP):
                    step(u, e, h, 3, more)
                for h in range(3 if more else 0):
                    step(u + 1, 1 - e, h, 3, True)

            units(pe, first, rest)
            G = NU * GRP - 1
            turn_maxima(G)
            spread_maxima(G)
            for g in range(NCK):
                attend(G - 1, 1, GRP - 2, g)
            project(NU - 1, GRP - 3)
            turn_out(G - 1)
            for g in range(NCK):
                attend(G, 1, GRP - 1, g)
            project(NU - 1, GRP - 2)
            pe.wait_ge(ot_lo, G + 2)
            pe.wait_ge(o_done, G + 2)
            for q in range(QT):
                last = nc.tensor.transpose(small[0][:, q * 128:(q + 1) * 128], o32[:, q, :], K["id32"][:, :])
            last.then_inc(ot_ready, 1)
            project(NU - 1, GRP - 1)


def layer_norm_turned(nc, ps, K, xT, scale, tag, loads):
    with ExitStack() as c:
        def sb(name, shape, dt):
            return c.enter_context(nc.sbuf_tensor(name + tag, shape, dt))

        def sem(name):
            return c.enter_context(nc.semaphore(tag + "n_" + name))

        xln = sb("xlnn", [128, NT, D], fp32)
        stats = stats_tiles(sb, "n")
        mv, ve, yh = stats
        var_ready, pow_ready, chain_s, xln_ready, t_ready, t_hi, t_lo = (
            sem(n) for n in ("var_ready", "pow_ready", "chain", "xln_ready", "t_ready", "t_hi", "t_lo"))
        block = c.enter_context(nc.Block())

        @block.sync
        def _(sp):
            loads(sp)

        @block.gpsimd
        def _(pool):
            pool.wait_ge(var_ready, 1)
            nc.gpsimd.tensor_tensor(yh[:, 0, :], ve[:, :], K["mhalf"][:, :], ALU.pow).then_inc(pow_ready, 1)

        @block.vector
        def _(dve):
            def low(n):
                dve.wait_ge(t_hi, n + 1)
                nc.vector.scalar_tensor_tensor(xT[:, 1, :, n * 128:(n + 1) * 128],
                                               ps[:, n % 4, :].rearrange("p (c n) -> p c n", c=DC), scale,
                                               xT[:, 0, :, n * 128:(n + 1) * 128], ALU.mult,
                                               ALU.subtract).then_inc(t_lo, 1)

            layer_norm_stats(nc, dve, Chain(dve, chain_s), K, stats, var_ready, pow_ready, range(NT))
            for n in range(NT):
                nc.vector.tensor_scalar(xln[:, n, :], K["x"][:, n, :], mv[:, n, 0:1], yh[:, 2, n:n + 1],
                                        ALU.subtract, ALU.mult).then_inc(xln_ready, 1)
                if n >= 3:
                    low(n - 3)
            for n in range(NT - 3, NT):
                low(n)

        @block.tensor
        def _(pe):
            for n in range(NT):
                pe.wait_ge(xln_ready, n + 1)
                if n >= 4:
                    pe.wait_ge(t_lo, n - 3)
                for i in range(DC):
                    last = nc.tensor.transpose(ps[:, n % 4, i * 128:(i + 1) * 128],
                                               xln[:, n, i * 128:(i + 1) * 128], K["id32"][:, :])
                last.then_inc(t_ready, 1)

        @block.scalar
        def _(act):
            for n in range(NT):
                act.wait_ge(t_ready, n + 1)
                nc.scalar.activation(xT[:, 0, :, n * 128:(n + 1) * 128],
                                     ps[:, n % 4, :].rearrange("p (c n) -> p c n", c=DC), ACT.Copy,
                                     scale=scale).then_inc(t_hi, 1)


def ffn1(nc, ps, K, baseW, gateW, loraA, loraB, out):
    GA = NE + NR
    HR = NR // 2
    with ExitStack() as c:
        def sb(name, shape, dt):
            return c.enter_context(nc.sbuf_tensor(name, shape, dt))

        def sem(name):
            return c.enter_context(nc.semaphore("d_" + name))

        xT = sb("xT2", [128, 2, DC, NB * NTOK], fp16)
        braw = sb("base_raw", [128, DC, D], fp32)
        graw = sb("gate_raw", [NE, D], fp32)
        araw = sb("a_raw", [HR, 2, D], fp32)
        lraw = sb("b_raw", [128, DC, NE, RANK], fp32)
        bT = sb("base_T", [128, 2, DC, D], fp16)
        gaT = sb("ga_T", [128, 2, DC, GA], fp16)
        lT = sb("b_T", [HR, 2, 2, D], fp16)
        iota = sb("iota", [128, NE], fp32)
        ga = sb("ga", [128, 2, GA], fp32)
        top = sb("top", [128, 2, 8], fp32)
        topi = sb("topi", [128, 2, 8], u32)
        tf = sb("tf", [128, 2, 8], fp32)
        gate = sb("gate", [128, 2, 2, NE], fp32)
        hg = sb("hg", [128, 2, NR], fp32)
        hgT = sb("hgT", [HR, 2, 2, 2, 128], fp16)
        y = sb("y", [128, 2, D], fp32)
        loaded = [sem(f"loaded{i}") for i in range(4)]

        def loads(sp):
            sp.dma_start(braw[:, :, :], baseW.rearrange("(c p) n -> p c n", p=128)).then_inc(loaded[0], 16)
            sp.dma_start(graw[:, :], gateW).then_inc(loaded[1], 16)
            sp.dma_start(araw[:, :, :], loraA.rearrange("e r n -> (e r) n").rearrange("(c p) n -> p c n", p=HR)
                         ).then_inc(loaded[2], 16)
            for i in range(DC):
                sp.dma_start(lraw[:, i], loraB[:, i * 128:(i + 1) * 128, :].rearrange("e p r -> p e r")
                             ).then_inc(loaded[3], 16)

        layer_norm_turned(nc, ps, K, xT, SX, "d", loads)
        (iota_s, w_ready, w_hi, w_lo, ga_ready, ga_free, top_s, ex_ready, hg_ready, ht_ready, ht_hi, ht_lo,
         y_ready, y_free, chain_s) = (sem(n) for n in (
             "iota", "w_ready", "w_hi", "w_lo", "ga_ready", "ga_free", "top", "ex_ready", "hg_ready",
             "ht_ready", "ht_hi", "ht_lo", "y_ready", "y_free", "chain"))
        stored = [sem(f"stored{i}") for i in range(2)]
        block = c.enter_context(nc.Block())

        prep = []
        for i in range(DC):
            prep.append(([bT[:, s, i, :] for s in range(2)], D, 128))
        for i in range(DC):
            prep.append(([gaT[:, s, i, :] for s in range(2)], GA, 128))
        for r in range(2):
            prep.append(([lT[:, s, r, :] for s in range(2)], D, HR))

        @block.sync
        def _(sp):
            for n in range(NT):
                sp.wait_ge(y_free, n + 1)
                sp.dma_start(out[n // QT, (n % QT) * 128:(n % QT + 1) * 128, :], y[:, n % 2, :]).then_inc(stored[n % 2], 16)
            for s in stored:
                sp.wait_ge(s, 16 * NT // 2)

        @block.gpsimd
        def _(pool):
            nc.gpsimd.iota(iota[:, :], pattern=[[1, NE]], base=0, channel_multiplier=0,
                           allow_small_or_imprecise_dtypes=True).then_inc(iota_s, 1)

        @block.tensor
        def _(pe):
            for n in range(len(prep)):
                if n >= 4:
                    pe.wait_ge(w_lo, n - 3)
                o = ps[:, n % 4, :]
                if n < DC:
                    pe.wait_ge(loaded[0], 16)
                    for a in range(DC):
                        last = nc.tensor.transpose(o[:, a * 128:(a + 1) * 128], braw[:, a, n * 128:(n + 1) * 128],
                                                   K["id32"][:, :])
                elif n < 2 * DC:
                    i = n - DC
                    pe.wait_ge(loaded[1], 16)
                    pe.wait_ge(loaded[2], 16)
                    nc.tensor.transpose(o[:, 0:NE], graw[:, i * 128:(i + 1) * 128], K["id32"][0:NE, 0:NE])
                    for a in range(2):
                        last = nc.tensor.transpose(o[:, NE + a * HR:NE + (a + 1) * HR], araw[:, a, i * 128:(i + 1) * 128],
                                                   K["id32"][0:HR, 0:HR])
                else:
                    r = n - 2 * DC
                    pe.wait_ge(loaded[3], 16 * DC)
                    for a in range(DC):
                        last = nc.tensor.transpose(o[0:HR, a * 128:(a + 1) * 128],
                                                   lraw[:, a].rearrange("p e r -> p (e r)")[:, r * HR:(r + 1) * HR],
                                                   K["id32"][:, :])
                last.then_inc(w_ready, 1)
            pe.wait_ge(w_lo, len(prep))

            def gates(n):
                if n >= 2:
                    pe.wait_ge(ga_free, n - 1)
                for i in range(DC):
                    last = mm3(nc, ps[:, 4 + n % 2, 0:GA], [xT[:, s, i, n * 128:(n + 1) * 128] for s in range(2)],
                               [gaT[:, s, i, :] for s in range(2)], i == 0, i == DC - 1)
                last.then_inc(ga_ready, 1)

            def base(n):
                if n >= 2:
                    pe.wait_ge(y_free, n - 1)
                for i in range(DC):
                    mm3(nc, ps[:, 6 + n % 2, :], [xT[:, s, i, n * 128:(n + 1) * 128] for s in range(2)],
                        [bT[:, s, i, :] for s in range(2)], i == 0, False)

            gates(0)
            base(0)
            gates(1)
            for n in range(NT):
                pe.wait_ge(hg_ready, n + 1)
                if n >= 2:
                    pe.wait_ge(ht_lo, n - 1)
                for r in range(2):
                    last = nc.tensor.transpose(ps[0:HR, n % 2, r * 128:(r + 1) * 128],
                                               hg[:, n % 2, r * HR:(r + 1) * HR], K["id32"][:, :])
                last.then_inc(ht_ready, 1)
                if n + 1 < NT:
                    base(n + 1)
                pe.wait_ge(ht_lo, n + 1)
                for r in range(2):
                    last = mm3(nc, ps[:, 6 + n % 2, :], [hgT[:, n % 2, s, r, :] for s in range(2)],
                               [lT[:, s, r, :] for s in range(2)], False, r == 1)
                last.then_inc(y_ready, 1)
                if n + 2 < NT:
                    gates(n + 2)

        @block.scalar
        def _(act):
            for n, (dst, w, r) in enumerate(prep):
                act.wait_ge(w_ready, n + 1)
                nc.scalar.activation(dst[0], ps[0:r, n % 4, 0:w], ACT.Copy, scale=SW).then_inc(w_hi, 1)
            def exp_gap(n):
                act.wait_ge(top_s, n + 1)
                nc.scalar.activation(tf[:, n % 2, 3:4], tf[:, n % 2, 2:3], ACT.Exp).then_inc(ex_ready, 1)

            exp_gap(0)
            for n in range(NT):
                act.wait_ge(ht_ready, n + 1)
                nc.scalar.activation(hgT[:, n % 2, 0], ps[0:HR, n % 2, 0:256].rearrange("p (r n) -> p r n", r=2),
                                     ACT.Copy, scale=SX).then_inc(ht_hi, 1)
                if n + 1 < NT:
                    exp_gap(n + 1)

        @block.vector
        def _(dve):
            chain = Chain(dve, chain_s)
            for n, (dst, w, r) in enumerate(prep):
                dve.wait_ge(w_hi, n + 1)
                nc.vector.scalar_tensor_tensor(dst[1], ps[0:r, n % 4, 0:w], SW, dst[0], ALU.mult,
                                               ALU.subtract).then_inc(w_lo, 1)
            dve.wait_ge(iota_s, 1)
            def gated(n):
                p = n % 2
                dve.wait_ge(ga_ready, n + 1)
                nc.vector.tensor_scalar(ga[:, p, :], ps[:, 4 + p, 0:GA], 1.0 / (SX * SW), None,
                                        ALU.mult).then_inc(ga_free, 1)
                dve.wait_ge(ga_free, n + 1)
                chain(nc.vector.max(top[:, p, :], ga[:, p, 0:NE]))
                chain(nc.vector.max_index(topi[:, p, :], top[:, p, :], ga[:, p, 0:NE]))
                nc.vector.tensor_tensor(tf[:, p, 2:3], top[:, p, 1:2], top[:, p, 0:1], ALU.subtract).then_inc(top_s, 1)
                chain(nc.vector.tensor_copy(tf[:, p, 0:2], topi[:, p, 0:2]))
                dve.wait_ge(ex_ready, n + 1)
                chain(nc.vector.tensor_scalar(tf[:, p, 4:5], tf[:, p, 3:4], 1.0, None, ALU.add))
                chain(nc.vector.reciprocal(tf[:, p, 5:6], tf[:, p, 4:5]))
                chain(nc.vector.tensor_scalar(tf[:, p, 6:7], tf[:, p, 5:6], TOPK_SCALE, None, ALU.mult))
                chain(nc.vector.tensor_scalar(tf[:, p, 7:8], tf[:, p, 6:7], tf[:, p, 3:4], None, ALU.mult))
                nc.vector.tensor_scalar(gate[:, p, 0, :], iota[:, :], tf[:, p, 0:1], tf[:, p, 6:7], ALU.is_equal, ALU.mult)
                chain(nc.vector.tensor_scalar(gate[:, p, 1, :], iota[:, :], tf[:, p, 1:2], tf[:, p, 7:8], ALU.is_equal,
                                              ALU.mult))
                chain(nc.vector.tensor_tensor(gate[:, p, 0, :], gate[:, p, 0, :], gate[:, p, 1, :], ALU.add))
                nc.vector.tensor_tensor(hg[:, p, :].rearrange("p (e r) -> p e r", r=RANK),
                                        ga[:, p, NE:GA].rearrange("p (e r) -> p e r", r=RANK),
                                        gate[:, p, 0, :].rearrange("p (e a) -> p e a", a=1).to_broadcast([128, NE, RANK]),
                                        ALU.mult).then_inc(hg_ready, 1)

            gated(0)
            for n in range(NT):
                p = n % 2
                dve.wait_ge(ht_hi, n + 1)
                nc.vector.scalar_tensor_tensor(hgT[:, p, 1], ps[0:HR, p, 0:256].rearrange("p (r n) -> p r n", r=2), SX,
                                               hgT[:, p, 0], ALU.mult, ALU.subtract).then_inc(ht_lo, 1)
                if n + 1 < NT:
                    gated(n + 1)
                dve.wait_ge(y_ready, n + 1)
                if n >= 2:
                    dve.wait_ge(stored[p], 16 * (n // 2))
                nc.vector.scalar_tensor_tensor(y[:, p, :], ps[:, 6 + p, :], 1.0 / (SX * SW), K["x"][:, n, :], ALU.mult,
                                               ALU.add).then_inc(y_free, 1)


_INS = ['x', 'ctx_4096', 'L0_xattn_Wq', 'L0_xattn_bq', 'L0_xattn_Wk', 'L0_xattn_bk', 'L0_ffn_w_up', 'L0_ffn_w_down',
        'L1_xattn_Wq', 'L1_xattn_Wk', 'L1_xattn_Wv', 'L1_xattn_Wo', 'L1_ffn_base_W', 'L1_ffn_gate_W', 'L1_ffn_lora_A',
        'L1_ffn_lora_B']
_OUTS = [((4, 256, 512), 'float32')]


def kernel(**inputs):
    import numpy as _np
    import concourse.bacc as _bacc
    from concourse import mybir as _mybir
    from concourse.bass_utils import run_bass_kernel_spmd as _run

    nc = _bacc.Bacc("TRN2", target_bir_lowering=False, num_devices=1)
    arrays, args = {}, []
    for name in _INS:
        a = _np.ascontiguousarray(inputs[name])
        arrays[f"in_{name}_dram"] = a
        args.append(nc.dram_tensor(f"in_{name}_dram", a.shape, _mybir.dt.from_np(a.dtype), kind="ExternalInput").ap())
    for i, (shape, dtype) in enumerate(_OUTS):
        dt = _mybir.dt.from_np(_np.dtype(dtype))
        args.append(nc.dram_tensor(f"out_{i}_dram", shape, dt, kind="ExternalOutput").ap())
    build(nc, *args)
    r = _run(nc, [arrays], core_ids=[0])
    got = tuple(r.results[0][f"out_{i}_dram"] for i in range(len(_OUTS)))
    return got[0]
```
